# Optimizing a Trainium2 kernel written in Bass

```python
import numpy as np
import jax
import jax.numpy as jnp

def _softmax(x, axis=-1):
    return jax.nn.softmax(x, axis=axis)

def _gelu(x):
    return jax.nn.gelu(x, approximate=True)

def _silu(x):
    return jax.nn.silu(x)

def _sigmoid(x):
    return jax.nn.sigmoid(x)

def _layernorm(x, axis=-1, eps=1e-05):
    m = jnp.mean(x, axis=axis, keepdims=True)
    v = jnp.var(x, axis=axis, keepdims=True)
    return (x - m) / jnp.sqrt(v + eps)

def _scatter_add(tgt, idx, src, axis=0):
    return tgt.at[idx].add(src)

def _segment_sum(src, seg, n):
    return jax.ops.segment_sum(src, seg, n)
kernel_name = 'mk_xattn_ffn_d2_seqx_r8_9aeafa'

def setup_inputs(seed: int=0):
    np.random.seed(seed)
    _w = jnp.asarray

    def _rec_inputs():
        import jax
        import jax.numpy as jnp
        _rk = jax.random.key(seed)
        x = -0.0002928 + 1 * jax.random.normal(jax.random.fold_in(_rk, 1), (2, 512, 128), jnp.float32)
        _lenS = 512 - jax.random.randint(jax.random.fold_in(_rk, 7), (2,), 0, max(1, 512 // 4) + 1, jnp.int32)
        _lenS2 = 154 - jax.random.randint(jax.random.fold_in(_rk, 8), (2,), 0, max(1, 154 // 4) + 1, jnp.int32)
        _ctx_1024P = jax.random.normal(jax.random.fold_in(_rk, 11), (2, 16, 128), jnp.float32)
        _ctx_1024c = jax.random.dirichlet(jax.random.fold_in(_rk, 511), 0.3 * jnp.ones((16,), jnp.float32), (2, 154))
        _ctx_1024t = jnp.einsum('bsk,bkd->bsd', _ctx_1024c, _ctx_1024P)
        _ctx_1024t = _ctx_1024t * jax.lax.rsqrt(jnp.mean(jnp.square(_ctx_1024t)) + 1e-12) * 0.953939
        ctx_1024 = -1.39393e-06 + 0.999914 * (_ctx_1024t + 0.3 * jax.random.normal(jax.random.fold_in(_rk, 611), (2, 154, 128), jnp.float32))
        _validS = jnp.arange(512)[None, :] < _lenS[:, None]
        _validS2 = jnp.arange(154)[None, :] < _lenS2[:, None]
        _causal = jnp.tril(jnp.ones((512, 512), dtype=bool))
        mask_BxS2_bk0 = jnp.logical_not(jnp.broadcast_to(_validS2[:, :], (2, 154)))
        mask_BxS_ik0 = jnp.where(jnp.broadcast_to(_validS[:, :], (2, 512)), 0, 1).astype(jnp.int32)
        return (x, ctx_1024, mask_BxS2_bk0, mask_BxS_ik0)
    x, ctx_1024, mask_BxS2_bk0, mask_BxS_ik0 = _rec_inputs()

    def _L0_xattn_setup():
        import jax, jax.numpy as jnp
        import numpy as np
        B, TQ, TK = (2, 256, 256)
        DQ = DK = DV = 128
        QK_DIM, H = (32, 8)
        HD = QK_DIM // H
        OUT_DIM = 128
        key = jax.random.key(seed)
        ks = jax.random.split(key, 10)
        std = 0.02
        return {'Q': jax.random.normal(ks[0], (B, TQ, DQ), jnp.float32), 'K': jax.random.normal(ks[1], (B, TK, DK), jnp.float32), 'V': jax.random.normal(ks[2], (B, TK, DV), jnp.float32), 'Wq': jax.random.normal(ks[3], (QK_DIM, DQ), jnp.float32) * std, 'bq': jnp.zeros((QK_DIM,), jnp.float32), 'Wk': jax.random.normal(ks[4], (QK_DIM, DK), jnp.float32) * std, 'bk': jnp.zeros((QK_DIM,), jnp.float32), 'Wo': jax.random.normal(ks[5], (OUT_DIM, H * DV), jnp.float32) * std, 'bo': jnp.zeros((OUT_DIM,), jnp.float32), 'key_padding_mask': jax.random.randint(ks[6], (B, TK), 0, 2) > 0}
    _L0_xattn_all = _L0_xattn_setup()
    _L0_xattn_in = {k: v for k, v in _L0_xattn_all.items() if k in ('Wq', 'bq', 'Wk', 'bk', 'Wo', 'bo')}
    del _L0_xattn_all

    def _L0_ffn_setup():
        import jax, jax.numpy as jnp
        import numpy as np
        EPS = 1e-05

        def _layernorm(x, w, b):
            mu = jnp.mean(x, axis=-1, keepdims=True)
            var = jnp.mean((x - mu) ** 2, axis=-1, keepdims=True)
            return (x - mu) * jax.lax.rsqrt(var + EPS) * w + b

        def _rope_tables(T, D, base=10000.0):
            inv_freq = 1.0 / base ** (jnp.arange(0, D, 2, dtype=jnp.float32) / D)
            t = jnp.arange(T, dtype=jnp.float32)
            freqs = jnp.einsum('i,j->ij', t, inv_freq)
            emb = jnp.concatenate([freqs, freqs], axis=-1)
            return (jnp.cos(emb), jnp.sin(emb))

        def _rotate_half(x):
            x1, x2 = (x[..., :x.shape[-1] // 2], x[..., x.shape[-1] // 2:])
            return jnp.concatenate([-x2, x1], axis=-1)

        def _attn(x, ln_w, ln_b, conv_w, attn_w, proj_w, n_head):
            B, T, C = x.shape
            D = C // n_head
            h = _layernorm(x, ln_w, ln_b)
            hc = jnp.transpose(h, (0, 2, 1))
            hc = jnp.pad(hc, ((0, 0), (0, 0), (2, 0)))
            hc = jax.lax.conv_general_dilated(hc, conv_w, window_strides=(1,), padding='VALID', dimension_numbers=('NCH', 'OIH', 'NCH'), feature_group_count=C)
            h = jnp.transpose(hc, (0, 2, 1))
            qkv = h @ attn_w
            q, k, v = jnp.split(qkv, 3, axis=-1)
            q = q.reshape(B, T, n_head, D)
            k = k.reshape(B, T, n_head, D)
            v = v.reshape(B, T, n_head, D)
            cos, sin = _rope_tables(T, D)
            cos = cos[None, :, None, :]
            sin = sin[None, :, None, :]
            q = q * cos + _rotate_half(q) * sin
            k = k * cos + _rotate_half(k) * sin
            scores = jnp.einsum('bqhd,bkhd->bhqk', q, k) / jnp.sqrt(jnp.float32(D))
            causal = jnp.tril(jnp.ones((T, T), dtype=bool))
            scores = jnp.where(causal, scores, jnp.float32(-1e+30))
            p = jax.nn.softmax(scores, axis=-1)
            y = jnp.einsum('bhqk,bkhd->bqhd', p, v).reshape(B, T, C)
            return y @ proj_w

        def _moe(x, ln_w, ln_b, router_w, expert_wv, expert_proj):
            h = _layernorm(x, ln_w, ln_b)
            logits = h @ router_w
            expert_idx = jnp.argmax(logits, axis=-1)
            E = router_w.shape[-1]
            out = jnp.zeros_like(x)
            for e in range(E):
                gv = h @ expert_wv[e]
                gate_raw, value = jnp.split(gv, 2, axis=-1)
                y = gate_raw * jax.nn.sigmoid(gate_raw) * value @ expert_proj[e]
                out = out + jnp.where((expert_idx == e)[..., None], y, 0.0)
            return out
        C, H, E, B, T = (128, 16, 4, 4, 128)
        Dff = 4 * C
        key = jax.random.key(seed)
        ks = jax.random.split(key, 8)
        s = 0.02
        return {'x': jax.random.normal(ks[0], (B, T, C), dtype=jnp.float32), 'ln1_w': jnp.ones((C,), jnp.float32), 'ln1_b': jnp.zeros((C,), jnp.float32), 'ln2_w': jnp.ones((C,), jnp.float32), 'ln2_b': jnp.zeros((C,), jnp.float32), 'conv_w': jax.random.normal(ks[1], (C, 1, 3), dtype=jnp.float32) * 0.1, 'attn_w': jax.random.normal(ks[2], (C, 3 * C), dtype=jnp.float32) * s, 'proj_w': jax.random.normal(ks[3], (C, C), dtype=jnp.float32) * s, 'router_w': jax.random.normal(ks[4], (C, E), dtype=jnp.float32) * s, 'expert_wv': jax.random.normal(ks[5], (E, C, 2 * Dff), dtype=jnp.float32) * s, 'expert_proj': jax.random.normal(ks[6], (E, Dff, C), dtype=jnp.float32) * s}
    _L0_ffn_all = _L0_ffn_setup()
    _L0_ffn_in = {k: v for k, v in _L0_ffn_all.items() if k in ('ln1_w', 'ln1_b', 'ln2_w', 'ln2_b', 'conv_w', 'attn_w', 'proj_w', 'router_w', 'expert_wv', 'expert_proj')}
    del _L0_ffn_all

    def _L1_xattn_setup():
        import jax, jax.numpy as jnp
        import numpy as np
        HEADS = 16
        DIM_HEAD = 64
        SCALE = DIM_HEAD ** (-0.5)
        MASK_NEG = 1000000.0

        def _split_heads(t):
            b, n, _ = t.shape
            return t.reshape(b, n, HEADS, DIM_HEAD).transpose(0, 2, 1, 3)
        key = jax.random.key(seed)
        ks = jax.random.split(key, 6)
        B, N, M, D = (2, 256, 256, 128)
        inner = HEADS * DIM_HEAD
        x = jax.random.normal(ks[0], (B, N, D), dtype=jnp.float32)
        context = jax.random.normal(ks[1], (B, M, D), dtype=jnp.float32)
        mask = jax.random.randint(ks[2], (B, N), 0, 2, dtype=jnp.int32)
        Wq = jax.random.normal(ks[3], (D, inner), dtype=jnp.float32) * D ** (-0.5)
        Wkv = jax.random.normal(ks[4], (D, 2 * inner), dtype=jnp.float32) * D ** (-0.5)
        Wout = jax.random.normal(ks[5], (inner, D), dtype=jnp.float32) * inner ** (-0.5)
        bout = jnp.zeros((D,), dtype=jnp.float32)
        return {'x': x, 'context': context, 'mask': mask, 'Wq': Wq, 'Wkv': Wkv, 'Wout': Wout, 'bout': bout}
    _L1_xattn_all = _L1_xattn_setup()
    _L1_xattn_in = {k: v for k, v in _L1_xattn_all.items() if k in ('Wq', 'Wkv', 'Wout', 'bout')}
    del _L1_xattn_all

    def _L1_ffn_setup():
        import jax, jax.numpy as jnp
        import numpy as np
        D_MODEL = 128
        M = 64
        INNER = 16
        key = jax.random.key(seed)
        ks = jax.random.split(key, 9)

        def init(k, shape, fan_in):
            bound = 1.0 / np.sqrt(fan_in)
            return jax.random.uniform(k, shape, jnp.float32, -bound, bound)
        x = jax.random.normal(ks[0], (16, 512, D_MODEL), dtype=jnp.float32)
        Win = init(ks[1], (D_MODEL, M), D_MODEL)
        bin_ = init(ks[2], (M,), D_MODEL)
        W1 = init(ks[3], (M, INNER), 1)
        b1 = init(ks[4], (M, INNER), 1)
        W2 = init(ks[5], (M, INNER), INNER)
        b2 = init(ks[6], (M,), INNER)
        Wout = init(ks[7], (M, D_MODEL), M)
        bout = init(ks[8], (D_MODEL,), M)
        return {'x': x, 'Win': Win, 'bin_': bin_, 'W1': W1, 'b1': b1, 'W2': W2, 'b2': b2, 'Wout': Wout, 'bout': bout}
    _L1_ffn_all = _L1_ffn_setup()
    _L1_ffn_in = {k: v for k, v in _L1_ffn_all.items() if k in ('Win', 'bin_', 'W1', 'b1', 'W2', 'b2', 'Wout', 'bout')}
    del _L1_ffn_all
    return {'x': x, 'ctx_1024': ctx_1024, 'mask_BxS2_bk0': mask_BxS2_bk0, 'mask_BxS_ik0': mask_BxS_ik0, 'L0_xattn_Wq': _L0_xattn_in['Wq'], 'L0_xattn_bq': _L0_xattn_in['bq'], 'L0_xattn_Wk': _L0_xattn_in['Wk'], 'L0_xattn_bk': _L0_xattn_in['bk'], 'L0_xattn_Wo': _L0_xattn_in['Wo'], 'L0_xattn_bo': _L0_xattn_in['bo'], 'L0_ffn_ln1_w': _L0_ffn_in['ln1_w'], 'L0_ffn_ln1_b': _L0_ffn_in['ln1_b'], 'L0_ffn_ln2_w': _L0_ffn_in['ln2_w'], 'L0_ffn_ln2_b': _L0_ffn_in['ln2_b'], 'L0_ffn_conv_w': _L0_ffn_in['conv_w'], 'L0_ffn_attn_w': _L0_ffn_in['attn_w'], 'L0_ffn_proj_w': _L0_ffn_in['proj_w'], 'L0_ffn_router_w': _L0_ffn_in['router_w'], 'L0_ffn_expert_wv': _L0_ffn_in['expert_wv'], 'L0_ffn_expert_proj': _L0_ffn_in['expert_proj'], 'L1_xattn_Wq': _L1_xattn_in['Wq'], 'L1_xattn_Wkv': _L1_xattn_in['Wkv'], 'L1_xattn_Wout': _L1_xattn_in['Wout'], 'L1_xattn_bout': _L1_xattn_in['bout'], 'L1_ffn_Win': _L1_ffn_in['Win'], 'L1_ffn_bin_': _L1_ffn_in['bin_'], 'L1_ffn_W1': _L1_ffn_in['W1'], 'L1_ffn_b1': _L1_ffn_in['b1'], 'L1_ffn_W2': _L1_ffn_in['W2'], 'L1_ffn_b2': _L1_ffn_in['b2'], 'L1_ffn_Wout': _L1_ffn_in['Wout'], 'L1_ffn_bout': _L1_ffn_in['bout']}

def reference(x, ctx_1024, mask_BxS2_bk0, mask_BxS_ik0, L0_xattn_Wq, L0_xattn_bq, L0_xattn_Wk, L0_xattn_bk, L0_xattn_Wo, L0_xattn_bo, L0_ffn_ln1_w, L0_ffn_ln1_b, L0_ffn_ln2_w, L0_ffn_ln2_b, L0_ffn_conv_w, L0_ffn_attn_w, L0_ffn_proj_w, L0_ffn_router_w, L0_ffn_expert_wv, L0_ffn_expert_proj, L1_xattn_Wq, L1_xattn_Wkv, L1_xattn_Wout, L1_xattn_bout, L1_ffn_Win, L1_ffn_bin_, L1_ffn_W1, L1_ffn_b1, L1_ffn_W2, L1_ffn_b2, L1_ffn_Wout, L1_ffn_bout):
    import jax
    import jax.numpy as jnp

    def _L0_xattn_ref(Q, K, V, Wq, bq, Wk, bk, Wo, bo, key_padding_mask):
        import jax, jax.numpy as jnp
        import numpy as np
        B, TQ, TK = (2, 256, 256)
        DQ = DK = DV = 128
        QK_DIM, H = (32, 8)
        HD = QK_DIM // H
        OUT_DIM = 128
        b, tq, _ = Q.shape
        tk = K.shape[1]
        dv = V.shape[-1]
        Ql = (Q @ Wq.T + bq).reshape(b, tq, H, HD).transpose(0, 2, 1, 3)
        Kl = (K @ Wk.T + bk).reshape(b, tk, H, HD).transpose(0, 2, 1, 3)
        scale = HD ** 0.5
        scores = jnp.einsum('bhqd,bhkd->bhqk', Ql, Kl) / scale
        neg_inf = jnp.float32(-jnp.inf)
        scores = jnp.where(jnp.isnan(scores), neg_inf, scores)
        scores = jnp.where(key_padding_mask[:, None, None, :], neg_inf, scores)
        attn = jax.nn.softmax(scores, axis=-1)
        out = jnp.einsum('bhqk,bkd->bqhd', attn, V).reshape(b, tq, H * dv)
        return out @ Wo.T + bo

    def _L0_ffn_ref(x, ln1_w, ln1_b, ln2_w, ln2_b, conv_w, attn_w, proj_w, router_w, expert_wv, expert_proj):
        import jax, jax.numpy as jnp
        import numpy as np
        EPS = 1e-05

        def _layernorm(x, w, b):
            mu = jnp.mean(x, axis=-1, keepdims=True)
            var = jnp.mean((x - mu) ** 2, axis=-1, keepdims=True)
            return (x - mu) * jax.lax.rsqrt(var + EPS) * w + b

        def _rope_tables(T, D, base=10000.0):
            inv_freq = 1.0 / base ** (jnp.arange(0, D, 2, dtype=jnp.float32) / D)
            t = jnp.arange(T, dtype=jnp.float32)
            freqs = jnp.einsum('i,j->ij', t, inv_freq)
            emb = jnp.concatenate([freqs, freqs], axis=-1)
            return (jnp.cos(emb), jnp.sin(emb))

        def _rotate_half(x):
            x1, x2 = (x[..., :x.shape[-1] // 2], x[..., x.shape[-1] // 2:])
            return jnp.concatenate([-x2, x1], axis=-1)

        def _attn(x, ln_w, ln_b, conv_w, attn_w, proj_w, n_head):
            B, T, C = x.shape
            D = C // n_head
            h = _layernorm(x, ln_w, ln_b)
            hc = jnp.transpose(h, (0, 2, 1))
            hc = jnp.pad(hc, ((0, 0), (0, 0), (2, 0)))
            hc = jax.lax.conv_general_dilated(hc, conv_w, window_strides=(1,), padding='VALID', dimension_numbers=('NCH', 'OIH', 'NCH'), feature_group_count=C)
            h = jnp.transpose(hc, (0, 2, 1))
            qkv = h @ attn_w
            q, k, v = jnp.split(qkv, 3, axis=-1)
            q = q.reshape(B, T, n_head, D)
            k = k.reshape(B, T, n_head, D)
            v = v.reshape(B, T, n_head, D)
            cos, sin = _rope_tables(T, D)
            cos = cos[None, :, None, :]
            sin = sin[None, :, None, :]
            q = q * cos + _rotate_half(q) * sin
            k = k * cos + _rotate_half(k) * sin
            scores = jnp.einsum('bqhd,bkhd->bhqk', q, k) / jnp.sqrt(jnp.float32(D))
            causal = jnp.tril(jnp.ones((T, T), dtype=bool))
            scores = jnp.where(causal, scores, jnp.float32(-1e+30))
            p = jax.nn.softmax(scores, axis=-1)
            y = jnp.einsum('bhqk,bkhd->bqhd', p, v).reshape(B, T, C)
            return y @ proj_w

        def _moe(x, ln_w, ln_b, router_w, expert_wv, expert_proj):
            h = _layernorm(x, ln_w, ln_b)
            logits = h @ router_w
            expert_idx = jnp.argmax(logits, axis=-1)
            E = router_w.shape[-1]
            out = jnp.zeros_like(x)
            for e in range(E):
                gv = h @ expert_wv[e]
                gate_raw, value = jnp.split(gv, 2, axis=-1)
                y = gate_raw * jax.nn.sigmoid(gate_raw) * value @ expert_proj[e]
                out = out + jnp.where((expert_idx == e)[..., None], y, 0.0)
            return out
        n_head = 16
        x = x + _attn(x, ln1_w, ln1_b, conv_w, attn_w, proj_w, n_head)
        x = x + _moe(x, ln2_w, ln2_b, router_w, expert_wv, expert_proj)
        return x

    def _L1_xattn_ref(x, context, mask, Wq, Wkv, Wout, bout):
        import jax, jax.numpy as jnp
        import numpy as np
        HEADS = 16
        DIM_HEAD = 64
        SCALE = DIM_HEAD ** (-0.5)
        MASK_NEG = 1000000.0

        def _split_heads(t):
            b, n, _ = t.shape
            return t.reshape(b, n, HEADS, DIM_HEAD).transpose(0, 2, 1, 3)
        kv = context @ Wkv
        k, v = jnp.split(kv, 2, axis=-1)
        q = x @ Wq
        q, k, v = (_split_heads(q), _split_heads(k), _split_heads(v))
        dots = jnp.einsum('bhnd,bhmd->bhnm', q, k) * SCALE
        dots = dots - (1.0 - mask.astype(jnp.float32))[:, None, :, None] * MASK_NEG
        attn = jax.nn.softmax(dots, axis=-1)
        out = jnp.einsum('bhnm,bhmd->bhnd', attn, v)
        b, h, n, d = out.shape
        out = out.transpose(0, 2, 1, 3).reshape(b, n, h * d)
        return out @ Wout + bout

    def _L1_ffn_ref(x, Win, bin_, W1, b1, W2, b2, Wout, bout):
        import jax, jax.numpy as jnp
        import numpy as np
        D_MODEL = 128
        M = 64
        INNER = 16
        s = jnp.einsum('btd,dm->btm', x, Win) + bin_
        h = jax.nn.relu(s[..., None] * W1 + b1)
        g = jnp.einsum('btmh,mh->btm', h, W2) + b2
        out = jnp.einsum('btm,md->btd', g, Wout) + bout
        return out
    x = x + _L0_xattn_ref(_layernorm(x, axis=-1), ctx_1024, ctx_1024, L0_xattn_Wq, L0_xattn_bq, L0_xattn_Wk, L0_xattn_bk, L0_xattn_Wo, L0_xattn_bo, mask_BxS2_bk0)
    x = x + _L0_ffn_ref(_layernorm(x, axis=-1), L0_ffn_ln1_w, L0_ffn_ln1_b, L0_ffn_ln2_w, L0_ffn_ln2_b, L0_ffn_conv_w, L0_ffn_attn_w, L0_ffn_proj_w, L0_ffn_router_w, L0_ffn_expert_wv, L0_ffn_expert_proj)
    x = x + _L1_xattn_ref(_layernorm(x, axis=-1), ctx_1024, mask_BxS_ik0, L1_xattn_Wq, L1_xattn_Wkv, L1_xattn_Wout, L1_xattn_bout)
    x = x + _L1_ffn_ref(_layernorm(x, axis=-1), L1_ffn_Win, L1_ffn_bin_, L1_ffn_W1, L1_ffn_b1, L1_ffn_W2, L1_ffn_b2, L1_ffn_Wout, L1_ffn_bout)
    return x

_drawn_inputs = setup_inputs


def setup_inputs(seed=0):
    import zlib

    import numpy as np

    out = dict(_drawn_inputs(seed))
    spreads = {'L0_xattn_bq': (0.0, 0.8),
     'L0_xattn_bk': (0.0, 2.0),
     'L0_xattn_bo': (0.0, 0.1),
     'L0_ffn_ln1_w': (1.0, 0.6),
     'L0_ffn_ln1_b': (0.0, 0.8),
     'L0_ffn_ln2_w': (1.0, 0.6),
     'L0_ffn_ln2_b': (0.0, 0.8),
     'L1_xattn_bout': (0.0, 2.0)}
    factors = {'L0_xattn_Wq': 8.0,
     'L0_xattn_Wk': 8.0,
     'L0_ffn_conv_w': 8.0,
     'L0_ffn_attn_w': 8.0,
     'L0_ffn_proj_w': 8.0,
     'L0_ffn_router_w': 8.0,
     'L0_ffn_expert_wv': 8.0,
     'L0_ffn_expert_proj': 8.0,
     'L1_ffn_bin_': 64.0,
     'L1_xattn_Wq': 6.946,
     'L1_xattn_Wkv': 2.735,
     'L1_xattn_Wout': 2.851,
     'L1_ffn_Win': 8.0,
     'L1_ffn_W1': 8.0,
     'L1_ffn_b1': 8.0,
     'L1_ffn_W2': 8.0,
     'L1_ffn_b2': 28.628,
     'L1_ffn_Wout': 8.0,
     'L1_ffn_bout': 64.0}
    for name, (base, spread) in spreads.items():
        noise = np.random.default_rng([zlib.crc32(name.encode()), seed]).standard_normal(out[name].shape)
        drawn = base * np.exp(spread * noise) if base else spread * noise
        out[name] = jnp.asarray(drawn.astype(out[name].dtype))
    for name, factor in factors.items():
        out[name] = (out[name] * factor).astype(out[name].dtype)
    return out
```

```python
from contextlib import ExitStack

import numpy as np

import concourse.bass as bass
from concourse import mybir

F32 = mybir.dt.float32
BF16 = mybir.dt.bfloat16
I32 = mybir.dt.int32
U8 = mybir.dt.uint8
ALU = mybir.AluOpType
ACT = mybir.ActivationFunctionType
AX = mybir.AxisListType

P = 128
B, T, D = 2, 512, 128
QT = T // P
NT = B * QT
KEYS = 154
KM, KR = 128, 26
KPAD = 160
HA, HDA = 8, 4
HB, HDB = 16, 8
HC, HDC = 16, 64
GH = 8
BANK_HEADS = ((0, 3), (3, 6), (6, 8))
UW = GH * KEYS
BLK = GH + GH // 4
E, FF = 4, 512
FC = FF // P
NEG = -1.0e30
EPS = 1.0e-5
MASK_NEG = 1.0e6
INNER = 16
M1 = 64
ROWS = 96
SPLIT = 9 * HDB

(V_LN1W, V_LN1B, V_LN2W, V_LN2B, V_CONV, V_W1, V_B1, V_W2, V_BIN, V_B2, V_BQ, V_BK, V_HM) = (
    0, 1, 2, 3, 4, 7, 15, 23, 31, 32, 33, 34, 35)
V_N = 43
R_BO, R_BOUT1, R_BOUT2, R_RANK, R_N = 0, 1, 2, 3, 4


class Own:

    def __init__(self, eng, sem):
        self.eng, self.sem, self.n = eng, sem, 0

    def __call__(self, ins):
        ins.then_inc(self.sem, 1)
        self.n += 1

    def wait(self):
        self.eng.wait_ge(self.sem, self.n)


class Carve:

    def __init__(self, tensor):
        self.t, self.at = tensor, 0

    def f32(self, cols, rows=P):
        a = self.t[0:rows, self.at:self.at + cols]
        self.at += cols
        return a

    def bf16(self, cols, rows=P):
        return self.f32(cols // 2, rows).bitcast(BF16)


def program(nc, t_in, out):
    ctx = ExitStack()
    with ctx:
        def sb(name, shape, dt=F32):
            return ctx.enter_context(nc.sbuf_tensor(name, shape, dt))

        def sem(name):
            return ctx.enter_context(nc.semaphore(name))

        X = sb("X", [P, NT, D])
        U = sb("U", [P, NT, D])
        XN = sb("XN", [P, NT, D])
        XT = sb("XT", [P, B, T])
        HT = sb("HT", [P, B, T + 2])
        HC2 = sb("HC2", [P, B, T])
        vec = sb("vec", [P, V_N])
        rowv = sb("rowv", [P, R_N, D])
        cst = sb("cst", [P, 3, P])
        cstb = sb("cstb", [P, 3, P], BF16)
        cossin = sb("cossin", [P, 2, T])
        ctxT = sb("ctxT", [P, B, KPAD])
        ones = sb("ones", [P, P])
        onesb = sb("onesb", [P, P], BF16)
        maskx = sb("maskx", [P, NT], I32)
        rowbias = sb("rowbias", [P, NT])
        stats = sb("stats", [P, NT, 6])
        mv = sb("mv", [P, NT, 2])
        ve = sb("ve", [P, NT])
        rstd = sb("rstd", [P, NT])
        minus_half = sb("minus_half", [P, NT])
        mraw = sb("mraw", [P, 2, GH])
        umax = sb("umax", [P, 2, GH])
        usum = sb("usum", [P, 3, GH])
        urec = sb("urec", [P, 3, GH])
        mB = sb("mB", [P, B, HB, QT])
        nmf = sb("nmf", [HB * QT, 3, P])
        nm3 = sb("nm3", [HB * QT, B, 3, P], BF16)
        rB = sb("rB", [P, 2, HB])
        lg = sb("lg", [P, 4, NT, E])
        mx = sb("mx", [P, 2, NT])
        onehot = sb("onehot", [P, NT, E])
        rw = sb("rw", [P, E])
        b2r = sb("b2r", [M1, P])
        wout2 = sb("wout2", [P, D])
        WW = sb("WW", [P, GH, D])
        win2 = sb("win2", [P, P])
        cbias = sb("cbias", [P, D])
        aqkv = sb("aqkv", [P, 5, P])
        projw = sb("projw", [P, D])
        kkC = sb("kkC", [P, B, HC * KEYS])
        vwCm = sb("vwCm", [P, B, HC * D])
        vwCr = sb("vwCr", [P, B, HC // 4, D])

        cw = sb("cw", [P, 7632])
        c = Carve(cw)
        wkC = c.f32(HC * HDC)
        wvC = c.f32(HC * HDC)
        wqT = c.f32(HC * HDC).rearrange("p (c d) -> p c d", c=8)
        woutZ = c.f32(HC * D).rearrange("p (c j o) -> p c j o", c=8, j=2)
        kz = c.f32(2 * 2 * B * KEYS).rearrange("p (r j n) -> p r j n", r=2, j=2)
        vT = c.f32(4 * B * KPAD).rearrange("p (r n) -> p r n", r=4)
        assert c.at <= 7632
        c = Carve(cw)
        vaug = c.f32(B * QT * HB * 32).rearrange("p (b t h m) -> p b t h m", b=B, t=QT, h=HB)
        yg = c.f32(4 * T).rearrange("p (g q) -> p g q", g=4)
        yn = c.f32(2 * D).rearrange("p (r d) -> p r d", r=2)
        yT = c.f32(2 * P).rearrange("p (r q) -> p r q", r=2)

        BIGW = 22000
        big = sb("big", [P, BIGW])
        c = Carve(big)
        Pt = [c.f32(UW).rearrange("p (h k) -> p h k", h=GH) for _ in range(3)]
        PN = [c.f32(BLK * P) for _ in range(2)]
        PT = [c.f32(BLK * P).rearrange("p (n q) -> p n q", n=BLK) for _ in range(2)]
        kkA = c.f32(B * UW).rearrange("p (b n) -> p b n", b=B)
        vwAm = c.f32(B * HA * D).rearrange("p (b n) -> p b n", b=B)
        vwAr = c.f32(B * 2 * D).rearrange("p (b g o) -> p b g o", b=B, g=2)
        woT = c.f32(HA * D)
        KzA = c.f32(B * UW, HA * HDA).rearrange("p (b h k) -> p b h k", b=B, h=HA)
        KTA = c.f32(B * KEYS, HA * HDA).rearrange("p (b k) -> p b k", b=B)
        wqA = c.f32(D, HA * HDA)
        wkTA = c.f32(HA * HDA)
        brow = c.f32(B * UW, 1)
        browb = c.bf16(B * UW).rearrange("p (b n) -> p b n", b=B)
        mrow = c.f32(B * KEYS, 1).rearrange("p (b k) -> p b k", b=B)
        mask_words = c.f32(B * KEYS // 4, 1).bitcast(I32)
        masku = mask_words.bitcast(U8)
        br1 = big[0:1, 0:B * UW]
        brh = big[0:1, B * UW:B * UW + B * UW // 2].bitcast(BF16)
        brl = big[0:1, 2 * B * UW:2 * B * UW + B * UW // 2].bitcast(BF16)
        assert c.at <= BIGW, c.at
        c = Carve(big)
        ks, qs = [], []
        for b in range(B):
            ks.append(c.bf16(HB * T, ROWS).rearrange("p (h t) -> p h t", h=HB))
            qs.append(c.bf16(HB * T, ROWS).rearrange("p (h t) -> p h t", h=HB))
        at = c.at
        qk = c.f32(2 * T).rearrange("p (s t) -> p s t", s=2)
        tsin = c.f32(2 * T).rearrange("p (s t) -> p s t", s=2)
        P3 = c.bf16(2 * 3 * T).rearrange("p (s a t) -> p s a t", s=2, a=3)
        assert c.at <= BIGW, c.at
        c.at = at
        PTb = c.f32(8 * T).rearrange("p (n q) -> p n q", n=8)
        assert c.at <= BIGW, c.at
        c = Carve(big)
        wv = c.f32(E * 2 * FF).rearrange("p (e n) -> p e n", e=E)
        pj = c.f32(E * FC * D).rearrange("p (e f d) -> p e f d", e=E, f=FC)
        c.at = HB * T
        sg = c.f32(2 * T).rearrange("p (r t) -> p r t", r=2)
        G = c.f32(2 * FC * T).rearrange("p (r f t) -> p r f t", r=2, f=FC)
        c = Carve(big)
        sT = c.f32(B * T).rearrange("p (b t) -> p b t", b=B)
        RJ = c.f32(B * GH * T).rearrange("p (b j t) -> p b j t", b=B, j=GH)

        PS = ctx.enter_context(nc.psum_tensor("PS", [P, 8, 512], F32))
        scr_qk = nc.dram_tensor("scr_qk", (B, 2, 3, P, T), BF16, kind="Internal").ap()
        scr_m = nc.dram_tensor("scr_m", (B, 3, HB * QT * P), BF16, kind="Internal").ap()

        def prec_jobs():
            for c in range(HC // 2 + 1):
                if c < HC // 2:
                    yield "k", c, 2
                    yield "v", c, 1
                if c >= 1:
                    yield "kk", 2 * c - 2, 1
                    yield "kk", 2 * c - 1, 1
                if c >= 2 and c % 2 == 0:
                    for b in range(B):
                        yield "vw", (c // 2 - 1, b), 1
                        yield "vr", (c // 2 - 1, b), 1

        PREC = list(prec_jobs())
        N_PREC = sum(j[2] for j in PREC)

        ld_x = [sem(f"ld_x{b}") for b in range(B)]
        ld_a, ld_vec, ld_c, ld_b, ld_moe, ld_d = (sem(n) for n in (
            "ld_a", "ld_vec", "ld_c", "ld_b", "ld_moe", "ld_d"))
        zeroed = sem("zeroed")
        zeroedB = sem("zeroedB")
        zeroedC = sem("zeroedC")
        LNS = ("a", "u", "b", "m", "c", "d")
        ln_var = {n: sem(f"ln_var_{n}") for n in LNS}
        ln_rstd = {n: sem(f"ln_rstd_{n}") for n in LNS}
        ln_norm = {n: sem(f"ln_norm_{n}") for n in LNS}
        ln_turned = {n: sem(f"ln_turned_{n}") for n in LNS if n != "u"}
        ln_T = {n: sem(f"ln_T_{n}") for n in LNS if n != "u"}
        preA_mm, preA_act, preA_dve = sem("preA_mm"), sem("preA_act"), sem("preA_dve")
        kzA_ready, brow_ready, consts_ready = sem("kzA_ready"), sem("brow_ready"), sem("consts_ready")
        preC_mm, preC_act = sem("preC_mm"), sem("preC_act")
        scores_mm = {s: sem(f"scores_mm_{s}") for s in "AC"}
        unit_max = {s: sem(f"unit_max_{s}") for s in "AC"}
        unit_shift = {s: sem(f"unit_shift_{s}") for s in "AC"}
        unit_exp = {s: sem(f"unit_exp_{s}") for s in "AC"}
        unit_rec = {s: sem(f"unit_rec_{s}") for s in "AC"}
        unit_norm = {s: sem(f"unit_norm_{s}") for s in "AC"}
        unit_turned = {s: sem(f"unit_turned_{s}") for s in "AC"}
        unit_PT = {s: sem(f"unit_PT_{s}") for s in "AC"}
        tile_mm = {s: sem(f"tile_mm_{s}") for s in "AC"}
        tile_added = {s: sem(f"tile_added_{s}") for s in "AC"}
        conv_ready = sem("conv_ready")
        qkv_mm, rope_read, v_ready = sem("qkv_mm"), sem("rope_read"), sem("v_ready")
        qk_ready, part_hi, part_r1, part_mid, part_lo = (sem(n) for n in (
            "qk_ready", "part_hi", "part_r1", "part_mid", "part_lo"))
        scr_written = [sem(f"scr_written{b}") for b in range(B)]
        stack_ready = [sem(f"stack_ready{b}") for b in range(B)]
        s_mm, s_max = sem("s_mm"), sem("s_max")
        m_turned, m_split = sem("m_turned"), sem("m_split")
        m_written = [sem(f"m_written{b}") for b in range(B)]
        m_ready = [sem(f"m_ready{b}") for b in range(B)]
        st_mm, st_exp, av_step, yg_ready = sem("st_mm"), sem("st_exp"), sem("av_step"), sem("yg_ready")
        y_turned, y_norm, yT_mm, yT_ready, proj_mm, attn_added = (sem(n) for n in (
            "y_turned", "y_norm", "yT_mm", "yT_ready", "proj_mm", "attn_added"))
        logit_mm, routed = sem("logit_mm"), sem("routed")
        gv_mm, gate_ready, g_ready, moe_mm, moe_added = (sem(n) for n in (
            "gv_mm", "gate_ready", "g_ready", "moe_mm", "moe_added"))
        cb_mm, cb_ready, ww_ready = sem("cb_mm"), sem("cb_ready"), sem("ww_ready")
        s_in_mm, s_in_ready, relu_ready, ffn_mm, ffn_added = (sem(n) for n in (
            "s_in_mm", "s_in_ready", "relu_ready", "ffn_mm", "ffn_added"))
        stored = sem("stored")
        own_dve, own_act, own_pool = sem("own_dve"), sem("own_act"), sem("own_pool")

        UNITS = {"A": NT, "C": 2 * NT}
        PER = {"A": 1, "C": 2}
        LN_BANK = 7
        NA_KK = B * len(BANK_HEADS)

        ident = cst[:, 0, :]
        identb, mask_qk, mask_kq = cstb[:, 0, :], cstb[:, 1, :], cstb[:, 2, :]
        block = ctx.enter_context(nc.Block())

        @block.sync
        def _(sp):
            i = t_in
            x_t = i["x"].rearrange("b (t p) d -> p b t d", p=P)
            sp.dma_start(ctxT[:, :, 0:KEYS], i["ctxT"]).then_inc(ld_a, 16)
            sp.dma_start(wkTA, i["A_WkT"]).then_inc(ld_a, 16)
            sp.dma_start(vec[:], i["vec"]).then_inc(ld_vec, 16)
            sp.dma_start(cst[:], i["consts"]).then_inc(ld_vec, 16)
            sp.dma_start(X[:, 0:QT, :], x_t[:, 0]).then_inc(ld_x[0], 16)
            sp.dma_start(wqA, i["A_Wq"]).then_inc(ld_a, 16)
            sp.dma_start(X[:, QT:NT, :], x_t[:, 1]).then_inc(ld_x[1], 16)
            sp.dma_start(woT, i["A_WoT"]).then_inc(ld_a, 16)
            sp.dma_start(mask_words, i["mask_keys"]).then_inc(ld_a, 16)
            sp.dma_start(rowv[:], i["rows"].unsqueeze(0).to_broadcast([P, R_N, D])).then_inc(ld_vec, 16)
            sp.dma_start(maskx[:], i["mask_x"]).then_inc(ld_vec, 16)
            sp.dma_start(wkC, i["C_Wk"]).then_inc(ld_c, 16)
            sp.dma_start(wvC, i["C_Wv"]).then_inc(ld_c, 16)
            sp.dma_start(wqT, i["C_WqT"].rearrange("(c p) d -> p c d", p=P)).then_inc(ld_c, 16)
            sp.wait_ge(zeroed, 1)
            for j in range(2):
                sp.dma_start(woutZ[64 * j:64 * j + 64, :, j, :],
                             i["C_Wout"].rearrange("(c j e) o -> j e c o", j=2, e=HDC)[j]).then_inc(ld_c, 16)
            sp.dma_start(aqkv[:], i["B_qkv"].rearrange("p (s n) -> p s n", s=5)).then_inc(ld_b, 16)
            sp.dma_start(cossin[:], i["cossin"]).then_inc(ld_b, 16)
            sp.dma_start(projw[:], i["B_proj"]).then_inc(ld_b, 16)
            sp.dma_start(rw[:], i["router"]).then_inc(ld_b, 16)
            for j in range(2):
                sp.dma_start(win2[:, 64 * j:64 * j + 64], i["D_Win"]).then_inc(ld_d, 16)
                sp.dma_start(wout2[64 * j:64 * j + 64, :], i["D_Wout"]).then_inc(ld_d, 16)
            for b in range(B):
                sp.wait_ge(part_lo, b + 1)
                sp.dma_start(scr_qk[b].rearrange("s a r t -> r s a t"), P3).then_inc(scr_written[b], 16)
                sp.wait_ge(scr_written[b], 16)
                sp.wait_ge(zeroedB, 4)
                for a in range(3):
                    sp.dma_start(ks[b][24 * a:24 * a + 24, :, :],
                                 scr_qk[b, 1].rearrange("a (d h) t -> (a d) h t", h=HB)).then_inc(stack_ready[b], 16)
                    for j in range(3):
                        r = 24 * a + 8 * j
                        sp.dma_start(qs[b][r:r + 8, :, :],
                                     scr_qk[b, 0, a].rearrange("(d h) t -> d h t", h=HB)).then_inc(stack_ready[b], 16)
            for b in range(B):
                sp.wait_ge(m_split, b + 1)
                sp.dma_start(scr_m[b].rearrange("a (n q) -> n a q", q=P), nm3[:, b]).then_inc(m_written[b], 16)
                sp.wait_ge(m_written[b], 16)
                sp.wait_ge(s_mm, 32 * (b + 1))
                sp.dma_start(qs[b][SPLIT:SPLIT + 3, :, :],
                             scr_m[b].rearrange("a (h t) -> a h t", h=HB)).then_inc(m_ready[b], 16)
            sp.wait_ge(st_mm, 32)
            sp.dma_start(wv, i["wv"].rearrange("e p n -> p e n")).then_inc(ld_moe, 16)
            sp.dma_start(pj, i["pj"].rearrange("e (f p) d -> p e f d", p=P)).then_inc(ld_moe, 16)
            for n in range(NT):
                sp.wait_ge(ffn_added, n + 1)
                sp.dma_start(out.rearrange("b (t p) d -> p (b t) d", p=P)[:, n, :], X[:, n, :]).then_inc(stored, 16)
            sp.wait_ge(stored, 16 * NT)

        @block.gpsimd
        def _(pool):
            own = Own(pool, own_pool)
            pool.memset(woutZ, 0.0).then_inc(zeroed, 1)
            pool.memset(ctxT[:, :, KEYS:KPAD], 0.0).then_inc(zeroed, 1)
            pool.memset(ones[:], 1.0).then_inc(zeroed, 1)
            pool.memset(onesb[:], 1.0).then_inc(zeroed, 1)
            pool.memset(browb, 0.0).then_inc(zeroed, 1)
            pool.memset(minus_half[:], -0.5).then_inc(zeroed, 1)
            pool.memset(HT[:, :, 0:2], 0.0).then_inc(zeroed, 1)
            pool.memset(kz, 0.0).then_inc(zeroed, 1)
            for r in range(2):
                pool.memset(PN[r][:, GH * P:BLK * P], 0.0).then_inc(zeroed, 1)
            pool.wait_ge(zeroed, 10)

            def ln_rsqrt(name):
                for b in range(B):
                    pool.wait_ge(ln_var[name], b + 1)
                    s = slice(b * QT, b * QT + QT)
                    pool.tensor_tensor(rstd[:, s], ve[:, s], minus_half[:, s], ALU.pow).then_inc(ln_rstd[name], 1)

            def unit_norms(st):
                for u in range(UNITS[st]):
                    pool.wait_ge(unit_rec[st], u + 1)
                    if u >= 2:
                        pool.wait_ge(unit_turned[st], u - 1)
                    r = urec[:, u % 3, :].unsqueeze(2)
                    pn = PN[u % 2]
                    pool.tensor_tensor(pn[:, 0:GH * P].rearrange("p (h k) -> p h k", h=GH),
                                       Pt[u % 3][:, :, 0:KM], r.to_broadcast([P, GH, KM]), ALU.mult).then_inc(unit_norm[st], 1)
                    pool.tensor_tensor(pn[:, GH * P:BLK * P].rearrange("p (h k) -> p h k", h=GH)[:, :, 0:KR],
                                       Pt[u % 3][:, :, KM:KEYS], r.to_broadcast([P, GH, KR]), ALU.mult).then_inc(unit_norm[st], 1)

            ln_rsqrt("a")
            unit_norms("A")
            ln_rsqrt("u")
            pool.wait_ge(tile_mm["A"], NT)
            pool.wait_ge(ln_rstd["u"], B)
            for b in range(B):
                pool.memset(qs[b][64:ROWS], 0.0).then_inc(zeroedB, 1)
                pool.memset(ks[b][64:ROWS], 1.0).then_inc(zeroedB, 1)
            pool.wait_ge(preC_act, N_PREC)
            pool.wait_ge(zeroedB, 4)
            pool.memset(vaug, 0.0).then_inc(zeroedB, 1)
            pool.wait_ge(zeroedB, 5)
            pool.memset(vaug[:, :, :, :, HDB:HDB + 1], 1.0).then_inc(zeroedB, 1)
            ln_rsqrt("b")
            ln_rsqrt("m")
            ln_rsqrt("c")
            for r in range(2):
                pool.memset(PN[r][:, GH * P:BLK * P], 0.0).then_inc(zeroedC, 1)
            pool.wait_ge(zeroedC, 2)
            unit_norms("C")
            ln_rsqrt("d")

        @block.vector
        def _(dve):
            own = Own(dve, own_dve)
            tile = lambda n: slice(n, n + 1)

            def ln_stats(name, src, b, ready):
                ready()
                for n in range(b * QT, b * QT + QT):
                    own(dve.bn_stats(stats[:, n, :], src[:, n, :]))
                own.wait()
                for n in range(b * QT, b * QT + QT):
                    own(dve.bn_aggr(mv[:, n, :], stats[:, n, :]))
                own.wait()
                s = slice(b * QT, b * QT + QT)
                dve.tensor_scalar(ve[:, s], mv[:, s, 1], EPS, None, ALU.add).then_inc(ln_var[name], 1)

            def ln_apply(name, src, dst, b):
                dve.wait_ge(ln_rstd[name], b + 1)
                for n in range(b * QT, b * QT + QT):
                    dve.tensor_scalar(dst[:, n, :], src[:, n, :], mv[:, n, 0:1], rstd[:, tile(n)],
                                      ALU.subtract, ALU.mult).then_inc(ln_norm[name], 1)

            def units(st, bias):
                op0 = ALU.max if st == "A" else ALU.add
                for u in range(UNITS[st] + 1):
                    if u < UNITS[st]:
                        bank = 3 * (u % 2)
                        for k, (h0, h1) in enumerate(BANK_HEADS):
                            dve.wait_ge(scores_mm[st], 3 * u + k + 1)
                            s = PS[:, bank + k, 0:(h1 - h0) * KEYS].rearrange("p (h k) -> p h k", h=h1 - h0)
                            own(dve.tensor_reduce(mraw[:, u % 2, h0:h1], s, AX.X, ALU.max))
                        own.wait()
                        sc = bias(u)
                        own(dve.tensor_scalar(umax[:, u % 2, :], mraw[:, u % 2, :], sc, None, op0))
                        own.wait()
                        if u >= 3:
                            dve.wait_ge(unit_norm[st], 2 * (u - 2))
                        for k, (h0, h1) in enumerate(BANK_HEADS):
                            s = PS[:, bank + k, 0:(h1 - h0) * KEYS].rearrange("p (h k) -> p h k", h=h1 - h0)
                            dve.scalar_tensor_tensor(
                                Pt[u % 3][:, h0:h1, :], s, sc,
                                umax[:, u % 2, h0:h1].unsqueeze(2).to_broadcast([P, h1 - h0, KEYS]),
                                op0, ALU.subtract).then_inc(unit_shift[st], 1)
                    if u >= 1:
                        v = u - 1
                        dve.wait_ge(unit_exp[st], v + 1)
                        own(dve.tensor_reduce(usum[:, v % 3, :], Pt[v % 3], AX.X, ALU.add))
                        own.wait()
                        dve.reciprocal(urec[:, v % 3, :], usum[:, v % 3, :]).then_inc(unit_rec[st], 1)
                    if u >= 3 and (u - 3) % PER[st] == PER[st] - 1:
                        add_tile(st, (u - 3) // PER[st])
                for n in range((UNITS[st] - 2) // PER[st], NT):
                    add_tile(st, n)

            def add_tile(st, n):
                dve.wait_ge(tile_mm[st], n + 1)
                dve.tensor_tensor(X[:, n, :], PS[:, 6, 0:D], X[:, n, :], ALU.add).then_inc(tile_added[st], 1)

            dve.wait_ge(ld_vec, 64)
            dve.tensor_copy(cstb[:], cst[:]).then_inc(consts_ready, 1)
            own(dve.tensor_copy(rowbias[:], maskx[:]))
            own.wait()
            own(dve.tensor_scalar(rowbias[:], rowbias[:], -1.0, 1.0, ALU.mult, ALU.add))
            own.wait()
            own(dve.tensor_scalar(rowbias[:], rowbias[:], -MASK_NEG, None, ALU.mult))
            dve.wait_ge(preA_mm, 1)
            dve.tensor_scalar(KTA, PS[0:32, 0, 0:B * KEYS].rearrange("p (b k) -> p b k", b=B),
                              vec[0:32, V_BK:V_BK + 1], None, ALU.add).then_inc(preA_dve, 1)
            dve.wait_ge(preA_dve, 1)
            dve.wait_ge(ld_a, 80)
            for b in range(B):
                dve.tensor_tensor(KzA[:, b], KTA[:, b:b + 1, :].to_broadcast([32, HA, KEYS]),
                                  vec[0:32, V_HM:V_HM + HA].unsqueeze(2).to_broadcast([32, HA, KEYS]),
                                  ALU.mult).then_inc(kzA_ready, 1)
            own(dve.tensor_scalar(mrow, masku.rearrange("p (b k) -> p b k", b=B), NEG, None, ALU.mult))
            own.wait()
            for b in range(B):
                for k, (h0, h1) in enumerate(BANK_HEADS):
                    n = 3 * b + k
                    dve.wait_ge(preA_mm, 1 + NA_KK + n + 1)
                    dve.scalar_tensor_tensor(
                        brow[:, b * UW + h0 * KEYS:b * UW + h1 * KEYS].rearrange("p (h k) -> p h k", h=h1 - h0),
                        PS[0:1, 3 + n % 3, 0:(h1 - h0) * KEYS].rearrange("p (h k) -> p h k", h=h1 - h0), 0.5,
                        mrow[:, b:b + 1, :].to_broadcast([1, h1 - h0, KEYS]), ALU.mult, ALU.add).then_inc(preA_dve, 1)
            dve.wait_ge(preA_dve, 1 + NA_KK)
            dve.wait_ge(zeroed, 10)
            own(dve.tensor_copy(brh, brow))
            own.wait()
            dve.tensor_copy(browb[0:1].rearrange("p b n -> p (b n)"), brh).then_inc(brow_ready, 1)
            own(dve.tensor_tensor(br1, brow, brh, ALU.subtract))
            own.wait()
            own(dve.tensor_copy(brl, br1))
            own.wait()
            dve.tensor_copy(browb[32:33].rearrange("p b n -> p (b n)"), brl).then_inc(brow_ready, 1)
            dve.tensor_tensor(browb[64:65].rearrange("p b n -> p (b n)"), br1, brl, ALU.subtract).then_inc(brow_ready, 1)
            for b in range(B):
                ln_stats("a", X, b, lambda: dve.wait_ge(ld_x[b], 16))
            for b in range(B):
                ln_apply("a", X, XN, b)
            dve.wait_ge(ln_norm["a"], NT)
            for n in range(NT):
                own(dve.tensor_tensor(X[:, n, :], X[:, n, :], rowv[:, R_BO, :], ALU.add))
            own.wait()
            dve.wait_ge(brow_ready, 3)
            units("A", lambda u: -3.0e38)
            for b in range(B):
                ln_stats("u", X, b, lambda: dve.wait_ge(tile_added["A"], QT * b + QT))
            for b in range(B):
                ln_apply("u", X, U, b)
            for b in range(B):
                ln_stats("b", U, b, lambda: dve.wait_ge(ln_norm["u"], QT * b + QT))
            for b in range(B):
                ln_apply("b", U, XN, b)
            for b in range(B):
                dve.wait_ge(ln_T["b"], b + 1)
                h = HT[:, b, :]
                o = HC2[:, b, :]
                own(dve.tensor_scalar(o, h[:, 0:T], vec[:, V_CONV:V_CONV + 1], None, ALU.mult))
                own.wait()
                own(dve.scalar_tensor_tensor(o, h[:, 1:T + 1], vec[:, V_CONV + 1:V_CONV + 2], o, ALU.mult, ALU.add))
                own.wait()
                dve.scalar_tensor_tensor(o, h[:, 2:T + 2], vec[:, V_CONV + 2:V_CONV + 3], o,
                                         ALU.mult, ALU.add).then_inc(conv_ready, 1)
            dve.wait_ge(ld_b, 64)
            dve.wait_ge(zeroedB, 6)
            for b in range(B):
                if b:
                    dve.wait_ge(part_lo, b)
                for s in range(2):
                    dve.wait_ge(qkv_mm, 5 * b + 2 * s + 2)
                    own(dve.tensor_tensor(qk[:, s], PS[:, 2 * s, :], cossin[:, 0], ALU.mult))
                    own(dve.tensor_tensor(tsin[:, s], PS[:, 2 * s + 1, :], cossin[:, 1], ALU.mult))
                own.wait()
                dve.tensor_tensor(qk, qk, tsin, ALU.add).then_inc(qk_ready, 1)
                dve.wait_ge(qkv_mm, 5 * b + 5)
                dve.tensor_copy(vaug[:, b, :, :, 0:HDB],
                                PS[:, 4, :].rearrange("p (t h d) -> p t h d", t=QT, h=HB)).then_inc(v_ready, 1)
                dve.wait_ge(part_hi, b + 1)
                dve.wait_ge(qk_ready, b + 1)
                own(dve.tensor_tensor(qk, qk, P3[:, :, 0, :], ALU.subtract))
                own.wait()
                own(dve.tensor_copy(P3[:, :, 1, :], qk))
                own.wait()
                dve.tensor_tensor(P3[:, :, 2, :], qk, P3[:, :, 1, :], ALU.subtract).then_inc(part_lo, 1)
            for b in range(B):
                for n in range(32):
                    hp, qt = divmod(n, QT)
                    w = (qt + 1) * P
                    m = 32 * b + n
                    dve.wait_ge(s_mm, m + 1)
                    dve.tensor_reduce(mB[:, b, 2 * hp:2 * hp + 2, qt], PS[:, 2 * (m % 2):2 * (m % 2) + 2, 0:w],
                                      AX.X, ALU.max).then_inc(s_max, 1)
                dve.wait_ge(m_turned, b + 1)
                mt = PS[0:HB * QT, 4, 0:P]
                own(dve.tensor_scalar(nmf[:, 0], mt, -1.0, None, ALU.mult))
                own.wait()
                own(dve.tensor_copy(nm3[:, b, 0], nmf[:, 0]))
                own.wait()
                own(dve.tensor_tensor(nmf[:, 1], nmf[:, 0], nm3[:, b, 0], ALU.subtract))
                own.wait()
                own(dve.tensor_copy(nm3[:, b, 1], nmf[:, 1]))
                own.wait()
                dve.tensor_tensor(nm3[:, b, 2], nmf[:, 1], nm3[:, b, 1], ALU.subtract).then_inc(m_split, 1)
            for b in range(B):
                for g in range(4):
                    dve.wait_ge(av_step, QT * (4 * b + g + 1))
                    if b:
                        dve.wait_ge(y_turned, QT * b)
                    dve.tensor_copy(yg[:, g, :], PS[:, 4 + g % 2, :]).then_inc(yg_ready, 1)
                for qt in range(QT):
                    n = QT * b + qt
                    dve.wait_ge(y_turned, n + 1)
                    yv = PS[:, 6, :].rearrange("p (h m) -> p h m", h=HB)
                    own(dve.reciprocal(rB[:, n % 2, :].unsqueeze(2), yv[:, :, HDB:HDB + 1]))
                    own.wait()
                    if n >= 2:
                        dve.wait_ge(yT_mm, n - 1)
                    dve.tensor_tensor(yn[:, n % 2].rearrange("p (h d) -> p h d", h=HB), yv[:, :, 0:HDB],
                                      rB[:, n % 2, :].unsqueeze(2).to_broadcast([P, HB, HDB]), ALU.mult).then_inc(y_norm, 1)
                    dve.wait_ge(proj_mm, n + 1)
                    dve.tensor_tensor(U[:, n, :], PS[:, 7, P:2 * P], U[:, n, :], ALU.add).then_inc(attn_added, 1)
            for b in range(B):
                ln_stats("m", U, b, lambda: dve.wait_ge(attn_added, QT * b + QT))
            for b in range(B):
                ln_apply("m", U, XN, b)
            own(dve.tensor_tensor(X[:], X[:], U[:], ALU.add))
            dve.wait_ge(logit_mm, 1)
            L = PS[:, 6, 0:NT * E].rearrange("p (n e) -> p n e", e=E)
            own(dve.tensor_copy(lg[:, 0], L))
            own.wait()
            own(dve.tensor_reduce(mx[:, 0, :], lg[:, 0], AX.X, ALU.max))
            own.wait()
            own(dve.tensor_tensor(lg[:, 1], lg[:, 0], mx[:, 0, :].unsqueeze(2).to_broadcast([P, NT, E]), ALU.is_equal))
            own.wait()
            own(dve.tensor_tensor(lg[:, 2], lg[:, 1], rowv[:, R_RANK, 0:NT * E].rearrange("p (n e) -> p n e", e=E), ALU.mult))
            own.wait()
            own(dve.tensor_reduce(mx[:, 1, :], lg[:, 2], AX.X, ALU.max))
            own.wait()
            own(dve.tensor_tensor(onehot[:], lg[:, 2], mx[:, 1, :].unsqueeze(2).to_broadcast([P, NT, E]), ALU.is_equal))
            own.wait()

            def add_expert(n):
                e, b = divmod(n, B)
                dve.wait_ge(moe_mm, n + 1)
                if n >= B:
                    dve.wait_ge(moe_added, QT * (n - B + 1))
                for t in range(QT):
                    i = QT * b + t
                    dve.scalar_tensor_tensor(X[:, i, :], PS[:, 4 + n % 2, t * P:t * P + P], onehot[:, i, e:e + 1],
                                             X[:, i, :], ALU.mult, ALU.add).then_inc(moe_added, 1)

            for n in range(E * B):
                if n >= 2:
                    dve.wait_ge(moe_mm, n - 1)
                for f in range(FC):
                    k = FC * n + f
                    dve.wait_ge(gate_ready, k + 1)
                    dve.tensor_tensor(G[:, n % 2, f, :], sg[:, k % 2, :], PS[:, 2 * (k % 2) + 1, :], ALU.mult).then_inc(g_ready, 1)
                if n >= 1:
                    add_expert(n - 1)
            add_expert(E * B - 1)
            for b in range(B):
                ln_stats("c", X, b, lambda: dve.wait_ge(moe_added, E * NT))
            for b in range(B):
                ln_apply("c", X, XN, b)
            dve.wait_ge(ln_norm["c"], NT)
            for n in range(NT):
                own(dve.tensor_tensor(X[:, n, :], X[:, n, :], rowv[:, R_BOUT1, :], ALU.add))
            own.wait()
            units("C", lambda u: rowbias[:, tile(u // 2)])
            for b in range(B):
                ln_stats("d", X, b, lambda: dve.wait_ge(tile_added["C"], QT * b + QT))
            for b in range(B):
                ln_apply("d", X, XN, b)
            dve.wait_ge(ln_norm["d"], NT)
            dve.wait_ge(ld_d, 64)
            for j in range(GH):
                dve.tensor_scalar(WW[:, j, :], wout2[:], vec[:, V_W2 + j:V_W2 + j + 1], None, ALU.mult).then_inc(ww_ready, 1)
            dve.tensor_scalar(b2r[:], ones[0:M1, :], vec[0:M1, V_B2:V_B2 + 1], None, ALU.mult).then_inc(ww_ready, 1)
            dve.wait_ge(cb_mm, 1)
            dve.tensor_tensor(cbias[:], PS[:, 6, 0:D], rowv[:, R_BOUT2, :], ALU.add).then_inc(cb_ready, 1)
            dve.wait_ge(cb_ready, 1)
            for n in range(NT):
                own(dve.tensor_tensor(X[:, n, :], X[:, n, :], cbias[:], ALU.add))
            own.wait()
            for n in range(NT):
                dve.wait_ge(ffn_mm, n + 1)
                dve.tensor_tensor(X[:, n, :], PS[:, 4 + n % 2, 0:D], X[:, n, :], ALU.add).then_inc(ffn_added, 1)

        @block.scalar
        def _(act):
            def copy(dst, src, scale=1.0):
                return act.activation(dst, src, ACT.Copy, scale=scale)

            def ln_out(name, dst, w=None, bias=None):
                for b in range(B):
                    act.wait_ge(ln_turned[name], b + 1)
                    if w is None:
                        copy(dst[:, b, :], PS[:, LN_BANK, :]).then_inc(ln_T[name], 1)
                    else:
                        act.activation(dst[:, b, :], PS[:, LN_BANK, :], ACT.Identity,
                                       scale=w, bias=bias).then_inc(ln_T[name], 1)

            def units(st):
                for u in range(UNITS[st] + 1):
                    if u < UNITS[st]:
                        act.wait_ge(unit_shift[st], 3 * u + 3)
                        act.activation(Pt[u % 3], Pt[u % 3], ACT.Exp).then_inc(unit_exp[st], 1)
                    if u >= 1:
                        v = u - 1
                        act.wait_ge(unit_turned[st], v + 1)
                        copy(PT[v % 2].rearrange("p n q -> p (n q)"),
                             PS[:, 3 * (v % 2):3 * (v % 2) + 3, :].rearrange("p k n -> p (k n)")[:, 0:BLK * P])\
                            .then_inc(unit_PT[st], 1)

            m = 0
            for b in range(B):
                for h0, h1 in BANK_HEADS:
                    act.wait_ge(preA_mm, 1 + m + 1)
                    copy(kkA[:, b, h0 * KEYS:h1 * KEYS], PS[:, 1 + m % 2, 0:(h1 - h0) * KEYS], 0.5).then_inc(preA_act, 1)
                    m += 1
            for b in range(B):
                for half in range(2):
                    act.wait_ge(preA_mm, 1 + NA_KK + m + 1)
                    copy(vwAm[:, b, 512 * half:512 * half + 512], PS[:, 1 + m % 2, :]).then_inc(preA_act, 1)
                    m += 1
            for b in range(B):
                act.wait_ge(preA_mm, 1 + NA_KK + m + 1)
                copy(vwAr[:, b].rearrange("p g o -> p (g o)"), PS[:, 1 + m % 2, 0:2 * D]).then_inc(preA_act, 1)
                m += 1
            ln_out("a", XT)
            units("A")
            for n, (kind, i, _) in enumerate(PREC):
                act.wait_ge(preC_mm, n + 1)
                bank = n % 4
                if kind == "k":
                    if n == 0:
                        act.wait_ge(zeroed, 10)
                    for j in range(2):
                        r = slice(64 * j, 64 * j + 64)
                        copy(kz[r, i % 2, j, :], PS[r, bank, 0:B * KEYS], float(HDC) ** -0.5).then_inc(preC_act, 1)
                elif kind == "v":
                    copy(vT[:, i % 4, :], PS[:, bank, 0:B * KPAD]).then_inc(preC_act, 1)
                elif kind == "kk":
                    copy(kkC[:, :, i * KEYS:(i + 1) * KEYS],
                         PS[:, bank, 0:B * KEYS].rearrange("p (b k) -> p b k", b=B)).then_inc(preC_act, 1)
                elif kind == "vw":
                    g, b = i
                    copy(vwCm[:, b, 512 * g:512 * g + 512], PS[:, bank, :]).then_inc(preC_act, 1)
                else:
                    g, b = i
                    copy(vwCr[:, b, g, :], PS[:, bank, 0:D]).then_inc(preC_act, 1)
            act.wait_ge(ld_vec, 64)
            ln_out("b", HT[:, :, 2:T + 2], vec[:, V_LN1W:V_LN1W + 1], vec[:, V_LN1B:V_LN1B + 1])
            for b in range(B):
                act.wait_ge(qk_ready, b + 1)
                if b:
                    act.wait_ge(scr_written[b - 1], 16)
                copy(P3[:, :, 0, :], qk).then_inc(part_hi, 1)
            act.wait_ge(scr_written[B - 1], 16)
            for n in range(B * 4 * QT * 2):
                s, pair = divmod(n, 2)
                w = T - P * (s % QT)
                act.wait_ge(st_mm, n + 1)
                if s >= 2:
                    act.wait_ge(av_step, s - 1)
                slot = 4 * (s % 2) + 2 * pair
                act.activation(PTb[:, slot:slot + 2, 0:w], PS[:, 2 * pair:2 * pair + 2, 0:w], ACT.Exp,
                               scale=float(HDB) ** -0.5).then_inc(st_exp, 1)
                if n % 32 == 31:
                    for qt in range(QT):
                        k = QT * (n // 32) + qt
                        act.wait_ge(yT_mm, k + 1)
                        copy(yT[:, k % 2], PS[:, LN_BANK, 0:P]).then_inc(yT_ready, 1)
            ln_out("m", XT, vec[:, V_LN2W:V_LN2W + 1], vec[:, V_LN2B:V_LN2B + 1])
            for k in range(E * B * FC):
                act.wait_ge(gv_mm, k + 1)
                act.activation(sg[:, k % 2, :], PS[:, 2 * (k % 2), :], ACT.Silu).then_inc(gate_ready, 1)
            ln_out("c", XT)
            units("C")
            ln_out("d", XT)
            for b in range(B):
                act.wait_ge(s_in_mm, b + 1)
                act.activation(sT[:, b, :], PS[:, b, :], ACT.Identity, bias=vec[:, V_BIN:V_BIN + 1]).then_inc(s_in_ready, 1)
                act.wait_ge(s_in_ready, b + 1)
                for j in range(GH):
                    act.activation(RJ[:, b, j, :], sT[:, b, :], ACT.Relu, scale=vec[:, V_W1 + j:V_W1 + j + 1],
                                   bias=vec[:, V_B1 + j:V_B1 + j + 1]).then_inc(relu_ready, 1)

        @block.tensor
        def _(pe):
            def mm(o, lhsT, rhs, start=True, stop=True):
                return pe.matmul(o, lhsT, rhs, start=start, stop=stop)

            def turn(name, src):
                for b in range(B):
                    pe.wait_ge(ln_norm[name], QT * b + QT)
                    if b:
                        pe.wait_ge(ln_T[name], b)
                    for t in range(QT):
                        i = pe.transpose(PS[:, LN_BANK, t * P:t * P + P], src[:, QT * b + t, :], ident)
                    i.then_inc(ln_turned[name], 1)

            def units(st, kk, vwm, vwr):
                n_u, per = UNITS[st], PER[st]
                for u in range(n_u + 2):
                    if u < n_u:
                        n, hg = divmod(u, per)
                        b, t = divmod(n, QT)
                        if t == 0 and hg == 0:
                            pe.wait_ge(ln_T["a" if st == "A" else "c"], b + 1)
                        if u >= 2:
                            pe.wait_ge(unit_PT[st], u - 1)
                        for k, (h0, h1) in enumerate(BANK_HEADS):
                            w = (h1 - h0) * KEYS
                            at = hg * UW + h0 * KEYS
                            o = PS[:, 3 * (u % 2) + k, 0:w]
                            i = mm(o, XT[:, b, t * P:t * P + P], kk[:, b, at:at + w], stop=st == "C")
                            if st == "A":
                                i = mm(o, onesb[:], browb[:, b, at:at + w], start=False)
                            i.then_inc(scores_mm[st], 1)
                    if 1 <= u <= n_u:
                        v = u - 1
                        pe.wait_ge(unit_norm[st], 2 * v + 2)
                        for k in range(BLK):
                            i = pe.transpose(PS[:, 3 * (v % 2) + k // 4, (k % 4) * P:(k % 4) * P + P],
                                             PN[v % 2][:, k * P:k * P + P], ident)
                        i.then_inc(unit_turned[st], 1)
                    if u >= 2:
                        v = u - 2
                        n, hg = divmod(v, per)
                        b = n // QT
                        pe.wait_ge(unit_PT[st], v + 1)
                        if hg == 0 and n >= 1:
                            pe.wait_ge(tile_added[st], n)
                        for k in range(BLK):
                            if k < GH:
                                h = GH * hg + k
                                w = vwm[:, b, h * D:h * D + D]
                            else:
                                w = vwr[:, b, 2 * hg + k - GH, :]
                            i = mm(PS[:, 6, 0:D], PT[v % 2][:, k, :], w,
                                   start=hg == 0 and k == 0, stop=hg == per - 1 and k == BLK - 1)
                        if hg == per - 1:
                            i.then_inc(tile_mm[st], 1)

            pe.wait_ge(ld_a, 80)
            pe.wait_ge(zeroed, 10)
            mm(PS[0:32, 0, 0:B * KEYS], wkTA, ctxT[:, :, 0:KEYS]).then_inc(preA_mm, 1)
            pe.wait_ge(kzA_ready, 2)
            m = 0
            for b in range(B):
                for h0, h1 in BANK_HEADS:
                    if m >= 2:
                        pe.wait_ge(preA_act, m - 1)
                    mm(PS[:, 1 + m % 2, 0:(h1 - h0) * KEYS], wqA, KzA[:, b, h0:h1, :]).then_inc(preA_mm, 1)
                    m += 1
            pe.wait_ge(ld_vec, 64)
            for b in range(B):
                for k, (h0, h1) in enumerate(BANK_HEADS):
                    n = 3 * b + k
                    if n >= 3:
                        pe.wait_ge(preA_dve, 1 + n - 2)
                    mm(PS[0:1, 3 + n % 3, 0:(h1 - h0) * KEYS], vec[0:32, V_BQ:V_BQ + 1],
                       KzA[:, b, h0:h1, :]).then_inc(preA_mm, 1)
            for b in range(B):
                for half in range(2):
                    pe.wait_ge(preA_act, m - 1)
                    mm(PS[:, 1 + m % 2, :], ctxT[:, b, 0:KM], woT[:, 512 * half:512 * half + 512]).then_inc(preA_mm, 1)
                    m += 1
            for b in range(B):
                pe.wait_ge(preA_act, m - 1)
                for g in range(2):
                    for j in range(4):
                        h = 4 * g + j
                        i = mm(PS[32 * j:32 * j + 32, 1 + m % 2, g * D:g * D + D], ctxT[:, b, KM:KPAD],
                               woT[:, h * D:h * D + D])
                i.then_inc(preA_mm, 1)
                m += 1
            turn("a", XN)
            pe.wait_ge(preA_act, m)
            pe.wait_ge(preA_dve, 1 + NA_KK)
            pe.wait_ge(brow_ready, 3)
            units("A", kkA, vwAm, vwAr)
            pe.wait_ge(ld_c, 80)
            done = [0]
            for kind, i, k in PREC:
                done.append(done[-1] + k)
            for n, (kind, i, _) in enumerate(PREC):
                bank = n % 4
                if n >= 4:
                    pe.wait_ge(preC_act, done[n - 3])
                if kind == "kk":
                    pe.wait_ge(preC_act, done[1 + PREC.index(("k", i // 2, 2))])
                elif kind in ("vw", "vr"):
                    pe.wait_ge(preC_act, done[1 + PREC.index(("v", 2 * i[0] + 1, 1))])
                if kind == "k":
                    q = mm(PS[:, bank, 0:B * KEYS], wkC[:, i * P:i * P + P], ctxT[:, :, 0:KEYS])
                elif kind == "v":
                    q = mm(PS[:, bank, 0:B * KPAD], wvC[:, i * P:i * P + P], ctxT[:])
                elif kind == "kk":
                    q = mm(PS[:, bank, 0:B * KEYS], wqT[:, i // 2, :], kz[:, (i // 2) % 2, i % 2, :])
                elif kind == "vw":
                    g, b = i
                    for c in range(2):
                        q = mm(PS[:, bank, 256 * c:256 * c + 256], vT[:, (2 * g + c) % 4, b * KPAD:b * KPAD + KM],
                               woutZ[:, 2 * g + c])
                else:
                    g, b = i
                    for j in range(4):
                        c = 2 * g + j // 2
                        q = mm(PS[32 * j:32 * j + 32, bank, 0:D], vT[:, c % 4, b * KPAD + KM:b * KPAD + KPAD],
                               woutZ[:, c, j % 2, :])
                q.then_inc(preC_mm, 1)
            turn("b", XN)
            pe.wait_ge(ld_b, 64)
            pe.wait_ge(preC_act, N_PREC)
            for b in range(B):
                pe.wait_ge(conv_ready, b + 1)
                if b:
                    pe.wait_ge(qk_ready, b)
                for s in range(4):
                    mm(PS[:, s, :], aqkv[:, s, :], HC2[:, b, :]).then_inc(qkv_mm, 1)
                if b:
                    pe.wait_ge(v_ready, b)
                for t in range(QT):
                    i = mm(PS[:, 4, t * P:t * P + P], HC2[:, b, t * P:t * P + P], aqkv[:, 4, :])
                i.then_inc(qkv_mm, 1)
            pe.wait_ge(qk_ready, B)
            pe.wait_ge(v_ready, B)
            pe.wait_ge(consts_ready, 1)
            for b in range(B):
                pe.wait_ge(stack_ready[b], 16 * 12)
                for n in range(32):
                    hp, qt = divmod(n, QT)
                    w = (qt + 1) * P
                    m = 32 * b + n
                    if m >= 2:
                        pe.wait_ge(s_max, m - 1)
                    for j in range(2):
                        h = 2 * hp + j
                        o = PS[:, 2 * (m % 2) + j, 0:w]
                        mm(o, qs[b][:, h, qt * P:w], ks[b][:, h, 0:w], stop=False)
                        i = mm(o[:, w - P:w], identb, mask_qk, start=False)
                    i.then_inc(s_mm, 1)
                pe.wait_ge(s_max, 32 * b + 32)
                if b:
                    pe.wait_ge(m_split, b)
                pe.transpose(PS[0:HB * QT, 4, 0:P], mB[:, b].rearrange("p h t -> p (h t)"), ident).then_inc(m_turned, 1)
            pe.wait_ge(m_split, B)

            def outputs(s):
                bg, kt = divmod(s, QT)
                b, g = divmod(bg, 4)
                pe.wait_ge(st_exp, 2 * s + 2)
                if kt == 0 and bg >= 2:
                    pe.wait_ge(yg_ready, bg - 1)
                for j in range(4):
                    i = mm(PS[32 * j:32 * j + 32, 4 + g % 2, kt * P:T], vaug[:, b, kt, 4 * g + j, :],
                           PTb[:, 4 * (s % 2) + j, 0:T - kt * P], start=kt == 0, stop=kt == QT - 1)
                i.then_inc(av_step, 1)

            for b in range(B):
                pe.wait_ge(m_ready[b], 16)
                for s in range(16 * b, 16 * b + 16):
                    g, kt = divmod(s % 16, QT)
                    w = T - kt * P
                    for pair in range(2):
                        if s >= 1:
                            pe.wait_ge(st_exp, 2 * (s - 1) + pair + 1)
                        for j in range(2):
                            h = 4 * g + 2 * pair + j
                            o = PS[:, 2 * pair + j, 0:w]
                            mm(o, ks[b][:, h, kt * P:kt * P + P], qs[b][:, h, kt * P:T], stop=False)
                            i = mm(o[:, 0:P], identb, mask_kq, start=False)
                        i.then_inc(st_mm, 1)
                    if s > 16 * b:
                        outputs(s - 1)
                outputs(16 * b + 15)
                pe.wait_ge(yg_ready, 4 * b + 4)
                for qt in range(QT):
                    n = QT * b + qt
                    if n >= 1:
                        pe.wait_ge(y_norm, n)
                    for g in range(4):
                        i = pe.transpose(PS[:, 6, g * P:g * P + P], yg[:, g, qt * P:qt * P + P], ident)
                    i.then_inc(y_turned, 1)
                    pe.wait_ge(y_norm, n + 1)
                    if n >= 1:
                        pe.wait_ge(attn_added, n)
                    pe.transpose(PS[:, LN_BANK, 0:P], yn[:, n % 2], ident).then_inc(yT_mm, 1)
                    pe.wait_ge(yT_ready, n + 1)
                    mm(PS[:, LN_BANK, P:2 * P], yT[:, n % 2], projw[:]).then_inc(proj_mm, 1)
            turn("m", XN)
            pe.wait_ge(ln_T["m"], B)
            for n in range(NT):
                b, t = divmod(n, QT)
                i = mm(PS[:, 6, n * E:n * E + E], XT[:, b, t * P:t * P + P], rw[:])
            i.then_inc(logit_mm, 1)
            pe.wait_ge(ld_moe, 32)

            def project(n):
                pe.wait_ge(g_ready, FC * n + FC)
                if n >= 2:
                    pe.wait_ge(moe_added, QT * (n - 1))
                for t in range(QT):
                    for f in range(FC):
                        i = mm(PS[:, 4 + n % 2, t * P:t * P + P], G[:, n % 2, f, t * P:t * P + P],
                               pj[:, n // B, f, :], start=f == 0, stop=f == FC - 1)
                i.then_inc(moe_mm, 1)

            for n in range(E * B):
                e, b = divmod(n, B)
                for f in range(FC):
                    k = FC * n + f
                    if k >= 2:
                        pe.wait_ge(g_ready, k - 1)
                    mm(PS[:, 2 * (k % 2), :], wv[:, e, f * P:f * P + P], XT[:, b, :])
                    mm(PS[:, 2 * (k % 2) + 1, :], wv[:, e, FF + f * P:FF + f * P + P], XT[:, b, :]).then_inc(gv_mm, 1)
                if n >= 1:
                    project(n - 1)
            project(E * B - 1)
            turn("c", XN)
            units("C", kkC, vwCm, vwCr)
            pe.wait_ge(tile_added["C"], NT)
            pe.wait_ge(ww_ready, GH + 1)
            mm(PS[:, 6, 0:D], b2r[:], wout2[0:M1, :]).then_inc(cb_mm, 1)
            turn("d", XN)
            for b in range(B):
                pe.wait_ge(ln_T["d"], b + 1)
                mm(PS[:, b, :], win2[:], XT[:, b, :]).then_inc(s_in_mm, 1)
            for n in range(NT):
                b, t = divmod(n, QT)
                pe.wait_ge(relu_ready, GH * (b + 1))
                if n >= 2:
                    pe.wait_ge(ffn_added, n - 1)
                for j in range(GH):
                    i = mm(PS[:, 4 + n % 2, 0:D], RJ[:, b, j, t * P:t * P + P], WW[:, j, :],
                           start=j == 0, stop=j == GH - 1)
                i.then_inc(ffn_mm, 1)


def _rope():
    f32 = np.float32
    inv = (f32(1.0) / f32(10000.0) ** (np.arange(0, HDB, 2, dtype=f32) / f32(HDB))).astype(f32)
    fr = np.arange(T, dtype=f32)[:, None] * inv[None, :]
    emb = np.concatenate([fr, fr], axis=1)
    sign = np.where(np.arange(HDB) < HDB // 2, -1.0, 1.0).astype(f32)
    cos, sin = np.cos(emb), np.sin(emb) * sign
    return np.ascontiguousarray(np.stack([np.repeat(cos.T, HB, 0), np.repeat(sin.T, HB, 0)], 1), f32)


def _consts():
    i = np.arange(P)
    later = i[None, :] > i[:, None]
    return np.ascontiguousarray(np.stack([np.eye(P), np.where(later, NEG, 0.0), np.where(later.T, NEG, 0.0)], 1), np.float32)


def _layout(a):
    f32 = np.float32
    vec = np.zeros((P, V_N), f32)
    vec[:, V_LN1W], vec[:, V_LN1B] = a["L0_ffn_ln1_w"], a["L0_ffn_ln1_b"]
    vec[:, V_LN2W], vec[:, V_LN2B] = a["L0_ffn_ln2_w"], a["L0_ffn_ln2_b"]
    vec[:, V_CONV:V_CONV + 3] = a["L0_ffn_conv_w"][:, 0, :]
    for half in range(2):
        r, j = slice(M1 * half, M1 * half + M1), slice(GH * half, GH * half + GH)
        vec[r, V_W1:V_W1 + GH] = a["L1_ffn_W1"][:, j]
        vec[r, V_B1:V_B1 + GH] = a["L1_ffn_b1"][:, j]
        vec[r, V_W2:V_W2 + GH] = a["L1_ffn_W2"][:, j]
        vec[r, V_BIN] = a["L1_ffn_bin_"]
        vec[r, V_B2] = a["L1_ffn_b2"]
    vec[0:32, V_BQ], vec[0:32, V_BK] = a["L0_xattn_bq"], a["L0_xattn_bk"]
    vec[0:32, V_HM:V_HM + HA] = np.repeat(np.eye(HA, dtype=f32), HDA, 0)
    rows = np.zeros((R_N, D), f32)
    rows[R_BO], rows[R_BOUT1], rows[R_BOUT2] = a["L0_xattn_bo"], a["L1_xattn_bout"], a["L1_ffn_bout"]
    rows[R_RANK, 0:NT * E] = np.tile(np.arange(E, 0, -1), NT)
    w = a["L0_ffn_attn_w"]
    by_dim = np.arange(HB * HDB).reshape(HB, HDB).T
    turned = np.roll(by_dim, -(HDB // 2), axis=0)
    q, k, v = w[:, 0:D], w[:, D:2 * D], w[:, 2 * D:3 * D]
    qkv = np.concatenate([q[:, by_dim.ravel()], q[:, turned.ravel()], k[:, by_dim.ravel()], k[:, turned.ravel()], v], 1)
    wkv = a["L1_xattn_Wkv"]
    return {
        "x": a["x"], "ctxT": a["ctx_1024"].transpose(2, 0, 1), "mask_keys": a["mask_BxS2_bk0"].reshape(-1).view(np.int32)[None, :],
        "mask_x": a["mask_BxS_ik0"].reshape(NT, P).T, "vec": vec, "rows": rows, "consts": _consts(), "cossin": _rope(),
        "A_WkT": a["L0_xattn_Wk"].T, "A_Wq": a["L0_xattn_Wq"],
        "A_WoT": a["L0_xattn_Wo"].reshape(D, HA, D).transpose(2, 1, 0).reshape(D, HA * D),
        "B_qkv": qkv, "B_proj": a["L0_ffn_proj_w"], "router": a["L0_ffn_router_w"],
        "wv": a["L0_ffn_expert_wv"], "pj": a["L0_ffn_expert_proj"],
        "C_WqT": a["L1_xattn_Wq"].T, "C_Wk": wkv[:, 0:HC * HDC], "C_Wv": wkv[:, HC * HDC:], "C_Wout": a["L1_xattn_Wout"],
        "D_Win": a["L1_ffn_Win"], "D_Wout": a["L1_ffn_Wout"],
    }


def kernel(**inputs):
    import concourse.bacc as bacc
    from concourse.bass_utils import run_bass_kernel_spmd

    arrays = {f"in_{k}": np.ascontiguousarray(v) for k, v in _layout({k: np.asarray(v) for k, v in inputs.items()}).items()}
    nc = bacc.Bacc("TRN2", target_bir_lowering=False, num_devices=1)
    t_in = {k[3:]: nc.dram_tensor(k, a.shape, mybir.dt.from_np(a.dtype), kind="ExternalInput").ap()
            for k, a in arrays.items()}
    out = nc.dram_tensor("out", (B, T, D), F32, kind="ExternalOutput").ap()
    program(nc, t_in, out)
    r = run_bass_kernel_spmd(nc, [arrays], core_ids=[0])
    return r.results[0]["out"]
```

```python
from contextlib import ExitStack

import numpy as np

import concourse.bass as bass
from concourse import mybir

F32 = mybir.dt.float32
BF16 = mybir.dt.bfloat16
I32 = mybir.dt.int32
U8 = mybir.dt.uint8
ALU = mybir.AluOpType
ACT = mybir.ActivationFunctionType
AX = mybir.AxisListType

P = 128
B, T, D = 2, 512, 128
QT = T // P
NT = B * QT
KEYS = 154
KM, KR = 128, 26
KPAD = 160
HA, HDA = 8, 4
HB, HDB = 16, 8
HC, HDC = 16, 64
GH = 8
BANK_HEADS = ((0, 3), (3, 6), (6, 8))
UW = GH * KEYS
BLK = GH + GH // 4
E, FF = 4, 512
FC = FF // P
NEG = -1.0e30
EPS = 1.0e-5
MASK_NEG = 1.0e6
INNER = 16
M1 = 64
ROWS = 96
SPLIT = 9 * HDB

(V_LN1W, V_LN1B, V_LN2W, V_LN2B, V_CONV, V_W1, V_B1, V_W2, V_BIN, V_B2, V_BQ, V_BK, V_HM) = (
    0, 1, 2, 3, 4, 7, 15, 23, 31, 32, 33, 34, 35)
V_N = 43
R_BO, R_BOUT1, R_BOUT2, R_RANK, R_N = 0, 1, 2, 3, 4


class Own:

    def __init__(self, eng, sem):
        self.eng, self.sem, self.n = eng, sem, 0

    def __call__(self, ins):
        ins.then_inc(self.sem, 1)
        self.n += 1

    def wait(self):
        self.eng.wait_ge(self.sem, self.n)


class Carve:

    def __init__(self, tensor):
        self.t, self.at = tensor, 0

    def f32(self, cols, rows=P):
        a = self.t[0:rows, self.at:self.at + cols]
        self.at += cols
        return a

    def bf16(self, cols, rows=P):
        return self.f32(cols // 2, rows).bitcast(BF16)


def program(nc, t_in, out):
    ctx = ExitStack()
    with ctx:
        def sb(name, shape, dt=F32):
            return ctx.enter_context(nc.sbuf_tensor(name, shape, dt))

        def sem(name):
            return ctx.enter_context(nc.semaphore(name))

        X = sb("X", [P, NT, D])
        U = sb("U", [P, NT, D])
        XN = sb("XN", [P, NT, D])
        XT = sb("XT", [P, B, T])
        HT = sb("HT", [P, B, T + 2])
        HC2 = sb("HC2", [P, B, T])
        vec = sb("vec", [P, V_N])
        rowv = sb("rowv", [P, R_N, D])
        cst = sb("cst", [P, 3, P])
        cstb = sb("cstb", [P, 3, P], BF16)
        cossin = sb("cossin", [P, 2, T])
        ctxT = sb("ctxT", [P, B, KPAD])
        ones = sb("ones", [P, P])
        onesb = sb("onesb", [P, P], BF16)
        maskx = sb("maskx", [P, NT], I32)
        rowbias = sb("rowbias", [P, NT])
        stats = sb("stats", [P, NT, 6])
        mv = sb("mv", [P, NT, 2])
        ve = sb("ve", [P, NT])
        rstd = sb("rstd", [P, NT])
        minus_half = sb("minus_half", [P, NT])
        mraw = sb("mraw", [P, 2, GH])
        umax = sb("umax", [P, 2, GH])
        usum = sb("usum", [P, 3, GH])
        urec = sb("urec", [P, 3, GH])
        mB = sb("mB", [P, B, HB, QT])
        nmf = sb("nmf", [HB * QT, 3, P])
        nm3 = sb("nm3", [HB * QT, B, 3, P], BF16)
        rB = sb("rB", [P, 2, HB])
        lg = sb("lg", [P, 4, NT, E])
        mx = sb("mx", [P, 2, NT])
        onehot = sb("onehot", [P, NT, E])
        rw = sb("rw", [P, E])
        b2r = sb("b2r", [M1, P])
        wout2 = sb("wout2", [P, D])
        WW = sb("WW", [P, GH, D])
        win2 = sb("win2", [P, P])
        cbias = sb("cbias", [P, D])
        aqkv = sb("aqkv", [P, 5, P])
        projw = sb("projw", [P, D])
        kkC = sb("kkC", [P, B, HC * KEYS])
        vwCm = sb("vwCm", [P, B, HC * D])
        vwCr = sb("vwCr", [P, B, HC // 4, D])

        cw = sb("cw", [P, 7632])
        c = Carve(cw)
        wkC = c.f32(HC * HDC)
        wvC = c.f32(HC * HDC)
        wqT = c.f32(HC * HDC).rearrange("p (c d) -> p c d", c=8)
        woutZ = c.f32(HC * D).rearrange("p (c j o) -> p c j o", c=8, j=2)
        kz = c.f32(2 * 2 * B * KEYS).rearrange("p (r j n) -> p r j n", r=2, j=2)
        vT = c.f32(4 * B * KPAD).rearrange("p (r n) -> p r n", r=4)
        assert c.at <= 7632
        c = Carve(cw)
        vaug = c.f32(B * QT * HB * 32).rearrange("p (b t h m) -> p b t h m", b=B, t=QT, h=HB)
        yg = c.f32(4 * T).rearrange("p (g q) -> p g q", g=4)
        yn = c.f32(QT * D).rearrange("p (t d) -> p t d", t=QT)
        yT = c.f32(T).rearrange("p (t q) -> p t q", t=QT)

        BIGW = 22000
        big = sb("big", [P, BIGW])
        c = Carve(big)
        Pt = [c.f32(UW).rearrange("p (h k) -> p h k", h=GH) for _ in range(3)]
        PN = [c.f32(BLK * P) for _ in range(2)]
        PT = [c.f32(BLK * P).rearrange("p (n q) -> p n q", n=BLK) for _ in range(2)]
        kkA = c.f32(B * UW).rearrange("p (b n) -> p b n", b=B)
        vwAm = c.f32(B * HA * D).rearrange("p (b n) -> p b n", b=B)
        vwAr = c.f32(B * 2 * D).rearrange("p (b g o) -> p b g o", b=B, g=2)
        woT = c.f32(HA * D)
        KzA = c.f32(B * UW, ROWS).rearrange("p (b h k) -> p b h k", b=B, h=HA)
        KTA = c.f32(B * KEYS, HA * HDA).rearrange("p (b k) -> p b k", b=B)
        wqA = c.f32(D, ROWS)
        wkTA = c.f32(HA * HDA)
        bqA = c.f32(HA, HA * HDA)
        browb = c.bf16(B * UW).rearrange("p (b n) -> p b n", b=B)
        bias8 = c.f32(B * KEYS, HA)
        rest8 = c.f32(B * KEYS, HA)
        part8 = c.bf16(3 * B * KEYS, HA).rearrange("p (a b k) -> p a b k", a=3, b=B)
        mrow = c.f32(B * KEYS, HA)
        mask_words = c.f32(B * KEYS // 4, HA).bitcast(I32)
        masku = mask_words.bitcast(U8)
        assert c.at <= BIGW, c.at
        c = Carve(big)
        ks, qs = [], []
        for b in range(B):
            ks.append(c.bf16(HB * T, ROWS).rearrange("p (h t) -> p h t", h=HB))
            qs.append(c.bf16(HB * T, ROWS).rearrange("p (h t) -> p h t", h=HB))
        at = c.at
        qk = c.f32(2 * T).rearrange("p (s t) -> p s t", s=2)
        tsin = c.f32(2 * T).rearrange("p (s t) -> p s t", s=2)
        P3 = c.bf16(2 * 3 * T).rearrange("p (s a t) -> p s a t", s=2, a=3)
        assert c.at <= BIGW, c.at
        c.at = at
        PTb = c.f32(8 * T).rearrange("p (n q) -> p n q", n=8)
        assert c.at <= BIGW, c.at
        c = Carve(big)
        wv = c.f32(E * 2 * FF).rearrange("p (e n) -> p e n", e=E)
        c.at = HB * T - E * FC * D
        pj = c.f32(E * FC * D).rearrange("p (e f d) -> p e f d", e=E, f=FC)
        c.at = HB * T
        sg = c.f32(2 * T).rearrange("p (r t) -> p r t", r=2)
        G = c.f32(2 * FC * T).rearrange("p (r f t) -> p r f t", r=2, f=FC)
        c = Carve(big)
        c.at = 3 * UW + 4 * BLK * P
        sT = c.f32(B * T).rearrange("p (b t) -> p b t", b=B)
        RJ = c.f32(B * GH * T).rearrange("p (b j t) -> p b j t", b=B, j=GH)

        PS = ctx.enter_context(nc.psum_tensor("PS", [P, 8, 512], F32))
        scr_qk = nc.dram_tensor("scr_qk", (B, 2, 3, P, T), BF16, kind="Internal").ap()
        scr_m = nc.dram_tensor("scr_m", (B, 3, HB * QT * P), BF16, kind="Internal").ap()

        F_UNIT = (3, 6, 9)
        F_QKV = (14, 28)
        F_LN = 20

        def prec_jobs():
            for c in range(HC // 2 + 1):
                if c < HC // 2:
                    yield "k", c, 2
                    yield "v", c, 1
                if c >= 1:
                    yield "kk", 2 * c - 2, 1
                    yield "kk", 2 * c - 1, 1
                if c >= 2 and c % 2 == 0:
                    for b in range(B):
                        yield "vw", (c // 2 - 1, b), 1
                        yield "vr", (c // 2 - 1, b), 1

        PREC = list(prec_jobs())
        for b in range(B):
            PREC.insert(F_QKV[b], ("xv", b, 1))
        N_PREC = sum(j[2] for j in PREC)

        ld_x = [sem(f"ld_x{b}") for b in range(B)]
        ld_a, ld_wo, ld_mask, ld_vec, ld_cst, ld_rows, ld_c, ld_b, ld_moe, ld_d = (sem(n) for n in (
            "ld_a", "ld_wo", "ld_mask", "ld_vec", "ld_cst", "ld_rows", "ld_c", "ld_b", "ld_moe", "ld_d"))
        zeroed = sem("zeroed")
        zeroedB = sem("zeroedB")
        zeroedC = sem("zeroedC")
        LNS = ("a", "u", "b", "m", "c", "d")
        ln_var = {n: sem(f"ln_var_{n}") for n in LNS}
        ln_rstd = {n: sem(f"ln_rstd_{n}") for n in LNS}
        ln_norm = {n: sem(f"ln_norm_{n}") for n in LNS}
        ln_turned = {n: sem(f"ln_turned_{n}") for n in LNS if n != "u"}
        ln_T = {n: sem(f"ln_T_{n}") for n in LNS if n != "u"}
        preA_mm, preA_act, ktA_ready = sem("preA_mm"), sem("preA_act"), sem("ktA_ready")
        bqA_ready, bias8_mm = sem("bqA_ready"), sem("bias8_mm")
        kzA_ready, part8_ready, brow_ready, consts_ready = sem("kzA_ready"), sem("part8_ready"), sem("brow_ready"), sem("consts_ready")
        preC_mm, preC_act = sem("preC_mm"), sem("preC_act")
        scores_mm = {s: sem(f"scores_mm_{s}") for s in "AC"}
        unit_max = {s: sem(f"unit_max_{s}") for s in "AC"}
        unit_shift = {s: sem(f"unit_shift_{s}") for s in "AC"}
        unit_exp = {s: sem(f"unit_exp_{s}") for s in "AC"}
        unit_rec = {s: sem(f"unit_rec_{s}") for s in "AC"}
        unit_norm = {s: sem(f"unit_norm_{s}") for s in "AC"}
        unit_turned = {s: sem(f"unit_turned_{s}") for s in "AC"}
        unit_PT = {s: sem(f"unit_PT_{s}") for s in "AC"}
        tile_mm = {s: sem(f"tile_mm_{s}") for s in "AC"}
        tile_added = {s: sem(f"tile_added_{s}") for s in "AC"}
        conv_ready = sem("conv_ready")
        qkv_mm, rope_read, v_ready = sem("qkv_mm"), sem("rope_read"), sem("v_ready")
        qk_ready, part_hi, part_r1, part_mid, part_lo = (sem(n) for n in (
            "qk_ready", "part_hi", "part_r1", "part_mid", "part_lo"))
        scr_written = [sem(f"scr_written{b}") for b in range(B)]
        stack_ready = [sem(f"stack_ready{b}") for b in range(B)]
        s_mm, s_max = sem("s_mm"), sem("s_max")
        s1_mm, s1_max = sem("s1_mm"), sem("s1_max")
        m_turned, m_split = sem("m_turned"), sem("m_split")
        m_written = [sem(f"m_written{b}") for b in range(B)]
        m_ready = [sem(f"m_ready{b}") for b in range(B)]
        st_mm, st_exp, av_step, yg_ready = sem("st_mm"), sem("st_exp"), sem("av_step"), sem("yg_ready")
        y_turned, y_norm, yT_mm, yT_ready, proj_mm, attn_added = (sem(n) for n in (
            "y_turned", "y_norm", "yT_mm", "yT_ready", "proj_mm", "attn_added"))
        logit_mm, routed = sem("logit_mm"), sem("routed")
        gv_mm, gate_ready, g_ready, moe_mm, moe_added = (sem(n) for n in (
            "gv_mm", "gate_ready", "g_ready", "moe_mm", "moe_added"))
        cb_mm, cb_ready, ww_ready = sem("cb_mm"), sem("cb_ready"), sem("ww_ready")
        s_in_mm, s_in_ready, relu_ready, ffn_mm, ffn_added = (sem(n) for n in (
            "s_in_mm", "s_in_ready", "relu_ready", "ffn_mm", "ffn_added"))
        stored = sem("stored")
        own_dve, own_act, own_pool = sem("own_dve"), sem("own_act"), sem("own_pool")

        UNITS = {"A": NT, "C": 2 * NT}
        PER = {"A": 1, "C": 2}
        LN_BANK = 7
        Z_EARLY, Z_WOUT, Z_ALL = 8, 9, 12
        S_BANK = (0, 3)
        F_BANK = ((0, 1, 2, 7), (4, 5, 6, 3))
        Y_BANK = (4, 5, 6, 4)
        M_TURN = 32 + 2
        M_MERGE = 32 + 8
        S_MAX = (64 - M_MERGE) // 2
        S_TAIL, S_LN = 17, 21
        K_LNM, K_LNC = 5, 5 * FC + 5
        U_LNC, U_LND = 4, 2 * QT + 6
        PREA = ([("kk", 0, k) for k in range(3)] + [("vw", 0, k) for k in range(2)] + [("kk", 1, k) for k in range(3)]
                + [("vr", 0, 0)] + [("vw", 1, k) for k in range(2)] + [("vr", 1, 0)])

        def max_parts(m):
            if m < M_MERGE:
                return [((0, 1), 2 * (m % 3), s_mm, s_max, m + 1)]
            k = 2 * (m - M_MERGE)
            return [((j,), 5 + (k + j) % 3, s1_mm, s1_max, k + j + 1) for j in range(2)]

        def av_bank(b, g):
            return 4 + g % 2 if b else 4

        ident = cst[:, 0, :]
        identb, mask_qk, mask_kq = cstb[:, 0, :], cstb[:, 1, :], cstb[:, 2, :]
        block = ctx.enter_context(nc.Block())

        @block.sync
        def _(sp):
            i = t_in
            sp.dma_start(vec[:], i["vec"]).then_inc(ld_vec, 16)
            sp.dma_start(wkTA, i["A_WkT"]).then_inc(ld_a, 16)
            sp.dma_start(ctxT[:, :, 0:KEYS], i["ctxT"]).then_inc(ld_a, 16)
            sp.wait_ge(zeroed, 1)
            sp.dma_start(wqA[0:HA * HDA], i["A_Wq"]).then_inc(ld_a, 16)
            sp.dma_start(cst[:], i["consts"]).then_inc(ld_cst, 16)
            sp.dma_start(mask_words, i["mask_keys"].to_broadcast([HA, B * KEYS // 4])).then_inc(ld_mask, 16)
            sp.dma_start(rowv[:], i["rows"].unsqueeze(0).to_broadcast([P, R_N, D])).then_inc(ld_rows, 16)
            sp.dma_start(maskx[:], i["mask_x"]).then_inc(ld_rows, 16)
            sp.wait_ge(zeroed, Z_EARLY)
            sp.wait_ge(part8_ready, 1)
            for a in range(3):
                for b in range(B):
                    sp.dma_start(browb[32 * a:32 * a + 1, b].rearrange("p (h k) -> p h k", h=HA),
                                 part8[:, a, b]).then_inc(brow_ready, 16)
            sp.dma_start(wkC, i["C_Wk"]).then_inc(ld_c, 16)
            sp.dma_start(wvC, i["C_Wv"]).then_inc(ld_c, 16)
            sp.dma_start(wqT, i["C_WqT"].rearrange("(c p) d -> p c d", p=P)).then_inc(ld_c, 16)
            sp.wait_ge(zeroed, Z_WOUT)
            for j in range(2):
                sp.dma_start(woutZ[64 * j:64 * j + 64, :, j, :],
                             i["C_Wout"].rearrange("(c j e) o -> j e c o", j=2, e=HDC)[j]).then_inc(ld_c, 16)
            sp.dma_start(aqkv[:], i["B_qkv"].rearrange("p (s n) -> p s n", s=5)).then_inc(ld_b, 16)
            sp.dma_start(cossin[:], i["cossin"]).then_inc(ld_b, 16)
            sp.dma_start(projw[:], i["B_proj"]).then_inc(ld_b, 16)
            sp.dma_start(rw[:], i["router"]).then_inc(ld_b, 16)
            for j in range(2):
                sp.dma_start(win2[:, 64 * j:64 * j + 64], i["D_Win"]).then_inc(ld_d, 16)
                sp.dma_start(wout2[64 * j:64 * j + 64, :], i["D_Wout"]).then_inc(ld_d, 16)
            for b in range(B):
                sp.wait_ge(part_lo, b + 1)
                sp.dma_start(scr_qk[b].rearrange("s a r t -> r s a t"), P3).then_inc(scr_written[b], 16)
                sp.wait_ge(scr_written[b], 16)
                sp.wait_ge(zeroedB, 2 * b + 2)
                for a in range(3):
                    sp.dma_start(ks[b][24 * a:24 * a + 24, :, :],
                                 scr_qk[b, 1].rearrange("a (d h) t -> (a d) h t", h=HB)).then_inc(stack_ready[b], 16)
                    for j in range(3):
                        r = 24 * a + 8 * j
                        sp.dma_start(qs[b][r:r + 8, :, :],
                                     scr_qk[b, 0, a].rearrange("(d h) t -> d h t", h=HB)).then_inc(stack_ready[b], 16)
            for b in range(B):
                sp.wait_ge(m_split, b + 1)
                sp.dma_start(scr_m[b].rearrange("a (n q) -> n a q", q=P), nm3[:, b]).then_inc(m_written[b], 16)
                sp.wait_ge(m_written[b], 16)
                sp.wait_ge(*((s1_mm, 2 * (64 - M_MERGE)) if b else (s_mm, 32)))
                sp.dma_start(qs[b][SPLIT:SPLIT + 3, :, :],
                             scr_m[b].rearrange("a (h t) -> a h t", h=HB)).then_inc(m_ready[b], 16)
            sp.wait_ge(st_mm, 32)
            sp.dma_start(wv, i["wv"].rearrange("e p n -> p e n")).then_inc(ld_moe, 16)
            sp.dma_start(pj, i["pj"].rearrange("e (f p) d -> p e f d", p=P)).then_inc(ld_moe, 16)
            for n in range(NT):
                sp.wait_ge(ffn_added, n + 1)
                sp.dma_start(out.rearrange("b (t p) d -> p (b t) d", p=P)[:, n, :], X[:, n, :]).then_inc(stored, 16)
            sp.wait_ge(stored, 16 * NT)

        @block.gpsimd
        def _(pool):
            own = Own(pool, own_pool)
            pool.memset(wqA, 0.0).then_inc(zeroed, 1)
            pool.memset(KzA, 0.0).then_inc(zeroed, 1)
            pool.memset(ctxT[:, :, KEYS:KPAD], 0.0).then_inc(zeroed, 1)
            pool.memset(minus_half[:], -0.5).then_inc(zeroed, 1)
            pool.memset(onesb[:], 1.0).then_inc(zeroed, 1)
            pool.memset(browb, 0.0).then_inc(zeroed, 1)
            for r in range(2):
                pool.memset(PN[r][:, GH * P:BLK * P], 0.0).then_inc(zeroed, 1)
            pool.wait_ge(zeroed, Z_EARLY)

            def ln_rsqrt(name, seqs=range(B)):
                for b in seqs:
                    pool.wait_ge(ln_var[name], b + 1)
                    s = slice(b * QT, b * QT + QT)
                    pool.tensor_tensor(rstd[:, s], ve[:, s], minus_half[:, s], ALU.pow).then_inc(ln_rstd[name], 1)

            def unit_norms(st, between={}):
                for u in range(UNITS[st]):
                    if u in between:
                        between[u]()
                    pool.wait_ge(unit_rec[st], u + 1)
                    if u >= 2:
                        pool.wait_ge(unit_turned[st], u - 1)
                    r = urec[:, u % 3, :].unsqueeze(2)
                    pn = PN[u % 2]
                    pool.tensor_tensor(pn[:, 0:GH * P].rearrange("p (h k) -> p h k", h=GH),
                                       Pt[u % 3][:, :, 0:KM], r.to_broadcast([P, GH, KM]), ALU.mult).then_inc(unit_norm[st], 1)
                    pool.tensor_tensor(pn[:, GH * P:BLK * P].rearrange("p (h k) -> p h k", h=GH)[:, :, 0:KR],
                                       Pt[u % 3][:, :, KM:KEYS], r.to_broadcast([P, GH, KR]), ALU.mult).then_inc(unit_norm[st], 1)

            ln_rsqrt("a")
            pool.memset(woutZ, 0.0).then_inc(zeroed, 1)
            pool.memset(ones[:], 1.0).then_inc(zeroed, 1)
            pool.memset(HT[:, :, 0:2], 0.0).then_inc(zeroed, 1)
            pool.memset(kz, 0.0).then_inc(zeroed, 1)
            unit_norms("A", {NT - 1: lambda: ln_rsqrt("u", (0,))})
            ln_rsqrt("b", (0,))
            ln_rsqrt("u", (1,))
            ln_rsqrt("b", (1,))
            pool.wait_ge(tile_mm["A"], NT)
            pool.wait_ge(ln_rstd["b"], B)
            two_ones = float(np.array([0x3F803F80], np.uint32).view(np.float32)[0])
            for b in range(B):
                pool.memset(qs[b][64:ROWS].bitcast(F32), 0.0).then_inc(zeroedB, 1)
                pool.memset(ks[b][64:ROWS].bitcast(F32), two_ones).then_inc(zeroedB, 1)
            pool.wait_ge(preC_act, N_PREC)
            pool.wait_ge(zeroedB, 4)
            pool.memset(vaug, 0.0).then_inc(zeroedB, 1)
            pool.wait_ge(zeroedB, 5)
            pool.memset(vaug[:, :, :, :, HDB:HDB + 1], 1.0).then_inc(zeroedB, 1)
            pool.wait_ge(zeroedB, 6)
            for b in range(B):
                pool.tensor_copy(vaug[:, b, :, :, 0:HDB],
                                 XN[:, QT * b:QT * b + QT, :].rearrange("p t (h d) -> p t h d", h=HB)).then_inc(v_ready, 1)
            ln_rsqrt("m")
            ln_rsqrt("c", (0,))
            pool.wait_ge(ln_rstd["c"], 1)
            pool.wait_ge(gv_mm, E * B * FC)
            pool.memset(PN[0][:, GH * P:BLK * P], 0.0).then_inc(zeroedC, 1)

            def second_blocks():
                ln_rsqrt("c", (1,))
                pool.wait_ge(moe_mm, E * B)
                pool.memset(PN[1][:, GH * P:BLK * P], 0.0).then_inc(zeroedC, 1)
                pool.wait_ge(zeroedC, 2)

            pool.wait_ge(zeroedC, 1)
            unit_norms("C", {1: second_blocks, 2 * QT + 3: lambda: ln_rsqrt("d", (0,))})
            ln_rsqrt("d", (1,))

        @block.vector
        def _(dve):
            own = Own(dve, own_dve)
            tile = lambda n: slice(n, n + 1)

            def ln_stats(name, src, b, ready):
                ready()
                for n in range(b * QT, b * QT + QT):
                    own(dve.bn_stats(stats[:, n, :], src[:, n, :]))
                own.wait()
                for n in range(b * QT, b * QT + QT):
                    own(dve.bn_aggr(mv[:, n, :], stats[:, n, :]))
                own.wait()
                s = slice(b * QT, b * QT + QT)
                dve.tensor_scalar(ve[:, s], mv[:, s, 1], EPS, None, ALU.add).then_inc(ln_var[name], 1)

            def ln_apply(name, src, dst, b):
                dve.wait_ge(ln_rstd[name], b + 1)
                for n in range(b * QT, b * QT + QT):
                    dve.tensor_scalar(dst[:, n, :], src[:, n, :], mv[:, n, 0:1], rstd[:, tile(n)],
                                      ALU.subtract, ALU.mult).then_inc(ln_norm[name], 1)

            def units(st, bias, between={}):
                op0 = ALU.max if st == "A" else ALU.add
                n_u = UNITS[st]
                for u in range(n_u + 1):
                    if u >= 4 and (u - 4) % PER[st] == PER[st] - 1:
                        add_tile(st, (u - 4) // PER[st])
                    if u < n_u:
                        for k, (h0, h1) in enumerate(BANK_HEADS):
                            dve.wait_ge(scores_mm[st], 3 * u + k + 1)
                            s = PS[:, k, 0:(h1 - h0) * KEYS].rearrange("p (h k) -> p h k", h=h1 - h0)
                            own(dve.tensor_reduce(mraw[:, u % 2, h0:h1], s, AX.X, ALU.max))
                        own.wait()
                        sc = bias(u)
                        own(dve.tensor_scalar(umax[:, u % 2, :], mraw[:, u % 2, :], sc, None, op0))
                    if u >= 1:
                        v = u - 1
                        dve.wait_ge(unit_exp[st], v + 1)
                        own(dve.tensor_reduce(usum[:, v % 3, :], Pt[v % 3], AX.X, ALU.add))
                        own.wait()
                        dve.reciprocal(urec[:, v % 3, :], usum[:, v % 3, :]).then_inc(unit_rec[st], 1)
                    if u < n_u:
                        own.wait()
                        if u >= 3:
                            dve.wait_ge(unit_norm[st], 2 * (u - 2))
                        for k, (h0, h1) in enumerate(BANK_HEADS):
                            s = PS[:, k, 0:(h1 - h0) * KEYS].rearrange("p (h k) -> p h k", h=h1 - h0)
                            dve.scalar_tensor_tensor(
                                Pt[u % 3][:, h0:h1, :], s, sc,
                                umax[:, u % 2, h0:h1].unsqueeze(2).to_broadcast([P, h1 - h0, KEYS]),
                                op0, ALU.subtract).then_inc(unit_shift[st], 1)
                    if u in between:
                        between[u]()

            def add_tile(st, n):
                dve.wait_ge(tile_mm[st], n + 1)
                dve.tensor_tensor(X[:, n, :], PS[:, 6, 0:D], X[:, n, :], ALU.add).then_inc(tile_added[st], 1)

            for b in range(B):
                ln_stats("a", X, b, lambda: dve.wait_ge(ld_x[b], 16))
            dve.wait_ge(ld_vec, 16)
            dve.tensor_scalar(bqA, vec[0:32, V_HM:V_HM + HA], vec[0:32, V_BQ:V_BQ + 1], None, ALU.mult).then_inc(bqA_ready, 1)
            dve.wait_ge(preA_mm, 1)
            dve.tensor_scalar(KTA, PS[0:32, 0, 0:B * KEYS].rearrange("p (b k) -> p b k", b=B),
                              vec[0:32, V_BK:V_BK + 1], None, ALU.add).then_inc(ktA_ready, 1)
            dve.wait_ge(ktA_ready, 1)
            dve.wait_ge(zeroed, 2)
            def keys_by_head(b):
                dve.tensor_tensor(KzA[0:HA * HDA, b], KTA[:, b:b + 1, :].to_broadcast([32, HA, KEYS]),
                                  vec[0:32, V_HM:V_HM + HA].unsqueeze(2).to_broadcast([32, HA, KEYS]),
                                  ALU.mult).then_inc(kzA_ready, 1)

            keys_by_head(0)
            dve.wait_ge(ld_mask, 16)
            own(dve.tensor_scalar(mrow, masku, NEG, None, ALU.mult))
            own.wait()
            dve.wait_ge(bias8_mm, 1)
            own(dve.scalar_tensor_tensor(bias8, PS[0:HA, 1, 0:B * KEYS], 0.5, mrow, ALU.mult, ALU.add))
            own.wait()
            parts = part8.rearrange("p a b k -> p a (b k)")
            own(dve.tensor_copy(parts[:, 0], bias8))
            own.wait()
            own(dve.tensor_tensor(rest8, bias8, parts[:, 0], ALU.subtract))
            own.wait()
            own(dve.tensor_copy(parts[:, 1], rest8))
            own.wait()
            dve.tensor_tensor(parts[:, 2], rest8, parts[:, 1], ALU.subtract).then_inc(part8_ready, 1)

            def x_plus(b, row):
                s = slice(QT * b, QT * b + QT)
                own(dve.tensor_tensor(X[:, s, :], X[:, s, :], row.unsqueeze(1).to_broadcast([P, QT, D]), ALU.add))
                own.wait()

            def constants():
                dve.wait_ge(ld_rows, 32)
                for b in range(B):
                    x_plus(b, rowv[:, R_BO, :])
                dve.tensor_copy(cstb[:], cst[:]).then_inc(consts_ready, 1)
                own(dve.tensor_copy(rowbias[:], maskx[:]))
                own.wait()
                own(dve.tensor_scalar(rowbias[:], rowbias[:], -1.0, 1.0, ALU.mult, ALU.add))
                own.wait()
                own(dve.tensor_scalar(rowbias[:], rowbias[:], -MASK_NEG, None, ALU.mult))

            ln_apply("a", X, XN, 0)
            keys_by_head(1)
            ln_apply("a", X, XN, 1)
            dve.wait_ge(ln_norm["a"], NT)

            def ln_u_stats(b):
                ln_stats("u", X, b, lambda: dve.wait_ge(tile_added["A"], QT * b + QT))

            def ln_b_stats(b):
                ln_apply("u", X, U, b)
                ln_stats("b", U, b, lambda: dve.wait_ge(ln_norm["u"], QT * b + QT))

            def convolve(b):
                dve.wait_ge(ln_T["b"], b + 1)
                dve.wait_ge(zeroed, Z_ALL)
                h = HT[:, b, :]
                o = HC2[:, b, :]
                own(dve.tensor_scalar(o, h[:, 0:T], vec[:, V_CONV:V_CONV + 1], None, ALU.mult))
                own.wait()
                own(dve.scalar_tensor_tensor(o, h[:, 1:T + 1], vec[:, V_CONV + 1:V_CONV + 2], o, ALU.mult, ALU.add))
                own.wait()
                dve.scalar_tensor_tensor(o, h[:, 2:T + 2], vec[:, V_CONV + 2:V_CONV + 3], o,
                                         ALU.mult, ALU.add).then_inc(conv_ready, 1)

            def rotate_split(b):
                dve.wait_ge(ld_b, 64)
                if b:
                    dve.wait_ge(scr_written[b - 1], 16)
                for s in range(2):
                    dve.wait_ge(qkv_mm, 4 * b + 2 * s + 2)
                    own(dve.tensor_tensor(qk[:, s], PS[:, 3 + 2 * s, :], cossin[:, 0], ALU.mult))
                    own(dve.tensor_tensor(tsin[:, s], PS[:, 4 + 2 * s, :], cossin[:, 1], ALU.mult))
                own.wait()
                dve.tensor_tensor(qk, qk, tsin, ALU.add).then_inc(qk_ready, 1)
                dve.wait_ge(qk_ready, b + 1)
                own(dve.tensor_copy(P3[:, :, 0, :], qk))
                own.wait()
                own(dve.tensor_tensor(qk, qk, P3[:, :, 0, :], ALU.subtract))
                own.wait()
                own(dve.tensor_copy(P3[:, :, 1, :], qk))
                own.wait()
                dve.tensor_tensor(P3[:, :, 2, :], qk, P3[:, :, 1, :], ALU.subtract).then_inc(part_lo, 1)

            units("A", lambda u: -3.0e38, {0: constants, NT - 1: lambda: ln_u_stats(0), NT: lambda: ln_b_stats(0)})
            add_tile("A", NT - 3)
            ln_apply("b", U, XN, 0)
            add_tile("A", NT - 2)
            add_tile("A", NT - 1)
            ln_u_stats(1)
            convolve(0)
            ln_b_stats(1)
            ln_apply("b", U, XN, 1)
            rotate_split(0)
            convolve(1)
            rotate_split(1)
            def split_maxima(b):
                dve.wait_ge(m_turned, b + 1)
                mt = PS[0:HB * QT, 6, 0:P]
                own(dve.tensor_scalar(nmf[:, 0], mt, -1.0, None, ALU.mult))
                own.wait()
                own(dve.tensor_copy(nm3[:, b, 0], nmf[:, 0]))
                own.wait()
                own(dve.tensor_tensor(nmf[:, 1], nmf[:, 0], nm3[:, b, 0], ALU.subtract))
                own.wait()
                own(dve.tensor_copy(nm3[:, b, 1], nmf[:, 1]))
                own.wait()
                dve.tensor_tensor(nm3[:, b, 2], nmf[:, 1], nm3[:, b, 1], ALU.subtract).then_inc(m_split, 1)

            def maximum(m):
                b, n = divmod(m, 32)
                hp, qt = divmod(n, QT)
                for heads, bank, mm_done, max_done, count in max_parts(m):
                    k = len(heads)
                    h = 2 * hp + heads[0]
                    dve.wait_ge(mm_done, count)
                    dve.tensor_reduce(mB[:, b, h:h + k, qt], PS[:, bank:bank + k, 0:(qt + 1) * P],
                                      AX.X, ALU.max).then_inc(max_done, 1)

            def copy_outputs(b, groups):
                for g in groups:
                    dve.wait_ge(av_step, 2 * QT * (4 * b + g + 1))
                    if b:
                        dve.wait_ge(y_turned, QT * b)
                    dve.tensor_copy(yg[:, g, :], PS[:, av_bank(b, g), :]).then_inc(yg_ready, 1)

            def normalise_outputs(b):
                for qt in range(QT):
                    n = QT * b + qt
                    dve.wait_ge(y_turned, n + 1)
                    yv = PS[:, Y_BANK[qt], :].rearrange("p (h m) -> p h m", h=HB)
                    own(dve.reciprocal(rB[:, n % 2, :].unsqueeze(2), yv[:, :, HDB:HDB + 1]))
                    own.wait()
                    if b:
                        dve.wait_ge(yT_mm, b)
                    dve.tensor_tensor(yn[:, qt].rearrange("p (h d) -> p h d", h=HB), yv[:, :, 0:HDB],
                                      rB[:, n % 2, :].unsqueeze(2).to_broadcast([P, HB, HDB]), ALU.mult).then_inc(y_norm, 1)

            def add_attention(b):
                dve.wait_ge(proj_mm, b + 1)
                s = slice(QT * b, QT * b + QT)
                dve.tensor_tensor(U[:, s, :], PS[:, 5, :].rearrange("p (t d) -> p t d", t=QT), U[:, s, :],
                                  ALU.add).then_inc(attn_added, 1)

            def x_plus_u(b):
                s = slice(QT * b, QT * b + QT)
                own(dve.tensor_tensor(X[:, s, :], X[:, s, :], U[:, s, :], ALU.add))
                own.wait()

            def route(b):
                s = slice(QT * b, QT * b + QT)
                dve.wait_ge(logit_mm, b + 1)
                L = PS[:, 6, b * QT * E:(b + 1) * QT * E].rearrange("p (n e) -> p n e", e=E)
                dve.tensor_copy(lg[:, 0, s], L).then_inc(routed, 1)
                dve.wait_ge(routed, b + 1)
                own(dve.tensor_reduce(mx[:, 0, s], lg[:, 0, s], AX.X, ALU.max))
                own.wait()
                own(dve.tensor_tensor(lg[:, 1, s], lg[:, 0, s], mx[:, 0, s].unsqueeze(2).to_broadcast([P, QT, E]), ALU.is_equal))
                own.wait()
                own(dve.tensor_tensor(lg[:, 2, s], lg[:, 1, s],
                                      rowv[:, R_RANK, 0:QT * E].rearrange("p (n e) -> p n e", e=E), ALU.mult))
                own.wait()
                own(dve.tensor_reduce(mx[:, 1, s], lg[:, 2, s], AX.X, ALU.max))
                own.wait()
                own(dve.tensor_tensor(onehot[:, s], lg[:, 2, s], mx[:, 1, s].unsqueeze(2).to_broadcast([P, QT, E]), ALU.is_equal))
                own.wait()

            def fold_last():
                dve.wait_ge(ld_d, 64)
                for j in range(GH):
                    dve.tensor_scalar(WW[:, j, :], wout2[:], vec[:, V_W2 + j:V_W2 + j + 1], None, ALU.mult).then_inc(ww_ready, 1)
                dve.tensor_scalar(b2r[:], ones[0:M1, :], vec[0:M1, V_B2:V_B2 + 1], None, ALU.mult).then_inc(ww_ready, 1)
                dve.wait_ge(cb_mm, 1)
                dve.tensor_tensor(cbias[:], PS[:, LN_BANK, 0:D], rowv[:, R_BOUT2, :], ALU.add).then_inc(cb_ready, 1)

            def ln_m(b):
                ln_stats("m", U, b, lambda: dve.wait_ge(attn_added, b + 1))
                x_plus_u(b)
                dve.wait_ge(v_ready, B)
                ln_apply("m", U, XN, b)

            def expert_gates(k):
                n, f = divmod(k, FC)
                if n >= 2 and f == 0:
                    dve.wait_ge(moe_mm, n - 1)
                dve.wait_ge(gate_ready, k + 1)
                dve.tensor_tensor(G[:, n % 2, f, :], sg[:, k % 2, :], PS[:, 2 * (k % 2) + 1, :], ALU.mult).then_inc(g_ready, 1)

            def add_expert(n):
                b, e = divmod(n, E)
                dve.wait_ge(moe_mm, n + 1)
                if e:
                    dve.wait_ge(moe_added, QT * n)
                for t in range(QT):
                    i = QT * b + t
                    dve.scalar_tensor_tensor(X[:, i, :], PS[:, 4 + n % 2, t * P:t * P + P], onehot[:, i, e:e + 1],
                                             X[:, i, :], ALU.mult, ALU.add).then_inc(moe_added, 1)

            for m in range(M_TURN):
                maximum(m)
            split_maxima(0)
            for m in range(M_TURN, M_MERGE):
                maximum(m)
            for step in range(S_MAX + 1):
                if step < S_MAX:
                    maximum(M_MERGE + 2 * step)
                    maximum(M_MERGE + 2 * step + 1)
                if step >= QT and step % QT == 0:
                    copy_outputs(0, (step // QT - 1,))
            split_maxima(1)
            copy_outputs(0, (3,))
            normalise_outputs(0)
            add_attention(0)
            ln_m(0)
            copy_outputs(1, (0,))
            fold_last()
            route(0)
            copy_outputs(1, (1, 2, 3))
            normalise_outputs(1)
            for k in range(2):
                expert_gates(k)
            add_attention(1)
            for k in range(2, E * B * FC):
                n, f = divmod(k, FC)
                expert_gates(k)
                if f == FC - 1 and 1 <= n < E * B - 1:
                    add_expert(n - 1)
                if k == 2:
                    ln_stats("m", U, 1, lambda: dve.wait_ge(attn_added, 2))
                elif k == 3:
                    x_plus_u(1)
                    ln_apply("m", U, XN, 1)
                elif k == FC + 3:
                    route(1)
                elif k == 5 * FC:
                    ln_stats("c", X, 0, lambda: dve.wait_ge(moe_added, QT * E))
                elif k == 5 * FC + 3:
                    ln_apply("c", X, XN, 0)
                    dve.wait_ge(ln_norm["c"], QT)
                    x_plus(0, rowv[:, R_BOUT1, :])

            def last_expert():
                add_expert(E * B - 1)
                ln_stats("c", X, 1, lambda: dve.wait_ge(moe_added, QT * E * B))

            def ln_c_second():
                ln_apply("c", X, XN, 1)
                dve.wait_ge(ln_norm["c"], NT)
                x_plus(1, rowv[:, R_BOUT1, :])

            def ln_d_first():
                ln_apply("d", X, XN, 0)
                dve.wait_ge(ln_norm["d"], QT)
                dve.wait_ge(cb_ready, 1)
                x_plus(0, cbias[:])

            units("C", lambda u: rowbias[:, tile(u // 2)], {
                0: lambda: add_expert(E * B - 2),
                1: last_expert,
                2: ln_c_second,
                2 * QT + 3: lambda: ln_stats("d", X, 0, lambda: dve.wait_ge(tile_added["C"], QT)),
                2 * QT + 5: ln_d_first})
            add_tile("C", NT - 2)
            add_tile("C", NT - 1)
            def add_last(b):
                for t in range(QT):
                    n = QT * b + t
                    dve.wait_ge(ffn_mm, n + 1)
                    dve.tensor_tensor(X[:, n, :], PS[:, F_BANK[b][t], 0:D], X[:, n, :], ALU.add).then_inc(ffn_added, 1)

            ln_stats("d", X, 1, lambda: dve.wait_ge(tile_added["C"], NT))
            ln_apply("d", X, XN, 1)
            add_last(0)
            dve.wait_ge(ln_norm["d"], NT)
            x_plus(1, cbias[:])
            add_last(1)

        @block.scalar
        def _(act):
            def copy(dst, src, scale=1.0):
                return act.activation(dst, src, ACT.Copy, scale=scale)

            def ln_out(name, dst, w=None, bias=None, seqs=range(B)):
                for b in seqs:
                    act.wait_ge(ln_turned[name], b + 1)
                    if w is None:
                        copy(dst[:, b, :], PS[:, LN_BANK, :]).then_inc(ln_T[name], 1)
                    else:
                        act.activation(dst[:, b, :], PS[:, LN_BANK, :], ACT.Identity,
                                       scale=w, bias=bias).then_inc(ln_T[name], 1)

            def units(st, between={}):
                for u in range(UNITS[st] + 2):
                    if u >= 2:
                        v = u - 2
                        act.wait_ge(unit_turned[st], v + 1)
                        copy(PT[v % 2].rearrange("p n q -> p (n q)"),
                             PS[:, 3:6, :].rearrange("p k n -> p (k n)")[:, 0:BLK * P]).then_inc(unit_PT[st], 1)
                    if u < UNITS[st]:
                        act.wait_ge(unit_shift[st], 3 * u + 3)
                        act.activation(Pt[u % 3], Pt[u % 3], ACT.Exp).then_inc(unit_exp[st], 1)
                    if u in between:
                        between[u]()

            def copy_A(m0, m1):
                for m in range(m0, m1):
                    kind, b, k = PREA[m]
                    bank = 3 + m % 3
                    act.wait_ge(preA_mm, 1 + m + 1)
                    if kind == "kk":
                        h0, h1 = BANK_HEADS[k]
                        copy(kkA[:, b, h0 * KEYS:h1 * KEYS], PS[:, bank, 0:(h1 - h0) * KEYS], 0.5).then_inc(preA_act, 1)
                    elif kind == "vw":
                        copy(vwAm[:, b, 512 * k:512 * k + 512], PS[:, bank, :]).then_inc(preA_act, 1)
                    else:
                        copy(vwAr[:, b].rearrange("p g o -> p (g o)"), PS[:, bank, 0:2 * D]).then_inc(preA_act, 1)

            def copy_C(n0, n1):
                for n in range(n0, n1):
                    kind, i, _ = PREC[n]
                    act.wait_ge(preC_mm, n + 1)
                    bank = n % 3
                    if kind == "k":
                        if n == 0:
                            act.wait_ge(zeroed, Z_ALL)
                        for j in range(2):
                            r = slice(64 * j, 64 * j + 64)
                            copy(kz[r, i % 2, j, :], PS[r, bank, 0:B * KEYS], float(HDC) ** -0.5).then_inc(preC_act, 1)
                    elif kind == "v":
                        copy(vT[:, i % 4, :], PS[:, bank, 0:B * KPAD]).then_inc(preC_act, 1)
                    elif kind == "kk":
                        copy(kkC[:, :, i * KEYS:(i + 1) * KEYS],
                             PS[:, bank, 0:B * KEYS].rearrange("p (b k) -> p b k", b=B)).then_inc(preC_act, 1)
                    elif kind == "vw":
                        g, b = i
                        copy(vwCm[:, b, 512 * g:512 * g + 512], PS[:, bank, :]).then_inc(preC_act, 1)
                    elif kind == "vr":
                        g, b = i
                        copy(vwCr[:, b, g, :], PS[:, bank, 0:D]).then_inc(preC_act, 1)
                    else:
                        copy(XN[:, QT * i:QT * i + QT, :].rearrange("p t d -> p (t d)"), PS[:, bank, :]).then_inc(preC_act, 1)

            x_t = t_in["x"].rearrange("b (t p) d -> p b t d", p=P)
            for b in range(B):
                act.dma_start(X[:, QT * b:QT * b + QT, :], x_t[:, b]).then_inc(ld_x[b], 16)
            act.dma_start(woT, t_in["A_WoT"]).then_inc(ld_wo, 16)
            copy_A(0, 3)
            ln_out("a", XT, seqs=(0,))
            copy_A(3, 7)
            ln_out("a", XT, seqs=(1,))
            units("A", {0: lambda: copy_A(7, 10), 1: lambda: copy_A(10, len(PREA)), NT: lambda: copy_C(0, F_UNIT[0]),
                        NT + 1: lambda: copy_C(F_UNIT[0], F_UNIT[1])})
            copy_C(F_UNIT[1], F_UNIT[2])
            ln1 = (vec[:, V_LN1W:V_LN1W + 1], vec[:, V_LN1B:V_LN1B + 1])
            ln_out("b", HT[:, :, 2:T + 2], *ln1, seqs=(0,))
            copy_C(F_UNIT[2], F_LN)
            ln_out("b", HT[:, :, 2:T + 2], *ln1, seqs=(1,))
            copy_C(F_LN, len(PREC))
            act.wait_ge(scr_written[B - 1], 16)
            def turn_outputs(b):
                act.wait_ge(yT_mm, b + 1)
                copy(yT[:].rearrange("p t q -> p (t q)"), PS[:, LN_BANK, :]).then_inc(yT_ready, 1)

            ln2 = (vec[:, V_LN2W:V_LN2W + 1], vec[:, V_LN2B:V_LN2B + 1])
            for n in range(B * 4 * QT * 2):
                s, pair = divmod(n, 2)
                w = T - P * (s % QT)
                act.wait_ge(st_mm, n + 1)
                if s >= 2:
                    act.wait_ge(av_step, 2 * (s - 2) + pair + 1)
                slot = 4 * (s % 2) + 2 * pair
                act.activation(PTb[:, slot:slot + 2, 0:w], PS[:, 2 * pair:2 * pair + 2, 0:w], ACT.Exp,
                               scale=float(HDB) ** -0.5).then_inc(st_exp, 1)
                if n == 2 * S_TAIL + 1:
                    turn_outputs(0)
                if n == 2 * S_LN + 1:
                    ln_out("m", XT, *ln2, seqs=(0,))
            for k in range(E * B * FC):
                act.wait_ge(gv_mm, k + 1)
                act.activation(sg[:, k % 2, :], PS[:, 2 * (k % 2), :], ACT.Silu).then_inc(gate_ready, 1)
                if k == 1:
                    turn_outputs(1)
                elif k == K_LNM:
                    ln_out("m", XT, *ln2, seqs=(1,))
                elif k == K_LNC:
                    ln_out("c", XT, seqs=(0,))
            def inner_input(b):
                act.wait_ge(s_in_mm, b + 1)
                act.activation(sT[:, b, :], PS[:, S_BANK[b], :], ACT.Identity, bias=vec[:, V_BIN:V_BIN + 1]).then_inc(s_in_ready, 1)
                act.wait_ge(s_in_ready, b + 1)

            def inner_units(b, js):
                for j in js:
                    act.activation(RJ[:, b, j, :], sT[:, b, :], ACT.Relu, scale=vec[:, V_W1 + j:V_W1 + j + 1],
                                   bias=vec[:, V_B1 + j:V_B1 + j + 1]).then_inc(relu_ready, 1)

            def first_inner():
                inner_input(0)
                inner_units(0, range(1))

            units("C", {U_LNC: lambda: ln_out("c", XT, seqs=(1,)), U_LND: lambda: ln_out("d", XT, seqs=(0,)),
                        2 * NT: first_inner})
            inner_units(0, range(1, GH))
            ln_out("d", XT, seqs=(1,))
            inner_input(1)
            inner_units(1, range(GH))

        @block.tensor
        def _(pe):
            def mm(o, lhsT, rhs, start=True, stop=True):
                return pe.matmul(o, lhsT, rhs, start=start, stop=stop)

            def turn(name, src, seqs=range(B)):
                for b in seqs:
                    pe.wait_ge(ln_norm[name], QT * b + QT)
                    if b:
                        pe.wait_ge(ln_T[name], b)
                    for t in range(QT):
                        i = pe.transpose(PS[:, LN_BANK, t * P:t * P + P], src[:, QT * b + t, :], ident)
                    i.then_inc(ln_turned[name], 1)

            def units(st, kk, vwm, vwr, between={}):
                n_u, per = UNITS[st], PER[st]
                for u in range(n_u + 3):
                    if u < n_u:
                        n, hg = divmod(u, per)
                        b, t = divmod(n, QT)
                        if t == 0 and hg == 0:
                            pe.wait_ge(ln_T["a" if st == "A" else "c"], b + 1)
                        for k, (h0, h1) in enumerate(BANK_HEADS):
                            w = (h1 - h0) * KEYS
                            at = hg * UW + h0 * KEYS
                            o = PS[:, k, 0:w]
                            if u >= 1:
                                pe.wait_ge(unit_shift[st], 3 * (u - 1) + k + 1)
                            i = mm(o, XT[:, b, t * P:t * P + P], kk[:, b, at:at + w], stop=st == "C")
                            if st == "A":
                                i = mm(o, onesb[:], browb[:, b, at:at + w], start=False)
                            i.then_inc(scores_mm[st], 1)
                    if u >= 3:
                        v = u - 3
                        n, hg = divmod(v, per)
                        b = n // QT
                        pe.wait_ge(unit_PT[st], v + 1)
                        if hg == 0 and n >= 1:
                            pe.wait_ge(tile_added[st], n)
                        for k in range(BLK):
                            if k < GH:
                                h = GH * hg + k
                                w = vwm[:, b, h * D:h * D + D]
                            else:
                                w = vwr[:, b, 2 * hg + k - GH, :]
                            i = mm(PS[:, 6, 0:D], PT[v % 2][:, k, :], w,
                                   start=hg == 0 and k == 0, stop=hg == per - 1 and k == BLK - 1)
                        if hg == per - 1:
                            i.then_inc(tile_mm[st], 1)
                    if 2 <= u <= n_u + 1:
                        v = u - 2
                        pe.wait_ge(unit_norm[st], 2 * v + 2)
                        if v >= 1:
                            pe.wait_ge(unit_PT[st], v)
                        elif st == "A":
                            pe.wait_ge(preA_act, len(PREA))
                        else:
                            pe.wait_ge(moe_added, E * NT)
                        for k in range(BLK):
                            i = pe.transpose(PS[:, 3 + k // 4, (k % 4) * P:(k % 4) * P + P],
                                             PN[v % 2][:, k * P:k * P + P], ident)
                        i.then_inc(unit_turned[st], 1)
                    if u in between:
                        between[u]()

            def fold_A(m0, m1):
                for m in range(m0, m1):
                    kind, b, k = PREA[m]
                    bank = 3 + m % 3
                    if m >= 3:
                        pe.wait_ge(preA_act, m - 2)
                    if kind == "kk":
                        h0, h1 = BANK_HEADS[k]
                        pe.wait_ge(kzA_ready, b + 1)
                        i = mm(PS[:, bank, 0:(h1 - h0) * KEYS], wqA, KzA[:, b, h0:h1, :])
                    elif kind == "vw":
                        pe.wait_ge(ld_wo, 16)
                        i = mm(PS[:, bank, :], ctxT[:, b, 0:KM], woT[:, 512 * k:512 * k + 512])
                    else:
                        for h in range(HA):
                            g, j = divmod(h, 4)
                            i = mm(PS[32 * j:32 * j + 32, bank, g * D:g * D + D], ctxT[:, b, KM:KPAD],
                                   woT[:, h * D:h * D + D])
                    i.then_inc(preA_mm, 1)

            def fold_C(n0, n1):
                done = [0]
                for kind, i, k in PREC:
                    done.append(done[-1] + k)
                for n in range(n0, n1):
                    kind, i, _ = PREC[n]
                    bank = n % 3
                    if n == 0:
                        pe.wait_ge(ld_c, 80)
                        pe.wait_ge(unit_shift["A"], 3 * NT)
                    if n >= 3:
                        pe.wait_ge(preC_act, done[n - 2])
                    if kind == "kk":
                        pe.wait_ge(preC_act, done[1 + PREC.index(("k", i // 2, 2))])
                    elif kind in ("vw", "vr"):
                        pe.wait_ge(preC_act, done[1 + PREC.index(("v", 2 * i[0] + 1, 1))])
                    if kind == "k":
                        q = mm(PS[:, bank, 0:B * KEYS], wkC[:, i * P:i * P + P], ctxT[:, :, 0:KEYS])
                    elif kind == "v":
                        q = mm(PS[:, bank, 0:B * KPAD], wvC[:, i * P:i * P + P], ctxT[:])
                    elif kind == "kk":
                        q = mm(PS[:, bank, 0:B * KEYS], wqT[:, i // 2, :], kz[:, (i // 2) % 2, i % 2, :])
                    elif kind == "vw":
                        g, b = i
                        for c in range(2):
                            q = mm(PS[:, bank, 256 * c:256 * c + 256], vT[:, (2 * g + c) % 4, b * KPAD:b * KPAD + KM],
                                   woutZ[:, 2 * g + c])
                    elif kind == "vr":
                        g, b = i
                        for j in range(4):
                            c = 2 * g + j // 2
                            q = mm(PS[32 * j:32 * j + 32, bank, 0:D], vT[:, c % 4, b * KPAD + KM:b * KPAD + KPAD],
                                   woutZ[:, c, j % 2, :])
                    else:
                        pe.wait_ge(conv_ready, i + 1)
                        for t in range(QT):
                            q = mm(PS[:, bank, t * P:t * P + P], HC2[:, i, t * P:t * P + P], aqkv[:, 4, :])
                    q.then_inc(preC_mm, 1)

            pe.wait_ge(zeroed, 3)
            pe.wait_ge(ld_a, 48)
            mm(PS[0:32, 0, 0:B * KEYS], wkTA, ctxT[:, :, 0:KEYS]).then_inc(preA_mm, 1)
            pe.wait_ge(ktA_ready, 1)
            mm(PS[0:HA, 1, 0:B * KEYS], bqA, KTA.rearrange("p b k -> p (b k)")).then_inc(bias8_mm, 1)
            fold_A(0, 3)
            pe.wait_ge(ld_cst, 16)
            turn("a", XN, (0,))
            pe.wait_ge(preA_act, 3)
            pe.wait_ge(brow_ready, 96)

            def first_gap():
                fold_A(3, 7)
                turn("a", XN, (1,))
                fold_A(7, 10)

            units("A", kkA, vwAm, vwAr, {0: first_gap, 1: lambda: fold_A(10, len(PREA)), NT: lambda: fold_C(0, F_UNIT[0]),
                                         NT + 1: lambda: fold_C(F_UNIT[0], F_UNIT[1]),
                                         NT + 2: lambda: fold_C(F_UNIT[1], F_UNIT[2])})
            def queries_keys(b):
                pe.wait_ge(conv_ready, b + 1)
                if b:
                    pe.wait_ge(qk_ready, b)
                else:
                    pe.wait_ge(tile_added["A"], NT)
                for s in range(4):
                    mm(PS[:, 3 + s, :], aqkv[:, s, :], HC2[:, b, :]).then_inc(qkv_mm, 1)

            turn("b", XN, (0,))
            fold_C(F_UNIT[2], F_QKV[0])
            pe.wait_ge(ld_b, 64)
            queries_keys(0)
            fold_C(F_QKV[0], F_LN)
            turn("b", XN, (1,))
            fold_C(F_LN, F_QKV[1])
            queries_keys(1)
            fold_C(F_QKV[1], len(PREC))
            pe.wait_ge(preC_act, N_PREC)
            pe.wait_ge(qk_ready, B)
            pe.wait_ge(consts_ready, 1)
            def turn_maxima(b):
                pe.wait_ge(*((s1_max, 2 * (64 - M_MERGE)) if b else (s_max, 32)))
                if b:
                    pe.wait_ge(m_split, b)
                pe.transpose(PS[0:HB * QT, 6, 0:P], mB[:, b].rearrange("p h t -> p (h t)"), ident).then_inc(m_turned, 1)

            def scores_for_maximum(m):
                b, n = divmod(m, 32)
                hp, qt = divmod(n, QT)
                w = (qt + 1) * P
                if m == M_MERGE:
                    pe.wait_ge(m_split, 1)
                elif 3 <= m < M_MERGE:
                    pe.wait_ge(s_max, m - 2)
                for heads, bank, mm_done, _, count in max_parts(m):
                    if m > M_MERGE and count > 3:
                        pe.wait_ge(s1_max, count - 3)
                    for j in heads:
                        h = 2 * hp + j
                        o = PS[:, bank + j - heads[0], 0:w]
                        mm(o, qs[b][:, h, qt * P:w], ks[b][:, h, 0:w], stop=False)
                        i = mm(o[:, w - P:w], identb, mask_qk, start=False)
                    i.then_inc(mm_done, 1)

            pe.wait_ge(stack_ready[0], 16 * 12)
            for m in range(32):
                scores_for_maximum(m)
            pe.wait_ge(stack_ready[1], 16 * 12)
            for m in range(32, M_MERGE):
                scores_for_maximum(m)
                if m == M_TURN - 1:
                    turn_maxima(0)

            def outputs(s, pair):
                bg, kt = divmod(s, QT)
                b, g = divmod(bg, 4)
                pe.wait_ge(st_exp, 2 * s + pair + 1)
                if s == 0 and pair == 0:
                    pe.wait_ge(v_ready, B)
                if kt == 0 and pair == 0:
                    if b == 0 and g >= 1:
                        pe.wait_ge(yg_ready, bg)
                    elif bg == 4:
                        pe.wait_ge(y_norm, QT)
                    elif bg == 5:
                        pe.wait_ge(attn_added, 1)
                    elif bg >= 6:
                        pe.wait_ge(yg_ready, bg - 1)
                for j in range(2 * pair, 2 * pair + 2):
                    i = mm(PS[32 * j:32 * j + 32, av_bank(b, g), kt * P:T], vaug[:, b, kt, 4 * g + j, :],
                           PTb[:, 4 * (s % 2) + j, 0:T - kt * P], start=kt == 0, stop=kt == QT - 1)
                i.then_inc(av_step, 1)

            def turn_outputs(b, tiles):
                for qt in tiles:
                    if qt == 0:
                        pe.wait_ge(yg_ready, 4 * b + 4)
                        pe.wait_ge(m_split, B)
                        if b:
                            pe.wait_ge(routed, b)
                    if qt == QT - 1:
                        pe.wait_ge(y_norm, QT * b + 1)
                    for g in range(4):
                        i = pe.transpose(PS[:, Y_BANK[qt], g * P:g * P + P], yg[:, g, qt * P:qt * P + P], ident)
                    i.then_inc(y_turned, 1)

            def turn_normalised(b):
                pe.wait_ge(y_norm, QT * b + QT)
                if b:
                    pe.wait_ge(cb_ready, 1)
                for qt in range(QT):
                    i = pe.transpose(PS[:, LN_BANK, qt * P:qt * P + P], yn[:, qt], ident)
                i.then_inc(yT_mm, 1)

            def project_outputs(b):
                pe.wait_ge(yT_ready, b + 1)
                for qt in range(QT):
                    i = mm(PS[:, 5, qt * P:qt * P + P], yT[:, qt], projw[:])
                i.then_inc(proj_mm, 1)

            def logits(b):
                pe.wait_ge(ln_T["m"], b + 1)
                for t in range(QT):
                    n = QT * b + t
                    i = mm(PS[:, 6, n * E:n * E + E], XT[:, b, t * P:t * P + P], rw[:])
                i.then_inc(logit_mm, 1)

            for s in range(2 * 16):
                b, step = divmod(s, 16)
                if step == 0:
                    pe.wait_ge(m_ready[b], 16)
                g, kt = divmod(step, QT)
                w = T - kt * P
                for pair in range(2):
                    if s >= 1:
                        pe.wait_ge(st_exp, 2 * (s - 1) + pair + 1)
                    else:
                        pe.wait_ge(s_max, M_MERGE)
                    for j in range(2):
                        h = 4 * g + 2 * pair + j
                        o = PS[:, 2 * pair + j, 0:w]
                        mm(o, ks[b][:, h, kt * P:kt * P + P], qs[b][:, h, kt * P:T], stop=False)
                        i = mm(o[:, 0:P], identb, mask_kq, start=False)
                    i.then_inc(st_mm, 1)
                    if s < S_MAX:
                        scores_for_maximum(M_MERGE + 2 * s + pair)
                    if s >= 1:
                        outputs(s - 1, pair)
                if s == S_MAX:
                    turn_maxima(1)
                if s == 16:
                    turn_outputs(0, range(QT))
                    turn_normalised(0)
                elif s == S_TAIL + 1:
                    project_outputs(0)
                elif s == S_LN:
                    turn("m", XN, (0,))
                elif s == S_LN + 1:
                    logits(0)
                    pe.wait_ge(ww_ready, GH + 1)
                    mm(PS[:, LN_BANK, 0:D], b2r[:], wout2[0:M1, :]).then_inc(cb_mm, 1)
            for pair in range(2):
                outputs(31, pair)
            turn_outputs(1, range(QT - 1))

            def hidden(k):
                n, f = divmod(k, FC)
                b, e = divmod(n, E)
                if k == 0:
                    pe.wait_ge(ld_moe, 32)
                if k >= 2:
                    pe.wait_ge(g_ready, k - 1)
                if k == E * FC:
                    pe.wait_ge(ln_T["m"], B)
                mm(PS[:, 2 * (k % 2), :], wv[:, e, f * P:f * P + P], XT[:, b, :])
                mm(PS[:, 2 * (k % 2) + 1, :], wv[:, e, FF + f * P:FF + f * P + P], XT[:, b, :]).then_inc(gv_mm, 1)

            def project(n):
                pe.wait_ge(g_ready, FC * n + FC)
                if n >= 2:
                    pe.wait_ge(moe_added, QT * (n - 1))
                if n == 1:
                    pe.wait_ge(attn_added, B)
                for t in range(QT):
                    for f in range(FC):
                        i = mm(PS[:, 4 + n % 2, t * P:t * P + P], G[:, n % 2, f, t * P:t * P + P],
                               pj[:, n % E, f, :], start=f == 0, stop=f == FC - 1)
                i.then_inc(moe_mm, 1)

            for k in range(E * B * FC):
                hidden(k)
                n, f = divmod(k, FC)
                if k == 1:
                    turn_outputs(1, (QT - 1,))
                    turn_normalised(1)
                elif k == 2:
                    project_outputs(1)
                elif k == K_LNM:
                    turn("m", XN, (1,))
                elif k == K_LNM + 2:
                    logits(1)
                elif k == K_LNC:
                    turn("c", XN, (0,))
                if f == 1 and 1 <= n < E * B - 1:
                    project(n - 1)
            pe.wait_ge(g_ready, E * B * FC)
            def inner_input(b):
                pe.wait_ge(ln_T["d"], b + 1)
                if b == 0:
                    pe.wait_ge(unit_shift["C"], 6 * NT)
                mm(PS[:, S_BANK[b], :], win2[:], XT[:, b, :]).then_inc(s_in_mm, 1)

            def last_outputs(b, js):
                for j in js:
                    pe.wait_ge(relu_ready, GH * b + j + 1)
                    for t in range(QT):
                        i = mm(PS[:, F_BANK[b][t], 0:D], RJ[:, b, j, t * P:t * P + P], WW[:, j, :],
                               start=j == 0, stop=j == GH - 1)
                        if j == GH - 1:
                            i.then_inc(ffn_mm, 1)

            units("C", kkC, vwCm, vwCr, {
                0: lambda: project(E * B - 2), 1: lambda: project(E * B - 1),
                U_LNC: lambda: turn("c", XN, (1,)), U_LND: lambda: turn("d", XN, (0,)),
                2 * NT: lambda: inner_input(0),
                2 * NT + 1: lambda: last_outputs(0, range(1)),
                2 * NT + 2: lambda: last_outputs(0, range(1, GH))})
            pe.wait_ge(ffn_added, QT)
            turn("d", XN, (1,))
            pe.wait_ge(tile_added["C"], NT)
            inner_input(1)
            last_outputs(1, range(GH))


def _rope():
    f32 = np.float32
    inv = (f32(1.0) / f32(10000.0) ** (np.arange(0, HDB, 2, dtype=f32) / f32(HDB))).astype(f32)
    fr = np.arange(T, dtype=f32)[:, None] * inv[None, :]
    emb = np.concatenate([fr, fr], axis=1)
    sign = np.where(np.arange(HDB) < HDB // 2, -1.0, 1.0).astype(f32)
    cos, sin = np.cos(emb), np.sin(emb) * sign
    return np.ascontiguousarray(np.stack([np.repeat(cos.T, HB, 0), np.repeat(sin.T, HB, 0)], 1), f32)


def _consts():
    i = np.arange(P)
    later = i[None, :] > i[:, None]
    return np.ascontiguousarray(np.stack([np.eye(P), np.where(later, NEG, 0.0), np.where(later.T, NEG, 0.0)], 1), np.float32)


def _layout(a):
    f32 = np.float32
    vec = np.zeros((P, V_N), f32)
    vec[:, V_LN1W], vec[:, V_LN1B] = a["L0_ffn_ln1_w"], a["L0_ffn_ln1_b"]
    vec[:, V_LN2W], vec[:, V_LN2B] = a["L0_ffn_ln2_w"], a["L0_ffn_ln2_b"]
    vec[:, V_CONV:V_CONV + 3] = a["L0_ffn_conv_w"][:, 0, :]
    for half in range(2):
        r, j = slice(M1 * half, M1 * half + M1), slice(GH * half, GH * half + GH)
        vec[r, V_W1:V_W1 + GH] = a["L1_ffn_W1"][:, j]
        vec[r, V_B1:V_B1 + GH] = a["L1_ffn_b1"][:, j]
        vec[r, V_W2:V_W2 + GH] = a["L1_ffn_W2"][:, j]
        vec[r, V_BIN] = a["L1_ffn_bin_"]
        vec[r, V_B2] = a["L1_ffn_b2"]
    vec[0:32, V_BQ], vec[0:32, V_BK] = a["L0_xattn_bq"], a["L0_xattn_bk"]
    vec[0:32, V_HM:V_HM + HA] = np.repeat(np.eye(HA, dtype=f32), HDA, 0)
    rows = np.zeros((R_N, D), f32)
    rows[R_BO], rows[R_BOUT1], rows[R_BOUT2] = a["L0_xattn_bo"], a["L1_xattn_bout"], a["L1_ffn_bout"]
    rows[R_RANK, 0:NT * E] = np.tile(np.arange(E, 0, -1), NT)
    w = a["L0_ffn_attn_w"]
    by_dim = np.arange(HB * HDB).reshape(HB, HDB).T
    turned = np.roll(by_dim, -(HDB // 2), axis=0)
    q, k, v = w[:, 0:D], w[:, D:2 * D], w[:, 2 * D:3 * D]
    qkv = np.concatenate([q[:, by_dim.ravel()], q[:, turned.ravel()], k[:, by_dim.ravel()], k[:, turned.ravel()], v], 1)
    wkv = a["L1_xattn_Wkv"]
    return {
        "x": a["x"], "ctxT": a["ctx_1024"].transpose(2, 0, 1), "mask_keys": a["mask_BxS2_bk0"].reshape(-1).view(np.int32)[None, :],
        "mask_x": a["mask_BxS_ik0"].reshape(NT, P).T, "vec": vec, "rows": rows, "consts": _consts(), "cossin": _rope(),
        "A_WkT": a["L0_xattn_Wk"].T, "A_Wq": a["L0_xattn_Wq"],
        "A_WoT": a["L0_xattn_Wo"].reshape(D, HA, D).transpose(2, 1, 0).reshape(D, HA * D),
        "B_qkv": qkv, "B_proj": a["L0_ffn_proj_w"], "router": a["L0_ffn_router_w"],
        "wv": a["L0_ffn_expert_wv"], "pj": a["L0_ffn_expert_proj"],
        "C_WqT": a["L1_xattn_Wq"].T, "C_Wk": wkv[:, 0:HC * HDC], "C_Wv": wkv[:, HC * HDC:], "C_Wout": a["L1_xattn_Wout"],
        "D_Win": a["L1_ffn_Win"], "D_Wout": a["L1_ffn_Wout"],
    }


def kernel(**inputs):
    import concourse.bacc as bacc
    from concourse.bass_utils import run_bass_kernel_spmd

    arrays = {f"in_{k}": np.ascontiguousarray(v) for k, v in _layout({k: np.asarray(v) for k, v in inputs.items()}).items()}
    nc = bacc.Bacc("TRN2", target_bir_lowering=False, num_devices=1)
    t_in = {k[3:]: nc.dram_tensor(k, a.shape, mybir.dt.from_np(a.dtype), kind="ExternalInput").ap()
            for k, a in arrays.items()}
    out = nc.dram_tensor("out", (B, T, D), F32, kind="ExternalOutput").ap()
    program(nc, t_in, out)
    r = run_bass_kernel_spmd(nc, [arrays], core_ids=[0])
    return r.results[0]["out"]
```

```python
from contextlib import ExitStack

import numpy as np

import concourse.bass as bass
from concourse import mybir

F32 = mybir.dt.float32
BF16 = mybir.dt.bfloat16
I32 = mybir.dt.int32
U8 = mybir.dt.uint8
ALU = mybir.AluOpType
ACT = mybir.ActivationFunctionType
AX = mybir.AxisListType

P = 128
B, T, D = 2, 512, 128
QT = T // P
NT = B * QT
KEYS = 154
KM, KR = 128, 26
KPAD = 160
HA, HDA = 8, 4
HB, HDB = 16, 8
HC, HDC = 16, 64
GH = 8
BANK_HEADS = ((0, 3), (3, 6), (6, 8))
UW = GH * KEYS
BLK = GH + GH // 4
E, FF = 4, 512
FC = FF // P
NEG = -1.0e30
EPS = 1.0e-5
MASK_NEG = 1.0e6
M1 = 64
ROWS = 96
SPLIT = 9 * HDB

(V_LN1W, V_LN1B, V_LN2W, V_LN2B, V_CONV, V_W1, V_B1, V_W2, V_BIN, V_B2, V_BQ, V_BK, V_HM) = (
    0, 1, 2, 3, 4, 7, 15, 23, 31, 32, 33, 34, 35)
V_N = 43
R_BO, R_BOUT1, R_BOUT2, R_RANK, R_N = 0, 1, 2, 3, 4


class Own:

    def __init__(self, eng, sem):
        self.eng, self.sem, self.n = eng, sem, 0

    def __call__(self, ins):
        ins.then_inc(self.sem, 1)
        self.n += 1

    def wait(self):
        self.eng.wait_ge(self.sem, self.n)


class Carve:

    def __init__(self, tensor):
        self.t, self.at = tensor, 0

    def f32(self, cols, rows=P):
        a = self.t[0:rows, self.at:self.at + cols]
        self.at += cols
        return a

    def bf16(self, cols, rows=P):
        return self.f32(cols // 2, rows).bitcast(BF16)


def program(nc, t_in, out):
    ctx = ExitStack()
    with ctx:
        def sb(name, shape, dt=F32):
            return ctx.enter_context(nc.sbuf_tensor(name, shape, dt))

        def sem(name):
            return ctx.enter_context(nc.semaphore(name))

        X = sb("X", [P, NT, D])
        U = sb("U", [P, NT, D])
        XN = sb("XN", [P, NT, D])
        XT = sb("XT", [P, B, T])
        HT = sb("HT", [P, B, T + 2])
        HC2 = sb("HC2", [P, B, T])
        vec = sb("vec", [P, V_N])
        rowv = sb("rowv", [P, R_N, D])
        cst = sb("cst", [P, 3, P])
        cstb = sb("cstb", [P, 3, P], BF16)
        cossin = sb("cossin", [P, 2, T])
        ctxT = sb("ctxT", [P, B, KPAD])
        ones = sb("ones", [P, P])
        onesb = sb("onesb", [P, P], BF16)
        maskx = sb("maskx", [P, NT], I32)
        rowbias = sb("rowbias", [P, NT])
        stats = sb("stats", [P, NT, 6])
        mv = sb("mv", [P, NT, 2])
        ve = sb("ve", [P, NT])
        rstd = sb("rstd", [P, NT])
        minus_half = sb("minus_half", [P, NT])
        mraw = sb("mraw", [P, 2, GH])
        umax = sb("umax", [P, 2, GH])
        usum = sb("usum", [P, 3, GH])
        urec = sb("urec", [P, 3, GH])
        mB = sb("mB", [P, B, HB, QT])
        nmf = sb("nmf", [HB * QT, 3, P])
        nm3 = sb("nm3", [HB * QT, B, 3, P], BF16)
        rB = sb("rB", [P, 2, HB])
        lg = sb("lg", [P, 4, NT, E])
        mx = sb("mx", [P, 2, NT])
        onehot = sb("onehot", [P, NT, E])
        rw = sb("rw", [P, E])
        b2r = sb("b2r", [M1, P])
        wout2 = sb("wout2", [P, D])
        WW = sb("WW", [P, GH, D])
        win2 = sb("win2", [P, P])
        cbias = sb("cbias", [P, D])
        aqkv = sb("aqkv", [P, 5, P])
        projw = sb("projw", [P, D])
        kkC = sb("kkC", [P, B, HC * KEYS])
        vwCm = sb("vwCm", [P, B, HC * D])
        vwCr = sb("vwCr", [P, B, HC // 4, D])

        cw = sb("cw", [P, 7632])
        c = Carve(cw)
        wkC = c.f32(HC * HDC)
        wvC = c.f32(HC * HDC)
        wqT = c.f32(HC * HDC).rearrange("p (c d) -> p c d", c=8)
        woutZ = c.f32(HC * D).rearrange("p (c j o) -> p c j o", c=8, j=2)
        kz = c.f32(2 * 2 * B * KEYS).rearrange("p (r j n) -> p r j n", r=2, j=2)
        vT = c.f32(4 * B * KPAD).rearrange("p (r n) -> p r n", r=4)
        assert c.at <= 7632
        c = Carve(cw)
        vaug = c.f32(B * QT * HB * 32).rearrange("p (b t h m) -> p b t h m", b=B, t=QT, h=HB)
        yg = c.f32(4 * T).rearrange("p (g q) -> p g q", g=4)
        yn = c.f32(QT * D).rearrange("p (t d) -> p t d", t=QT)
        yT = c.f32(T).rearrange("p (t q) -> p t q", t=QT)

        BIGW = 22000
        big = sb("big", [P, BIGW])
        c = Carve(big)
        Pt = [c.f32(UW).rearrange("p (h k) -> p h k", h=GH) for _ in range(3)]
        PN = [c.f32(BLK * P) for _ in range(2)]
        PT = [c.f32(BLK * P).rearrange("p (n q) -> p n q", n=BLK) for _ in range(2)]
        kkA = c.f32(B * UW).rearrange("p (b n) -> p b n", b=B)
        vwAm = c.f32(B * HA * D).rearrange("p (b n) -> p b n", b=B)
        vwAr = c.f32(B * 2 * D).rearrange("p (b g o) -> p b g o", b=B, g=2)
        woT = c.f32(HA * D)
        KzA = c.f32(B * UW, ROWS).rearrange("p (b h k) -> p b h k", b=B, h=HA)
        KTA = c.f32(B * KEYS, HA * HDA).rearrange("p (b k) -> p b k", b=B)
        wqA = c.f32(D, ROWS)
        wkTA = c.f32(HA * HDA)
        bqA = c.f32(HA, HA * HDA)
        browb = c.bf16(B * UW).rearrange("p (h b k) -> p h b k", h=HA, b=B)
        bias8 = c.f32(B * KEYS, HA)
        rest8 = c.f32(B * KEYS, HA)
        part8 = c.bf16(3 * B * KEYS, HA).rearrange("p (a b k) -> p a b k", a=3, b=B)
        mrow = c.f32(B * KEYS, HA)
        mask_words = c.f32(B * KEYS // 4, HA).bitcast(I32)
        masku = mask_words.bitcast(U8)
        assert c.at <= BIGW, c.at
        c = Carve(big)
        ks, qs = [], []
        for b in range(B):
            ks.append(c.bf16(HB * T, ROWS).rearrange("p (h t) -> p h t", h=HB))
            qs.append(c.bf16(HB * T, ROWS).rearrange("p (h t) -> p h t", h=HB))
        at = c.at
        qk = c.f32(2 * T).rearrange("p (s t) -> p s t", s=2)
        tsin = c.f32(2 * T).rearrange("p (s t) -> p s t", s=2)
        P3 = c.bf16(2 * 3 * T).rearrange("p (s a t) -> p s a t", s=2, a=3)
        assert c.at <= BIGW, c.at
        c.at = at
        PTb = c.f32(8 * T).rearrange("p (n q) -> p n q", n=8)
        assert c.at <= BIGW, c.at
        c = Carve(big)
        wv = c.f32(E * 2 * FF).rearrange("p (e n) -> p e n", e=E)
        c.at = HB * T - E * FC * D
        pj = c.f32(E * FC * D).rearrange("p (e f d) -> p e f d", e=E, f=FC)
        c.at = HB * T
        sg = c.f32(2 * T).rearrange("p (r t) -> p r t", r=2)
        G = c.f32(2 * FC * T).rearrange("p (r f t) -> p r f t", r=2, f=FC)
        c = Carve(big)
        c.at = 3 * UW + 4 * BLK * P
        sT = c.f32(B * T)
        RJ = c.f32(GH * B * T).rearrange("p (j t) -> p j t", j=GH)
        inner = c.f32(2 * B * T).rearrange("p (r t) -> p r t", r=2)
        assert c.at <= BIGW, c.at

        PS = ctx.enter_context(nc.psum_tensor("PS", [P, 8, 512], F32))
        scr_qk = nc.dram_tensor("scr_qk", (B, 2, 3, P, T), BF16, kind="Internal").ap()
        scr_m = nc.dram_tensor("scr_m", (B, 3, HB * QT * P), BF16, kind="Internal").ap()

        F_UNIT = (3, 6, 9)
        F_QKV = (14,30)
        F_LN = 26
        F_LATE = 32

        def prec_jobs():
            for c in range(HC // 2 + 1):
                if c < HC // 2:
                    yield "k", c, 2
                    yield "v", c, 1
                if c >= 1:
                    yield "kk", 2 * c - 2, 1
                    yield "kk", 2 * c - 1, 1
                if c >= 2 and c % 2 == 0:
                    for b in range(B):
                        yield "vw", (c // 2 - 1, b), 1
                        yield "vr", (c // 2 - 1, b), 1

        PREC = list(prec_jobs())

        def fold_bank(n):
            return n % 3 if n < F_LATE else 6 + n % 2

        for b in range(B):
            PREC.insert(F_QKV[b], ("xv", b, 1))
        N_PREC = sum(j[2] for j in PREC)

        ld_x = [sem(f"ld_x{b}") for b in range(B)]
        ld_a, ld_wq, ld_wo, ld_mask, ld_vec, ld_cst, ld_rows, ld_c, ld_b, ld_moe, ld_d = (sem(n) for n in (
            "ld_a", "ld_wq", "ld_wo", "ld_mask", "ld_vec", "ld_cst", "ld_rows", "ld_c", "ld_b", "ld_moe", "ld_d"))
        zeroed = sem("zeroed")
        zeroedB = sem("zeroedB")
        zeroedC = sem("zeroedC")
        LNS = ("a", "u", "b", "m", "c", "d")
        ln_var = {n: sem(f"ln_var_{n}") for n in LNS}
        ln_rstd = {n: sem(f"ln_rstd_{n}") for n in LNS}
        ln_norm = {n: sem(f"ln_norm_{n}") for n in LNS}
        ln_turned = {n: sem(f"ln_turned_{n}") for n in LNS if n != "u"}
        ln_T = {n: sem(f"ln_T_{n}") for n in LNS if n != "u"}
        preA_mm, preA_act, ktA_ready = sem("preA_mm"), sem("preA_act"), sem("ktA_ready")
        bqA_ready, bias8_mm = sem("bqA_ready"), sem("bias8_mm")
        kzA_ready, part8_ready, brow_ready, consts_ready = sem("kzA_ready"), sem("part8_ready"), sem("brow_ready"), sem("consts_ready")
        preC_mm, preC_act = sem("preC_mm"), sem("preC_act")
        scores_mm = {s: sem(f"scores_mm_{s}") for s in "AC"}
        unit_shift = {s: sem(f"unit_shift_{s}") for s in "AC"}
        unit_exp = {s: sem(f"unit_exp_{s}") for s in "AC"}
        unit_rec = {s: sem(f"unit_rec_{s}") for s in "AC"}
        unit_norm = {s: sem(f"unit_norm_{s}") for s in "AC"}
        unit_turned = {s: sem(f"unit_turned_{s}") for s in "AC"}
        unit_PT = {s: sem(f"unit_PT_{s}") for s in "AC"}
        tile_mm = {s: sem(f"tile_mm_{s}") for s in "AC"}
        tile_added = {s: sem(f"tile_added_{s}") for s in "AC"}
        conv_ready = sem("conv_ready")
        qkv_mm, v_ready, qk_ready, part_step, part_lo = (sem(n) for n in (
            "qkv_mm", "v_ready", "qk_ready", "part_step", "part_lo"))
        scr_written = [sem(f"scr_written{b}") for b in range(B)]
        stack_ready = [sem(f"stack_ready{b}") for b in range(B)]
        s_mm, s_max = sem("s_mm"), sem("s_max")
        s1_mm, s1_max = sem("s1_mm"), sem("s1_max")
        m_turned, m_split = sem("m_turned"), sem("m_split")
        m_written = [sem(f"m_written{b}") for b in range(B)]
        m_ready = [sem(f"m_ready{b}") for b in range(B)]
        st_mm, st_exp, av_step, yg_ready = sem("st_mm"), sem("st_exp"), sem("av_step"), sem("yg_ready")
        y_turned, y_norm, yT_mm, yT_ready, proj_mm, attn_added = (sem(n) for n in (
            "y_turned", "y_norm", "yT_mm", "yT_ready", "proj_mm", "attn_added"))
        logit_mm, routed = sem("logit_mm"), sem("routed")
        gv_mm, gate_ready, g_ready, moe_mm, moe_added = (sem(n) for n in (
            "gv_mm", "gate_ready", "g_ready", "moe_mm", "moe_added"))
        cb_mm, cb_ready, b2_ready, inner_ready, ww_ready = (sem(n) for n in (
            "cb_mm", "cb_ready", "b2_ready", "inner_ready", "ww_ready"))
        s_in_mm, s_in_ready, relu_ready, ffn_mm, ffn_added = (sem(n) for n in (
            "s_in_mm", "s_in_ready", "relu_ready", "ffn_mm", "ffn_added"))
        stored = sem("stored")
        own_dve = sem("own_dve")

        UNITS = {"A": NT, "C": 2 * NT}
        PER = {"A": 1, "C": 2}
        LN_BANK = 7
        Z_EARLY, Z_WOUT, Z_ALL = 8, 9, 12
        PARTS = ((0, QT), (QT, NT - 1), (NT - 1, NT))
        S_BANK = (7, 1, 0)
        PIECES = (((0, 2), 2), ((2, 4), 3), ((7, 8), 6), ((4, 6), 4), ((6, 7), 5))
        PART_PIECES = ((0, 1), (3, 4), (2,))
        LAST = 2
        J_JOIN = GH - 2
        J_FIRST = 2
        J_EARLY1 = 4
        J_EARLY = 6
        J_SUM = 6
        Y_BANK = (4, 5, 6, 4)
        M_TURN = 32 + 2
        M_MERGE = 32+10
        S_MAX = (64 - M_MERGE) // 2
        S_TAIL = 17
        S_LN = 21
        K_LNM = 5
        K_LNC = 5 * FC + 6
        U_LNC, U_LND = 5, 2 * QT + 6
        PREA = ([("kk", 0, k) for k in range(3)] + [("vw", 0, k) for k in range(2)] + [("kk", 1, k) for k in range(3)]
                + [("vr", 0, 0)] + [("vw", 1, k) for k in range(2)] + [("vr", 1, 0)])

        def max_parts(m):
            if m < M_MERGE:
                return [((0, 1), 2 * (m % 3), s_mm, s_max, m + 1)]
            k = 2 * (m - M_MERGE)
            return [((j,), 5 + (k + j) % 3, s1_mm, s1_max, k + j + 1) for j in range(2)]

        def av_bank(b, g):
            return 4 + g % 2 if b else 4

        ident = cst[:, 0, :]
        identb, mask_qk, mask_kq = cstb[:, 0, :], cstb[:, 1, :], cstb[:, 2, :]
        block = ctx.enter_context(nc.Block())

        @block.sync
        def _(sp):
            i = t_in
            sp.dma_start(ctxT[:, :, 0:KEYS], i["ctxT"]).then_inc(ld_a, 16)
            sp.dma_start(wkTA, i["A_WkT"]).then_inc(ld_a, 16)
            sp.dma_start(vec[:], i["vec"]).then_inc(ld_vec, 16)
            sp.wait_ge(zeroed, 1)
            sp.dma_start(wqA[0:HA * HDA], i["A_Wq"]).then_inc(ld_wq, 16)
            sp.dma_start(cst[:], i["consts"]).then_inc(ld_cst, 16)
            sp.dma_start(mask_words, i["mask_keys"].to_broadcast([HA, B * KEYS // 4])).then_inc(ld_mask, 16)
            sp.dma_start(rowv[:], i["rows"].unsqueeze(0).to_broadcast([P, R_N, D])).then_inc(ld_rows, 16)
            sp.dma_start(maskx[:], i["mask_x"]).then_inc(ld_rows, 16)
            sp.wait_ge(zeroed, Z_EARLY)
            sp.wait_ge(part8_ready, 1)
            for a in range(3):
                sp.dma_start(browb[32 * a:32 * a + 1].rearrange("p h b k -> p h (b k)"),
                             part8[:, a].rearrange("p b k -> p (b k)")).then_inc(brow_ready, 16)
            sp.dma_start(wkC, i["C_Wk"]).then_inc(ld_c, 16)
            sp.dma_start(wvC, i["C_Wv"]).then_inc(ld_c, 16)
            sp.dma_start(wqT, i["C_WqT"].rearrange("(c p) d -> p c d", p=P)).then_inc(ld_c, 16)
            sp.wait_ge(zeroed, Z_WOUT)
            for j in range(2):
                sp.dma_start(woutZ[64 * j:64 * j + 64, :, j, :],
                             i["C_Wout"].rearrange("(c j e) o -> j e c o", j=2, e=HDC)[j]).then_inc(ld_c, 16)
            sp.dma_start(aqkv[:], i["B_qkv"].rearrange("p (s n) -> p s n", s=5)).then_inc(ld_b, 16)
            sp.dma_start(cossin[:], i["cossin"]).then_inc(ld_b, 16)
            sp.dma_start(projw[:], i["B_proj"]).then_inc(ld_b, 16)
            sp.dma_start(rw[:], i["router"]).then_inc(ld_b, 16)
            for j in range(2):
                sp.dma_start(win2[:, 64 * j:64 * j + 64], i["D_Win"]).then_inc(ld_d, 16)
                sp.dma_start(wout2[64 * j:64 * j + 64, :], i["D_Wout"]).then_inc(ld_d, 16)
            for b in range(B):
                sp.wait_ge(part_lo, b + 1)
                sp.dma_start(scr_qk[b].rearrange("s a r t -> r s a t"), P3).then_inc(scr_written[b], 16)
                sp.wait_ge(scr_written[b], 16)
                sp.wait_ge(zeroedB, 2 * b + 2)
                for a in range(3):
                    sp.dma_start(ks[b][24 * a:24 * a + 24, :, :],
                                 scr_qk[b, 1].rearrange("a (d h) t -> (a d) h t", h=HB)).then_inc(stack_ready[b], 16)
                    for j in range(3):
                        r = 24 * a + 8 * j
                        sp.dma_start(qs[b][r:r + 8, :, :],
                                     scr_qk[b, 0, a].rearrange("(d h) t -> d h t", h=HB)).then_inc(stack_ready[b], 16)
            for b in range(B):
                sp.wait_ge(m_split, b + 1)
                sp.dma_start(scr_m[b].rearrange("a (n q) -> n a q", q=P), nm3[:, b]).then_inc(m_written[b], 16)
                sp.wait_ge(m_written[b], 16)
                sp.wait_ge(*((s1_mm, 2 * (64 - M_MERGE)) if b else (s_mm, 32)))
                sp.dma_start(qs[b][SPLIT:SPLIT + 3, :, :],
                             scr_m[b].rearrange("a (h t) -> a h t", h=HB)).then_inc(m_ready[b], 16)
            sp.wait_ge(st_mm, 32)
            sp.dma_start(wv, i["wv"].rearrange("e p n -> p e n")).then_inc(ld_moe, 16)
            sp.dma_start(pj, i["pj"].rearrange("e (f p) d -> p e f d", p=P)).then_inc(ld_moe, 16)
            for k, ((lo, hi), _) in enumerate(PIECES):
                sp.wait_ge(ffn_added, k + 1)
                sp.dma_start(out.rearrange("b (t p) d -> p (b t) d", p=P)[:, lo:hi, :], X[:, lo:hi, :]).then_inc(stored, 16)
            sp.wait_ge(stored, 16 * len(PIECES))

        @block.gpsimd
        def _(pool):
            pool.memset(wqA, 0.0).then_inc(zeroed, 1)
            pool.memset(ctxT[:, :, KEYS:KPAD], 0.0).then_inc(zeroed, 1)
            pool.memset(KzA, 0.0).then_inc(zeroed, 1)
            pool.memset(minus_half[:], -0.5).then_inc(zeroed, 1)
            pool.memset(onesb[:], 1.0).then_inc(zeroed, 1)
            pool.memset(browb, 0.0).then_inc(zeroed, 1)
            for r in range(2):
                pool.memset(PN[r][:, GH * P:BLK * P], 0.0).then_inc(zeroed, 1)
            pool.wait_ge(zeroed, Z_EARLY)

            def ln_rsqrt(name, seqs=range(B), tiles=None):
                for b in seqs:
                    pool.wait_ge(ln_var[name], b + 1)
                    s = slice(*(tiles or (b * QT, b * QT + QT)))
                    pool.tensor_tensor(rstd[:, s], ve[:, s], minus_half[:, s], ALU.pow).then_inc(ln_rstd[name], 1)

            def unit_norms(st, between={}):
                for u in range(UNITS[st]):
                    if u in between:
                        between[u]()
                    pool.wait_ge(unit_rec[st], u + 1)
                    if u >= 2:
                        pool.wait_ge(unit_turned[st], u - 1)
                    r = urec[:, u % 3, :].unsqueeze(2)
                    pn = PN[u % 2]
                    pool.tensor_tensor(pn[:, 0:GH * P].rearrange("p (h k) -> p h k", h=GH),
                                       Pt[u % 3][:, :, 0:KM], r.to_broadcast([P, GH, KM]), ALU.mult).then_inc(unit_norm[st], 1)
                    pool.tensor_tensor(pn[:, GH * P:BLK * P].rearrange("p (h k) -> p h k", h=GH)[:, :, 0:KR],
                                       Pt[u % 3][:, :, KM:KEYS], r.to_broadcast([P, GH, KR]), ALU.mult).then_inc(unit_norm[st], 1)

            ln_rsqrt("a")
            pool.memset(woutZ, 0.0).then_inc(zeroed, 1)
            pool.memset(ones[:], 1.0).then_inc(zeroed, 1)
            pool.memset(HT[:, :, 0:2], 0.0).then_inc(zeroed, 1)
            pool.memset(kz, 0.0).then_inc(zeroed, 1)
            unit_norms("A", {NT - 1: lambda: ln_rsqrt("u", (0,))})
            ln_rsqrt("b", (0,))
            ln_rsqrt("u", (1,))
            pool.wait_ge(tile_mm["A"], NT)
            two_ones = float(np.array([0x3F803F80], np.uint32).view(np.float32)[0])

            def fill_stacks(b):
                pool.memset(qs[b][64:ROWS].bitcast(F32), 0.0).then_inc(zeroedB, 1)
                pool.memset(ks[b][64:ROWS].bitcast(F32), two_ones).then_inc(zeroedB, 1)

            pool.wait_ge(ln_rstd["u"], B)
            fill_stacks(0)
            pool.wait_ge(zeroedB, 2)
            ln_rsqrt("b", (1,))
            pool.wait_ge(ln_rstd["b"], B)
            fill_stacks(1)
            pool.wait_ge(qk_ready, B)
            pool.wait_ge(scr_written[0], 16)
            pool.wait_ge(zeroedB, 4)
            pool.tensor_copy(P3[:, :, 0, :], qk).then_inc(part_step, 1)
            pool.wait_ge(part_step, 1)
            pool.tensor_tensor(qk, qk, P3[:, :, 0, :], ALU.subtract).then_inc(part_step, 1)
            pool.wait_ge(part_step, 2)
            pool.tensor_copy(P3[:, :, 1, :], qk).then_inc(part_step, 1)
            pool.wait_ge(part_step, 3)
            pool.tensor_tensor(P3[:, :, 2, :], qk, P3[:, :, 1, :], ALU.subtract).then_inc(part_lo, 1)
            pool.wait_ge(part_lo, B)
            pool.wait_ge(preC_act, N_PREC)
            pool.wait_ge(zeroedB, 4)
            pool.memset(vaug, 0.0).then_inc(zeroedB, 1)
            pool.wait_ge(zeroedB, 5)
            pool.memset(vaug[:, :, :, :, HDB:HDB + 1], 1.0).then_inc(zeroedB, 1)
            pool.wait_ge(zeroedB, 6)
            for b in range(B):
                pool.tensor_copy(vaug[:, b, :, :, 0:HDB],
                                 XN[:, QT * b:QT * b + QT, :].rearrange("p t (h d) -> p t h d", h=HB)).then_inc(v_ready, 1)
            ln_rsqrt("m")
            ln_rsqrt("c", (0,))
            pool.wait_ge(ln_rstd["c"], 1)
            pool.wait_ge(gv_mm, E * B * FC)
            pool.memset(PN[0][:, GH * P:BLK * P], 0.0).then_inc(zeroedC, 1)

            def second_blocks():
                pool.wait_ge(unit_norm["C"], 2)
                pool.wait_ge(moe_mm, E * B)
                pool.memset(PN[1][:, GH * P:BLK * P], 0.0).then_inc(zeroedC, 1)
                pool.wait_ge(zeroedC, 2)

            pool.wait_ge(zeroedC, 1)
            unit_norms("C", {1: second_blocks, 2: lambda: ln_rsqrt("c", (1,)), 2 * QT + 3: lambda: ln_rsqrt("d", (0,))})
            for part in range(1, len(PARTS)):
                ln_rsqrt("d", (part,), PARTS[part])

        @block.vector
        def _(dve):
            own = Own(dve, own_dve)
            tile = lambda n: slice(n, n + 1)

            def ln_stats(name, src, b, ready, tiles=None):
                ready()
                lo, hi = tiles or (b * QT, b * QT + QT)
                for n in range(lo, hi):
                    own(dve.bn_stats(stats[:, n, :], src[:, n, :]))
                own.wait()
                for n in range(lo, hi):
                    own(dve.bn_aggr(mv[:, n, :], stats[:, n, :]))
                own.wait()
                s = slice(lo, hi)
                dve.tensor_scalar(ve[:, s], mv[:, s, 1], EPS, None, ALU.add).then_inc(ln_var[name], 1)

            def ln_apply(name, src, dst, b, tiles=None):
                dve.wait_ge(ln_rstd[name], b + 1)
                for n in range(*(tiles or (b * QT, b * QT + QT))):
                    dve.tensor_scalar(dst[:, n, :], src[:, n, :], mv[:, n, 0:1], rstd[:, tile(n)],
                                      ALU.subtract, ALU.mult).then_inc(ln_norm[name], 1)

            def units(st, bias, between={}):
                op0 = ALU.max if st == "A" else ALU.add
                n_u = UNITS[st]
                for u in range(n_u + 1):
                    if u >= 4 and (u - 4) % PER[st] == PER[st] - 1:
                        add_tile(st, (u - 4) // PER[st])
                    if u < n_u:
                        for k, (h0, h1) in enumerate(BANK_HEADS):
                            dve.wait_ge(scores_mm[st], 3 * u + k + 1)
                            s = PS[:, k, 0:(h1 - h0) * KEYS].rearrange("p (h k) -> p h k", h=h1 - h0)
                            own(dve.tensor_reduce(mraw[:, u % 2, h0:h1], s, AX.X, ALU.max))
                        own.wait()
                        sc = bias(u)
                        own(dve.tensor_scalar(umax[:, u % 2, :], mraw[:, u % 2, :], sc, None, op0))
                    if u >= 1:
                        v = u - 1
                        dve.wait_ge(unit_exp[st], v + 1)
                        own(dve.tensor_reduce(usum[:, v % 3, :], Pt[v % 3], AX.X, ALU.add))
                        own.wait()
                        dve.reciprocal(urec[:, v % 3, :], usum[:, v % 3, :]).then_inc(unit_rec[st], 1)
                    if u < n_u:
                        own.wait()
                        if u >= 3:
                            dve.wait_ge(unit_norm[st], 2 * (u - 2))
                        for k, (h0, h1) in enumerate(BANK_HEADS):
                            s = PS[:, k, 0:(h1 - h0) * KEYS].rearrange("p (h k) -> p h k", h=h1 - h0)
                            dve.scalar_tensor_tensor(
                                Pt[u % 3][:, h0:h1, :], s, sc,
                                umax[:, u % 2, h0:h1].unsqueeze(2).to_broadcast([P, h1 - h0, KEYS]),
                                op0, ALU.subtract).then_inc(unit_shift[st], 1)
                    if u in between:
                        between[u]()

            def add_tile(st, n):
                dve.wait_ge(tile_mm[st], n + 1)
                dve.tensor_tensor(X[:, n, :], PS[:, 6, 0:D], X[:, n, :], ALU.add).then_inc(tile_added[st], 1)

            for b in range(B):
                ln_stats("a", X, b, lambda: dve.wait_ge(ld_x[b], 16))
            dve.wait_ge(ld_vec, 16)
            dve.tensor_scalar(bqA, vec[0:32, V_HM:V_HM + HA], vec[0:32, V_BQ:V_BQ + 1], None, ALU.mult).then_inc(bqA_ready, 1)
            dve.wait_ge(preA_mm, 1)
            dve.tensor_scalar(KTA, PS[0:32, 0, 0:B * KEYS].rearrange("p (b k) -> p b k", b=B),
                              vec[0:32, V_BK:V_BK + 1], None, ALU.add).then_inc(ktA_ready, 1)
            dve.wait_ge(ktA_ready, 1)
            dve.wait_ge(zeroed, 3)
            def keys_by_head(b):
                dve.tensor_tensor(KzA[0:HA * HDA, b], KTA[:, b:b + 1, :].to_broadcast([32, HA, KEYS]),
                                  vec[0:32, V_HM:V_HM + HA].unsqueeze(2).to_broadcast([32, HA, KEYS]),
                                  ALU.mult).then_inc(kzA_ready, 1)

            keys_by_head(0)
            dve.wait_ge(ld_mask, 16)
            own(dve.tensor_scalar(mrow, masku, NEG, None, ALU.mult))
            own.wait()
            dve.wait_ge(bias8_mm, 1)
            own(dve.scalar_tensor_tensor(bias8, PS[0:HA, 1, 0:B * KEYS], 0.5, mrow, ALU.mult, ALU.add))
            own.wait()
            parts = part8.rearrange("p a b k -> p a (b k)")
            own(dve.tensor_copy(parts[:, 0], bias8))
            own.wait()
            own(dve.tensor_tensor(rest8, bias8, parts[:, 0], ALU.subtract))
            own.wait()
            own(dve.tensor_copy(parts[:, 1], rest8))
            own.wait()
            dve.tensor_tensor(parts[:, 2], rest8, parts[:, 1], ALU.subtract).then_inc(part8_ready, 1)

            def x_plus(b, row):
                s = slice(QT * b, QT * b + QT)
                own(dve.tensor_tensor(X[:, s, :], X[:, s, :], row.unsqueeze(1).to_broadcast([P, QT, D]), ALU.add))
                own.wait()

            def constants():
                dve.wait_ge(ld_rows, 32)
                for b in range(B):
                    x_plus(b, rowv[:, R_BO, :])
                dve.tensor_copy(cstb[:], cst[:]).then_inc(consts_ready, 1)
                own(dve.tensor_copy(rowbias[:], maskx[:]))
                own.wait()
                own(dve.tensor_scalar(rowbias[:], rowbias[:], -1.0, 1.0, ALU.mult, ALU.add))
                own.wait()
                own(dve.tensor_scalar(rowbias[:], rowbias[:], -MASK_NEG, None, ALU.mult))

            ln_apply("a", X, XN, 0)
            keys_by_head(1)
            ln_apply("a", X, XN, 1)
            dve.wait_ge(ln_norm["a"], NT)

            def ln_u_stats(b):
                ln_stats("u", X, b, lambda: dve.wait_ge(tile_added["A"], QT * b + QT))

            def ln_b_stats(b):
                ln_apply("u", X, U, b)
                ln_stats("b", U, b, lambda: dve.wait_ge(ln_norm["u"], QT * b + QT))

            def convolve(b):
                dve.wait_ge(ln_T["b"], b + 1)
                dve.wait_ge(zeroed, Z_ALL)
                h = HT[:, b, :]
                o = HC2[:, b, :]
                own(dve.tensor_scalar(o, h[:, 0:T], vec[:, V_CONV:V_CONV + 1], None, ALU.mult))
                own.wait()
                own(dve.scalar_tensor_tensor(o, h[:, 1:T + 1], vec[:, V_CONV + 1:V_CONV + 2], o, ALU.mult, ALU.add))
                own.wait()
                dve.scalar_tensor_tensor(o, h[:, 2:T + 2], vec[:, V_CONV + 2:V_CONV + 3], o,
                                         ALU.mult, ALU.add).then_inc(conv_ready, 1)

            def rotate(b):
                dve.wait_ge(ld_b, 64)
                for s in range(2):
                    dve.wait_ge(qkv_mm, 4 * b + 2 * s + 2)
                    own(dve.tensor_tensor(qk[:, s], PS[:, 3 + 2 * s, :], cossin[:, 0], ALU.mult))
                    own(dve.tensor_tensor(tsin[:, s], PS[:, 4 + 2 * s, :], cossin[:, 1], ALU.mult))
                own.wait()
                dve.tensor_tensor(qk, qk, tsin, ALU.add).then_inc(qk_ready, 1)

            def split_first():
                dve.wait_ge(qk_ready, 1)
                own(dve.tensor_copy(P3[:, :, 0, :], qk))
                own.wait()
                own(dve.tensor_tensor(qk, qk, P3[:, :, 0, :], ALU.subtract))
                own.wait()
                own(dve.tensor_copy(P3[:, :, 1, :], qk))
                own.wait()
                dve.tensor_tensor(P3[:, :, 2, :], qk, P3[:, :, 1, :], ALU.subtract).then_inc(part_lo, 1)

            units("A", lambda u: -3.0e38, {0: constants, NT - 1: lambda: ln_u_stats(0), NT: lambda: ln_b_stats(0)})
            add_tile("A", NT - 3)
            ln_apply("b", U, XN, 0)
            add_tile("A", NT - 2)
            convolve(0)
            add_tile("A", NT - 1)
            ln_u_stats(1)
            rotate(0)
            split_first()
            ln_b_stats(1)
            ln_apply("b", U, XN, 1)
            convolve(1)
            rotate(1)
            def split_maxima(b):
                dve.wait_ge(m_turned, b + 1)
                mt = PS[0:HB * QT, 6, 0:P]
                own(dve.tensor_scalar(nmf[:, 0], mt, -1.0, None, ALU.mult))
                own.wait()
                own(dve.tensor_copy(nm3[:, b, 0], nmf[:, 0]))
                own.wait()
                own(dve.tensor_tensor(nmf[:, 1], nmf[:, 0], nm3[:, b, 0], ALU.subtract))
                own.wait()
                own(dve.tensor_copy(nm3[:, b, 1], nmf[:, 1]))
                own.wait()
                dve.tensor_tensor(nm3[:, b, 2], nmf[:, 1], nm3[:, b, 1], ALU.subtract).then_inc(m_split, 1)

            def maximum(m):
                b, n = divmod(m, 32)
                hp, qt = divmod(n, QT)
                for heads, bank, mm_done, max_done, count in max_parts(m):
                    k = len(heads)
                    h = 2 * hp + heads[0]
                    dve.wait_ge(mm_done, count)
                    dve.tensor_reduce(mB[:, b, h:h + k, qt], PS[:, bank:bank + k, 0:(qt + 1) * P],
                                      AX.X, ALU.max).then_inc(max_done, 1)

            def copy_outputs(b, groups):
                for g in groups:
                    dve.wait_ge(av_step, 2 * QT * (4 * b + g + 1))
                    if b:
                        dve.wait_ge(y_turned, QT * b)
                    dve.tensor_copy(yg[:, g, :], PS[:, av_bank(b, g), :]).then_inc(yg_ready, 1)

            def normalise_outputs(b):
                for qt in range(QT):
                    n = QT * b + qt
                    dve.wait_ge(y_turned, n + 1)
                    yv = PS[:, Y_BANK[qt], :].rearrange("p (h m) -> p h m", h=HB)
                    own(dve.reciprocal(rB[:, n % 2, :].unsqueeze(2), yv[:, :, HDB:HDB + 1]))
                    own.wait()
                    if b:
                        dve.wait_ge(yT_mm, b)
                    dve.tensor_tensor(yn[:, qt].rearrange("p (h d) -> p h d", h=HB), yv[:, :, 0:HDB],
                                      rB[:, n % 2, :].unsqueeze(2).to_broadcast([P, HB, HDB]), ALU.mult).then_inc(y_norm, 1)

            def add_attention(b):
                dve.wait_ge(proj_mm, b + 1)
                s = slice(QT * b, QT * b + QT)
                dve.tensor_tensor(U[:, s, :], PS[:, 5, :].rearrange("p (t d) -> p t d", t=QT), U[:, s, :],
                                  ALU.add).then_inc(attn_added, 1)

            def x_plus_u(b):
                s = slice(QT * b, QT * b + QT)
                own(dve.tensor_tensor(X[:, s, :], X[:, s, :], U[:, s, :], ALU.add))
                own.wait()

            def route(b):
                s = slice(QT * b, QT * b + QT)
                dve.wait_ge(logit_mm, b + 1)
                L = PS[:, 6, b * QT * E:(b + 1) * QT * E].rearrange("p (n e) -> p n e", e=E)
                dve.tensor_copy(lg[:, 0, s], L).then_inc(routed, 1)
                dve.wait_ge(routed, b + 1)
                own(dve.tensor_reduce(mx[:, 0, s], lg[:, 0, s], AX.X, ALU.max))
                own.wait()
                own(dve.tensor_tensor(lg[:, 1, s], lg[:, 0, s], mx[:, 0, s].unsqueeze(2).to_broadcast([P, QT, E]), ALU.is_equal))
                own.wait()
                own(dve.tensor_tensor(lg[:, 2, s], lg[:, 1, s],
                                      rowv[:, R_RANK, 0:QT * E].rearrange("p (n e) -> p n e", e=E), ALU.mult))
                own.wait()
                own(dve.tensor_reduce(mx[:, 1, s], lg[:, 2, s], AX.X, ALU.max))
                own.wait()
                own(dve.tensor_tensor(onehot[:, s], lg[:, 2, s], mx[:, 1, s].unsqueeze(2).to_broadcast([P, QT, E]), ALU.is_equal))
                own.wait()

            def fold_last():
                dve.wait_ge(ld_d, 64)
                for j in range(GH):
                    dve.tensor_scalar(WW[:, j, :], wout2[:], vec[:, V_W2 + j:V_W2 + j + 1], None, ALU.mult).then_inc(ww_ready, 1)
                dve.tensor_scalar(b2r[:], ones[0:M1, :], vec[0:M1, V_B2:V_B2 + 1], None, ALU.mult).then_inc(b2_ready, 1)
                dve.wait_ge(cb_mm, 1)
                dve.tensor_tensor(cbias[:], PS[:, LN_BANK, 0:D], rowv[:, R_BOUT2, :], ALU.add).then_inc(cb_ready, 1)

            def ln_m(b):
                ln_stats("m", U, b, lambda: dve.wait_ge(attn_added, b + 1))
                x_plus_u(b)
                dve.wait_ge(v_ready, B)
                ln_apply("m", U, XN, b)

            def expert_gates(k):
                n, f = divmod(k, FC)
                if n >= 2 and f == 0:
                    dve.wait_ge(moe_mm, n - 1)
                dve.wait_ge(gate_ready, k + 1)
                dve.tensor_tensor(G[:, n % 2, f, :], sg[:, k % 2, :], PS[:, 2 * (k % 2) + 1, :], ALU.mult).then_inc(g_ready, 1)

            def add_expert(n):
                b, e = divmod(n, E)
                dve.wait_ge(moe_mm, n + 1)
                if e:
                    dve.wait_ge(moe_added, QT * n)
                for t in range(QT):
                    i = QT * b + t
                    dve.scalar_tensor_tensor(X[:, i, :], PS[:, 4 + n % 2, t * P:t * P + P], onehot[:, i, e:e + 1],
                                             X[:, i, :], ALU.mult, ALU.add).then_inc(moe_added, 1)

            for m in range(M_TURN):
                maximum(m)
            split_maxima(0)
            for m in range(M_TURN, M_MERGE):
                maximum(m)
            for step in range(S_MAX + 1):
                if step < S_MAX:
                    maximum(M_MERGE + 2 * step)
                    maximum(M_MERGE + 2 * step + 1)
                if step >= QT and step % QT == 0:
                    copy_outputs(0, (step // QT - 1,))
            split_maxima(1)
            copy_outputs(0, range(S_MAX // QT, 4))
            normalise_outputs(0)
            add_attention(0)
            ln_m(0)
            copy_outputs(1, (0,))
            fold_last()
            route(0)
            copy_outputs(1, (1, 2, 3))
            normalise_outputs(1)
            for k in range(2):
                expert_gates(k)
            add_attention(1)
            for k in range(2, E * B * FC):
                n, f = divmod(k, FC)
                expert_gates(k)
                if f == FC - 1 and 1 <= n < E * B - 1:
                    add_expert(n - 1)
                if k == 2:
                    ln_stats("m", U, 1, lambda: dve.wait_ge(attn_added, 2))
                elif k == 3:
                    x_plus_u(1)
                    ln_apply("m", U, XN, 1)
                elif k == FC + 3:
                    route(1)
                elif k == 5 * FC:
                    ln_stats("c", X, 0, lambda: dve.wait_ge(moe_added, QT * E))
                elif k == 5 * FC + 3:
                    ln_apply("c", X, XN, 0)
                    dve.wait_ge(ln_norm["c"], QT)
                    x_plus(0, rowv[:, R_BOUT1, :])

            def ln_c_stats():
                ln_stats("c", X, 1, lambda: dve.wait_ge(moe_added, QT * E * B))

            def ln_c_second():
                ln_apply("c", X, XN, 1)
                dve.wait_ge(ln_norm["c"], NT)
                x_plus(1, rowv[:, R_BOUT1, :])

            def ln_d_first():
                ln_apply("d", X, XN, 0)
                dve.wait_ge(ln_norm["d"], QT)
                dve.wait_ge(cb_ready, 1)
                x_plus(0, cbias[:])

            units("C", lambda u: rowbias[:, tile(u // 2)], {
                0: lambda: add_expert(E * B - 2),
                1: lambda: add_expert(E * B - 1),
                2: ln_c_stats,
                3: ln_c_second,
                2 * QT + 3: lambda: ln_stats("d", X, 0, lambda: dve.wait_ge(tile_added["C"], QT)),
                2 * QT + 5: ln_d_first})
            def sum_inner(b, js):
                def part(i):
                    i.then_inc(inner_ready, 1)

                c = slice(PARTS[b][0] * P, PARTS[b][1] * P)
                for j in js:
                    n = (GH + 1) * b + j
                    w2 = vec[:, V_W2 + j:V_W2 + j + 1]
                    if j == J_JOIN:
                        dve.wait_ge(inner_ready, n)
                        part(dve.tensor_tensor(inner[:, 0, c], inner[:, 0, c], inner[:, 1, c], ALU.add))
                    dve.wait_ge(relu_ready, GH * b + j + 1)
                    o = inner[:, j % 2 if j < J_JOIN else 0, c]
                    if j < 2:
                        part(dve.tensor_scalar(o, RJ[:, j, c], w2, None, ALU.mult))
                    else:
                        dve.wait_ge(inner_ready, n - 1 if j < J_JOIN else n + 1)
                        part(dve.scalar_tensor_tensor(o, RJ[:, j, c], w2, o, ALU.mult, ALU.add))

            def add_last(b):
                for k in PART_PIECES[b]:
                    (lo, hi), bank = PIECES[k]
                    dve.wait_ge(ffn_mm, k + 1)
                    dve.tensor_tensor(X[:, lo:hi, :], PS[:, bank, 0:(hi - lo) * D].rearrange("p (t d) -> p t d", d=D),
                                      X[:, lo:hi, :], ALU.add).then_inc(ffn_added, 1)

            add_tile("C", NT - 2)
            ln_stats("d", X, 1, lambda: dve.wait_ge(tile_added["C"], NT - 1), PARTS[1])
            sum_inner(0, range(1))
            ln_apply("d", X, XN, 1, PARTS[1])
            sum_inner(0, range(1, J_SUM))
            add_tile("C", NT - 1)
            ln_stats("d", X, 2, lambda: dve.wait_ge(tile_added["C"], NT), PARTS[2])
            ln_apply("d", X, XN, 2, PARTS[2])
            sum_inner(0, range(J_SUM, GH))
            dve.wait_ge(ln_norm["d"], NT)
            x_plus(1, cbias[:])
            sum_inner(1, range(2))
            add_last(0)
            sum_inner(1, range(2, GH))
            add_last(2)
            add_last(1)

        @block.scalar
        def _(act):
            def copy(dst, src, scale=1.0):
                return act.activation(dst, src, ACT.Copy, scale=scale)

            def ln_out(name, dst, w=None, bias=None, seqs=range(B)):
                for b in seqs:
                    act.wait_ge(ln_turned[name], b + 1)
                    if w is None:
                        copy(dst[:, b, :], PS[:, LN_BANK, :]).then_inc(ln_T[name], 1)
                    else:
                        act.activation(dst[:, b, :], PS[:, LN_BANK, :], ACT.Identity,
                                       scale=w, bias=bias).then_inc(ln_T[name], 1)

            def units(st, between={}):
                for u in range(UNITS[st] + 2):
                    if u >= 2:
                        v = u - 2
                        act.wait_ge(unit_turned[st], v + 1)
                        copy(PT[v % 2].rearrange("p n q -> p (n q)"),
                             PS[:, 3:6, :].rearrange("p k n -> p (k n)")[:, 0:BLK * P]).then_inc(unit_PT[st], 1)
                    if u < UNITS[st]:
                        act.wait_ge(unit_shift[st], 3 * u + 3)
                        act.activation(Pt[u % 3], Pt[u % 3], ACT.Exp).then_inc(unit_exp[st], 1)
                    if u in between:
                        between[u]()

            def copy_A(m0, m1):
                for m in range(m0, m1):
                    kind, b, k = PREA[m]
                    bank = 3 + m % 3
                    act.wait_ge(preA_mm, 1 + m + 1)
                    if kind == "kk":
                        h0, h1 = BANK_HEADS[k]
                        copy(kkA[:, b, h0 * KEYS:h1 * KEYS], PS[:, bank, 0:(h1 - h0) * KEYS], 0.5).then_inc(preA_act, 1)
                    elif kind == "vw":
                        copy(vwAm[:, b, 512 * k:512 * k + 512], PS[:, bank, :]).then_inc(preA_act, 1)
                    else:
                        copy(vwAr[:, b].rearrange("p g o -> p (g o)"), PS[:, bank, 0:2 * D]).then_inc(preA_act, 1)

            def copy_C(n0, n1):
                for n in range(n0, n1):
                    kind, i, _ = PREC[n]
                    act.wait_ge(preC_mm, n + 1)
                    bank = fold_bank(n)
                    if kind == "k":
                        if n == 0:
                            act.wait_ge(zeroed, Z_ALL)
                        for j in range(2):
                            r = slice(64 * j, 64 * j + 64)
                            copy(kz[r, i % 2, j, :], PS[r, bank, 0:B * KEYS], float(HDC) ** -0.5).then_inc(preC_act, 1)
                    elif kind == "v":
                        copy(vT[:, i % 4, :], PS[:, bank, 0:B * KPAD]).then_inc(preC_act, 1)
                    elif kind == "kk":
                        copy(kkC[:, :, i * KEYS:(i + 1) * KEYS],
                             PS[:, bank, 0:B * KEYS].rearrange("p (b k) -> p b k", b=B)).then_inc(preC_act, 1)
                    elif kind == "vw":
                        g, b = i
                        copy(vwCm[:, b, 512 * g:512 * g + 512], PS[:, bank, :]).then_inc(preC_act, 1)
                    elif kind == "vr":
                        g, b = i
                        copy(vwCr[:, b, g, :], PS[:, bank, 0:D]).then_inc(preC_act, 1)
                    else:
                        copy(XN[:, QT * i:QT * i + QT, :].rearrange("p t d -> p (t d)"), PS[:, bank, :]).then_inc(preC_act, 1)

            x_t = t_in["x"].rearrange("b (t p) d -> p b t d", p=P)
            for b in range(B):
                act.dma_start(X[:, QT * b:QT * b + QT, :], x_t[:, b]).then_inc(ld_x[b], 16)
            act.dma_start(woT, t_in["A_WoT"]).then_inc(ld_wo, 16)
            copy_A(0, 3)
            ln_out("a", XT, seqs=(0,))
            copy_A(3, 7)
            ln_out("a", XT, seqs=(1,))
            units("A", {0: lambda: copy_A(7, 10), 1: lambda: copy_A(10, len(PREA)), NT: lambda: copy_C(0, F_UNIT[0]),
                        NT + 1: lambda: copy_C(F_UNIT[0], F_UNIT[1])})
            ln1 = (vec[:, V_LN1W:V_LN1W + 1], vec[:, V_LN1B:V_LN1B + 1])
            ln_out("b", HT[:, :, 2:T + 2], *ln1, seqs=(0,))
            copy_C(F_UNIT[1], F_LN)
            ln_out("b", HT[:, :, 2:T + 2], *ln1, seqs=(1,))
            copy_C(F_LN, len(PREC))
            act.wait_ge(scr_written[B - 1], 16)
            def turn_outputs(b):
                act.wait_ge(yT_mm, b + 1)
                copy(yT[:].rearrange("p t q -> p (t q)"), PS[:, LN_BANK, :]).then_inc(yT_ready, 1)

            ln2 = (vec[:, V_LN2W:V_LN2W + 1], vec[:, V_LN2B:V_LN2B + 1])
            for n in range(B * 4 * QT * 2):
                s, pair = divmod(n, 2)
                w = T - P * (s % QT)
                act.wait_ge(st_mm, n + 1)
                if s >= 2:
                    act.wait_ge(av_step, 2 * (s - 2) + pair + 1)
                slot = 4 * (s % 2) + 2 * pair
                act.activation(PTb[:, slot:slot + 2, 0:w], PS[:, 2 * pair:2 * pair + 2, 0:w], ACT.Exp,
                               scale=float(HDB) ** -0.5).then_inc(st_exp, 1)
                if n == 2 * S_TAIL + 1:
                    turn_outputs(0)
                if n == 2 * S_LN + 1:
                    ln_out("m", XT, *ln2, seqs=(0,))
            for k in range(E * B * FC):
                act.wait_ge(gv_mm, k + 1)
                act.activation(sg[:, k % 2, :], PS[:, 2 * (k % 2), :], ACT.Silu).then_inc(gate_ready, 1)
                if k == 1:
                    turn_outputs(1)
                elif k == K_LNM:
                    ln_out("m", XT, *ln2, seqs=(1,))
                elif k == K_LNC:
                    ln_out("c", XT, seqs=(0,))
            def ln_d_out(b):
                lo, hi = PARTS[b]
                act.wait_ge(ln_turned["d"], b + 1)
                copy(XT[:].rearrange("p b t -> p (b t)")[:, lo * P:hi * P], PS[:, LN_BANK, 0:(hi - lo) * P]).then_inc(ln_T["d"], 1)

            def inner_input(b):
                lo, hi = PARTS[b]
                act.wait_ge(s_in_mm, b + 1)
                act.activation(sT[:, lo * P:hi * P], PS[:, S_BANK[b], 0:(hi - lo) * P], ACT.Identity,
                               bias=vec[:, V_BIN:V_BIN + 1]).then_inc(s_in_ready, 1)
                act.wait_ge(s_in_ready, b + 1)

            def inner_units(b, js):
                c = slice(PARTS[b][0] * P, PARTS[b][1] * P)
                for j in js:
                    act.activation(RJ[:, j, c], sT[:, c], ACT.Relu, scale=vec[:, V_W1 + j:V_W1 + j + 1],
                                   bias=vec[:, V_B1 + j:V_B1 + j + 1]).then_inc(relu_ready, 1)

            def first_inner():
                inner_input(0)
                inner_units(0, range(J_FIRST))

            units("C", {U_LNC: lambda: ln_out("c", XT, seqs=(1,)), U_LND: lambda: ln_d_out(0),
                        2 * NT - 1: first_inner, 2 * NT: lambda: inner_units(0, range(J_FIRST, J_EARLY))})
            ln_d_out(1)
            inner_input(1)
            inner_units(0, range(J_EARLY, GH))
            inner_units(1, range(J_EARLY1))
            ln_d_out(2)
            inner_input(2)
            inner_units(1, range(J_EARLY1, GH))
            inner_units(2, range(GH))

        @block.tensor
        def _(pe):
            def mm(o, lhsT, rhs, start=True, stop=True):
                return pe.matmul(o, lhsT, rhs, start=start, stop=stop)

            def turn(name, src, seqs=range(B)):
                for b in seqs:
                    pe.wait_ge(ln_norm[name], QT * b + QT)
                    if b:
                        pe.wait_ge(ln_T[name], b)
                    for t in range(QT):
                        i = pe.transpose(PS[:, LN_BANK, t * P:t * P + P], src[:, QT * b + t, :], ident)
                    i.then_inc(ln_turned[name], 1)

            def units(st, kk, vwm, vwr, between={}):
                n_u, per = UNITS[st], PER[st]
                for u in range(n_u + 3):
                    if u < n_u:
                        n, hg = divmod(u, per)
                        b, t = divmod(n, QT)
                        if t == 0 and hg == 0:
                            pe.wait_ge(ln_T["a" if st == "A" else "c"], b + 1)
                        for k, (h0, h1) in enumerate(BANK_HEADS):
                            w = (h1 - h0) * KEYS
                            at = hg * UW + h0 * KEYS
                            o = PS[:, k, 0:w]
                            if u >= 1:
                                pe.wait_ge(unit_shift[st], 3 * (u - 1) + k + 1)
                            i = mm(o, XT[:, b, t * P:t * P + P], kk[:, b, at:at + w], stop=st == "C")
                            if st == "A":
                                i = mm(o, onesb[:], browb[:, h0:h1, b, :], start=False)
                            i.then_inc(scores_mm[st], 1)
                    if u >= 3:
                        v = u - 3
                        n, hg = divmod(v, per)
                        b = n // QT
                        pe.wait_ge(unit_PT[st], v + 1)
                        if hg == 0 and n >= 1:
                            pe.wait_ge(tile_added[st], n)
                        for k in range(BLK):
                            if k < GH:
                                h = GH * hg + k
                                w = vwm[:, b, h * D:h * D + D]
                            else:
                                w = vwr[:, b, 2 * hg + k - GH, :]
                            i = mm(PS[:, 6, 0:D], PT[v % 2][:, k, :], w,
                                   start=hg == 0 and k == 0, stop=hg == per - 1 and k == BLK - 1)
                        if hg == per - 1:
                            i.then_inc(tile_mm[st], 1)
                    if 2 <= u <= n_u + 1:
                        v = u - 2
                        pe.wait_ge(unit_norm[st], 2 * v + 2)
                        if v >= 1:
                            pe.wait_ge(unit_PT[st], v)
                        elif st == "A":
                            pe.wait_ge(preA_act, len(PREA))
                        else:
                            pe.wait_ge(moe_added, E * NT)
                        for k in range(BLK):
                            i = pe.transpose(PS[:, 3 + k // 4, (k % 4) * P:(k % 4) * P + P],
                                             PN[v % 2][:, k * P:k * P + P], ident)
                        i.then_inc(unit_turned[st], 1)
                    if u in between:
                        between[u]()

            def fold_A(m0, m1):
                for m in range(m0, m1):
                    kind, b, k = PREA[m]
                    bank = 3 + m % 3
                    if m >= 3:
                        pe.wait_ge(preA_act, m - 2)
                    if kind == "kk":
                        h0, h1 = BANK_HEADS[k]
                        pe.wait_ge(kzA_ready, b + 1)
                        pe.wait_ge(ld_wq, 16)
                        i = mm(PS[:, bank, 0:(h1 - h0) * KEYS], wqA, KzA[:, b, h0:h1, :])
                    elif kind == "vw":
                        pe.wait_ge(ld_wo, 16)
                        i = mm(PS[:, bank, :], ctxT[:, b, 0:KM], woT[:, 512 * k:512 * k + 512])
                    else:
                        for h in range(HA):
                            g, j = divmod(h, 4)
                            i = mm(PS[32 * j:32 * j + 32, bank, g * D:g * D + D], ctxT[:, b, KM:KPAD],
                                   woT[:, h * D:h * D + D])
                    i.then_inc(preA_mm, 1)

            def fold_C(n0, n1):
                done = [0]
                for kind, i, k in PREC:
                    done.append(done[-1] + k)
                for n in range(n0, n1):
                    kind, i, _ = PREC[n]
                    bank = fold_bank(n)
                    if n == 0:
                        pe.wait_ge(ld_c, 80)
                        pe.wait_ge(unit_shift["A"], 3 * NT)
                    if n == F_LATE:
                        pe.wait_ge(ln_T["b"], B)
                        pe.wait_ge(qk_ready, B)
                    elif 3 <= n < F_LATE:
                        pe.wait_ge(preC_act, done[n - 2])
                    elif n >= F_LATE + 2:
                        pe.wait_ge(preC_act, done[n - 1])
                    if kind == "kk":
                        pe.wait_ge(preC_act, done[1 + PREC.index(("k", i // 2, 2))])
                    elif kind in ("vw", "vr"):
                        pe.wait_ge(preC_act, done[1 + PREC.index(("v", 2 * i[0] + 1, 1))])
                    if kind == "k":
                        q = mm(PS[:, bank, 0:B * KEYS], wkC[:, i * P:i * P + P], ctxT[:, :, 0:KEYS])
                    elif kind == "v":
                        q = mm(PS[:, bank, 0:B * KPAD], wvC[:, i * P:i * P + P], ctxT[:])
                    elif kind == "kk":
                        q = mm(PS[:, bank, 0:B * KEYS], wqT[:, i // 2, :], kz[:, (i // 2) % 2, i % 2, :])
                    elif kind == "vw":
                        g, b = i
                        for c in range(2):
                            q = mm(PS[:, bank, 256 * c:256 * c + 256], vT[:, (2 * g + c) % 4, b * KPAD:b * KPAD + KM],
                                   woutZ[:, 2 * g + c])
                    elif kind == "vr":
                        g, b = i
                        for j in range(4):
                            c = 2 * g + j // 2
                            q = mm(PS[32 * j:32 * j + 32, bank, 0:D], vT[:, c % 4, b * KPAD + KM:b * KPAD + KPAD],
                                   woutZ[:, c, j % 2, :])
                    else:
                        pe.wait_ge(conv_ready, i + 1)
                        for t in range(QT):
                            q = mm(PS[:, bank, t * P:t * P + P], HC2[:, i, t * P:t * P + P], aqkv[:, 4, :])
                    q.then_inc(preC_mm, 1)

            pe.wait_ge(zeroed, 2)
            pe.wait_ge(ld_a, 32)
            mm(PS[0:32, 0, 0:B * KEYS], wkTA, ctxT[:, :, 0:KEYS]).then_inc(preA_mm, 1)
            pe.wait_ge(ktA_ready, 1)
            mm(PS[0:HA, 1, 0:B * KEYS], bqA, KTA.rearrange("p b k -> p (b k)")).then_inc(bias8_mm, 1)
            fold_A(0, 3)
            pe.wait_ge(ld_cst, 16)
            turn("a", XN, (0,))
            pe.wait_ge(preA_act, 3)
            pe.wait_ge(brow_ready, 48)

            def first_gap():
                fold_A(3, 7)
                turn("a", XN, (1,))
                fold_A(7, 10)

            def second_gap():
                fold_C(F_UNIT[0], F_UNIT[1])
                turn("b", XN, (0,))

            units("A", kkA, vwAm, vwAr, {0: first_gap, 1: lambda: fold_A(10, len(PREA)), NT: lambda: fold_C(0, F_UNIT[0]),
                                         NT + 1: second_gap,
                                         NT + 2: lambda: fold_C(F_UNIT[1], F_UNIT[2])})
            def queries_keys(b):
                pe.wait_ge(conv_ready, b + 1)
                if b:
                    pe.wait_ge(qk_ready, b)
                else:
                    pe.wait_ge(tile_added["A"], NT)
                for s in range(4):
                    mm(PS[:, 3 + s, :], aqkv[:, s, :], HC2[:, b, :]).then_inc(qkv_mm, 1)

            pe.wait_ge(ld_b, 64)
            queries_keys(0)
            fold_C(F_UNIT[2], F_LN)
            turn("b", XN, (1,))
            fold_C(F_LN, F_QKV[1])
            queries_keys(1)
            fold_C(F_QKV[1], F_LATE)
            pe.wait_ge(preC_act, sum(j[2] for j in PREC[:F_LATE]))
            pe.wait_ge(qk_ready, B)
            pe.wait_ge(consts_ready, 1)
            def turn_maxima(b):
                pe.wait_ge(*((s1_max, 2 * (64 - M_MERGE)) if b else (s_max, 32)))
                if b:
                    pe.wait_ge(m_split, b)
                pe.transpose(PS[0:HB * QT, 6, 0:P], mB[:, b].rearrange("p h t -> p (h t)"), ident).then_inc(m_turned, 1)

            def scores_for_maximum(m):
                b, n = divmod(m, 32)
                hp, qt = divmod(n, QT)
                w = (qt + 1) * P
                if m == M_MERGE:
                    pe.wait_ge(m_split, 1)
                elif 3 <= m < M_MERGE:
                    pe.wait_ge(s_max, m - 2)
                for heads, bank, mm_done, _, count in max_parts(m):
                    if m > M_MERGE and count > 3:
                        pe.wait_ge(s1_max, count - 3)
                    for j in heads:
                        h = 2 * hp + j
                        o = PS[:, bank + j - heads[0], 0:w]
                        mm(o, qs[b][:, h, qt * P:w], ks[b][:, h, 0:w], stop=False)
                        i = mm(o[:, w - P:w], identb, mask_qk, start=False)
                    i.then_inc(mm_done, 1)

            pe.wait_ge(stack_ready[0], 16 * 12)
            late = F_LATE
            for m in range(32):
                scores_for_maximum(m)
                if m >= 2 and m % 2 == 0 and late < len(PREC):
                    fold_C(late, late + 1)
                    late += 1
            fold_C(late, len(PREC))
            pe.wait_ge(stack_ready[1], 16 * 12)
            for m in range(32, M_MERGE):
                scores_for_maximum(m)
                if m == M_TURN - 1:
                    pe.wait_ge(preC_act, N_PREC)
                    turn_maxima(0)

            def outputs(s, pair):
                bg, kt = divmod(s, QT)
                b, g = divmod(bg, 4)
                pe.wait_ge(st_exp, 2 * s + pair + 1)
                if s == 0 and pair == 0:
                    pe.wait_ge(v_ready, B)
                if kt == 0 and pair == 0:
                    if b == 0 and g >= 1:
                        pe.wait_ge(yg_ready, bg)
                    elif bg == 4:
                        pe.wait_ge(y_norm, QT)
                    elif bg == 5:
                        pe.wait_ge(attn_added, 1)
                    elif bg >= 6:
                        pe.wait_ge(yg_ready, bg - 1)
                for j in range(2 * pair, 2 * pair + 2):
                    i = mm(PS[32 * j:32 * j + 32, av_bank(b, g), kt * P:T], vaug[:, b, kt, 4 * g + j, :],
                           PTb[:, 4 * (s % 2) + j, 0:T - kt * P], start=kt == 0, stop=kt == QT - 1)
                i.then_inc(av_step, 1)

            def turn_outputs(b, tiles):
                for qt in tiles:
                    if qt == 0:
                        pe.wait_ge(yg_ready, 4 * b + 4)
                        pe.wait_ge(m_split, B)
                        if b:
                            pe.wait_ge(routed, b)
                    if qt == QT - 1:
                        pe.wait_ge(y_norm, QT * b + 1)
                    for g in range(4):
                        i = pe.transpose(PS[:, Y_BANK[qt], g * P:g * P + P], yg[:, g, qt * P:qt * P + P], ident)
                    i.then_inc(y_turned, 1)

            def turn_normalised(b):
                pe.wait_ge(y_norm, QT * b + QT)
                if b:
                    pe.wait_ge(cb_ready, 1)
                for qt in range(QT):
                    i = pe.transpose(PS[:, LN_BANK, qt * P:qt * P + P], yn[:, qt], ident)
                i.then_inc(yT_mm, 1)

            def project_outputs(b):
                pe.wait_ge(yT_ready, b + 1)
                for qt in range(QT):
                    i = mm(PS[:, 5, qt * P:qt * P + P], yT[:, qt], projw[:])
                i.then_inc(proj_mm, 1)

            def logits(b):
                pe.wait_ge(ln_T["m"], b + 1)
                for t in range(QT):
                    n = QT * b + t
                    i = mm(PS[:, 6, n * E:n * E + E], XT[:, b, t * P:t * P + P], rw[:])
                i.then_inc(logit_mm, 1)

            for s in range(2 * 16):
                b, step = divmod(s, 16)
                if s == 16:
                    for pair in range(2):
                        outputs(s - 1, pair)
                if step == 0:
                    pe.wait_ge(m_ready[b], 16)
                g, kt = divmod(step, QT)
                w = T - kt * P
                for pair in range(2):
                    if s >= 1:
                        pe.wait_ge(st_exp, 2 * (s - 1) + pair + 1)
                    else:
                        pe.wait_ge(s_max, M_MERGE)
                    for j in range(2):
                        h = 4 * g + 2 * pair + j
                        o = PS[:, 2 * pair + j, 0:w]
                        mm(o, ks[b][:, h, kt * P:kt * P + P], qs[b][:, h, kt * P:T], stop=False)
                        i = mm(o[:, 0:P], identb, mask_kq, start=False)
                    i.then_inc(st_mm, 1)
                    if s < S_MAX:
                        scores_for_maximum(M_MERGE + 2 * s + pair)
                    if s >= 1 and s != 16:
                        outputs(s - 1, pair)
                if s == S_MAX:
                    turn_maxima(1)
                if s == 16:
                    turn_outputs(0, range(QT))
                    turn_normalised(0)
                elif s == S_TAIL + 1:
                    project_outputs(0)
                elif s == S_LN:
                    turn("m", XN, (0,))
                elif s == S_LN + 1:
                    logits(0)
                    pe.wait_ge(b2_ready, 1)
                    mm(PS[:, LN_BANK, 0:D], b2r[:], wout2[0:M1, :]).then_inc(cb_mm, 1)
            for pair in range(2):
                outputs(31, pair)
            turn_outputs(1, range(QT - 1))

            def hidden(k):
                n, f = divmod(k, FC)
                b, e = divmod(n, E)
                if k == 0:
                    pe.wait_ge(ld_moe, 32)
                if k >= 2:
                    pe.wait_ge(g_ready, k - 1)
                if k == E * FC:
                    pe.wait_ge(ln_T["m"], B)
                mm(PS[:, 2 * (k % 2), :], wv[:, e, f * P:f * P + P], XT[:, b, :])
                mm(PS[:, 2 * (k % 2) + 1, :], wv[:, e, FF + f * P:FF + f * P + P], XT[:, b, :]).then_inc(gv_mm, 1)

            def project(n):
                pe.wait_ge(g_ready, FC * n + FC)
                if n >= 2:
                    pe.wait_ge(moe_added, QT * (n - 1))
                if n == 1:
                    pe.wait_ge(attn_added, B)
                for t in range(QT):
                    for f in range(FC):
                        i = mm(PS[:, 4 + n % 2, t * P:t * P + P], G[:, n % 2, f, t * P:t * P + P],
                               pj[:, n % E, f, :], start=f == 0, stop=f == FC - 1)
                i.then_inc(moe_mm, 1)

            for k in range(E * B * FC):
                hidden(k)
                n, f = divmod(k, FC)
                if k == 1:
                    turn_outputs(1, (QT - 1,))
                    turn_normalised(1)
                elif k == 2:
                    project_outputs(1)
                elif k == K_LNM:
                    turn("m", XN, (1,))
                elif k == K_LNM + 2:
                    logits(1)
                elif k == K_LNC:
                    turn("c", XN, (0,))
                if f == 1 and 1 <= n < E * B - 1:
                    project(n - 1)
            pe.wait_ge(g_ready, E * B * FC)
            def turn_d(b):
                lo, hi = PARTS[b]
                pe.wait_ge(ln_norm["d"], hi)
                if b:
                    pe.wait_ge(ln_T["d"], b)
                    pe.wait_ge(s_in_ready, 1)
                for t in range(hi - lo):
                    i = pe.transpose(PS[:, LN_BANK, t * P:t * P + P], XN[:, lo + t, :], ident)
                i.then_inc(ln_turned["d"], 1)

            def inner_input(b):
                lo, hi = PARTS[b]
                pe.wait_ge(ln_T["d"], b + 1)
                if b == 1:
                    pe.wait_ge(unit_shift["C"], 6 * NT)
                mm(PS[:, S_BANK[b], 0:(hi - lo) * P], win2[:],
                   XT[:].rearrange("p b t -> p (b t)")[:, lo * P:hi * P]).then_inc(s_in_mm, 1)

            def last_outputs(b):
                pe.wait_ge(inner_ready, (GH + 1) * (b + 1))
                for k in PART_PIECES[b]:
                    (lo, hi), bank = PIECES[k]
                    for t in range(lo, hi):
                        i = mm(PS[:, bank, (t - lo) * P:(t - lo) * P + P], inner[:, 0, t * P:t * P + P], wout2[:])
                    i.then_inc(ffn_mm, 1)

            def second_input():
                turn_d(1)
                inner_input(1)

            units("C", kkC, vwCm, vwCr, {
                0: lambda: project(E * B - 2), 1: lambda: project(E * B - 1),
                U_LNC: lambda: turn("c", XN, (1,)), U_LND: lambda: turn_d(0),
                2 * NT - 1: lambda: inner_input(0), 2 * NT + 1: second_input})
            turn_d(2)
            inner_input(2)
            last_outputs(0)
            pe.wait_ge(ww_ready, GH)
            (lo, hi), bank = PIECES[LAST]
            for j in range(GH):
                pe.wait_ge(relu_ready, GH * 2 + j + 1)
                i = mm(PS[:, bank, 0:D], RJ[:, j, lo * P:hi * P], WW[:, j, :], start=j == 0, stop=j == GH - 1)
            i.then_inc(ffn_mm, 1)
            last_outputs(1)


def _rope():
    f32 = np.float32
    inv = (f32(1.0) / f32(10000.0) ** (np.arange(0, HDB, 2, dtype=f32) / f32(HDB))).astype(f32)
    fr = np.arange(T, dtype=f32)[:, None] * inv[None, :]
    emb = np.concatenate([fr, fr], axis=1)
    sign = np.where(np.arange(HDB) < HDB // 2, -1.0, 1.0).astype(f32)
    cos, sin = np.cos(emb), np.sin(emb) * sign
    return np.ascontiguousarray(np.stack([np.repeat(cos.T, HB, 0), np.repeat(sin.T, HB, 0)], 1), f32)


def _consts():
    i = np.arange(P)
    later = i[None, :] > i[:, None]
    return np.ascontiguousarray(np.stack([np.eye(P), np.where(later, NEG, 0.0), np.where(later.T, NEG, 0.0)], 1), np.float32)


def _layout(a):
    f32 = np.float32
    vec = np.zeros((P, V_N), f32)
    vec[:, V_LN1W], vec[:, V_LN1B] = a["L0_ffn_ln1_w"], a["L0_ffn_ln1_b"]
    vec[:, V_LN2W], vec[:, V_LN2B] = a["L0_ffn_ln2_w"], a["L0_ffn_ln2_b"]
    vec[:, V_CONV:V_CONV + 3] = a["L0_ffn_conv_w"][:, 0, :]
    for half in range(2):
        r, j = slice(M1 * half, M1 * half + M1), slice(GH * half, GH * half + GH)
        vec[r, V_W1:V_W1 + GH] = a["L1_ffn_W1"][:, j]
        vec[r, V_B1:V_B1 + GH] = a["L1_ffn_b1"][:, j]
        vec[r, V_W2:V_W2 + GH] = a["L1_ffn_W2"][:, j]
        vec[r, V_BIN] = a["L1_ffn_bin_"]
        vec[r, V_B2] = a["L1_ffn_b2"]
    vec[0:32, V_BQ], vec[0:32, V_BK] = a["L0_xattn_bq"], a["L0_xattn_bk"]
    vec[0:32, V_HM:V_HM + HA] = np.repeat(np.eye(HA, dtype=f32), HDA, 0)
    rows = np.zeros((R_N, D), f32)
    rows[R_BO], rows[R_BOUT1], rows[R_BOUT2] = a["L0_xattn_bo"], a["L1_xattn_bout"], a["L1_ffn_bout"]
    rows[R_RANK, 0:NT * E] = np.tile(np.arange(E, 0, -1), NT)
    w = a["L0_ffn_attn_w"]
    by_dim = np.arange(HB * HDB).reshape(HB, HDB).T
    turned = np.roll(by_dim, -(HDB // 2), axis=0)
    q, k, v = w[:, 0:D], w[:, D:2 * D], w[:, 2 * D:3 * D]
    qkv = np.concatenate([q[:, by_dim.ravel()], q[:, turned.ravel()], k[:, by_dim.ravel()], k[:, turned.ravel()], v], 1)
    wkv = a["L1_xattn_Wkv"]
    return {
        "x": a["x"], "ctxT": a["ctx_1024"].transpose(2, 0, 1), "mask_keys": a["mask_BxS2_bk0"].reshape(-1).view(np.int32)[None, :],
        "mask_x": a["mask_BxS_ik0"].reshape(NT, P).T, "vec": vec, "rows": rows, "consts": _consts(), "cossin": _rope(),
        "A_WkT": a["L0_xattn_Wk"].T, "A_Wq": a["L0_xattn_Wq"],
        "A_WoT": a["L0_xattn_Wo"].reshape(D, HA, D).transpose(2, 1, 0).reshape(D, HA * D),
        "B_qkv": qkv, "B_proj": a["L0_ffn_proj_w"], "router": a["L0_ffn_router_w"],
        "wv": a["L0_ffn_expert_wv"], "pj": a["L0_ffn_expert_proj"],
        "C_WqT": a["L1_xattn_Wq"].T, "C_Wk": wkv[:, 0:HC * HDC], "C_Wv": wkv[:, HC * HDC:], "C_Wout": a["L1_xattn_Wout"],
        "D_Win": a["L1_ffn_Win"], "D_Wout": a["L1_ffn_Wout"],
    }


def kernel(**inputs):
    import concourse.bacc as bacc
    from concourse.bass_utils import run_bass_kernel_spmd

    arrays = {f"in_{k}": np.ascontiguousarray(v) for k, v in _layout({k: np.asarray(v) for k, v in inputs.items()}).items()}
    nc = bacc.Bacc("TRN2", target_bir_lowering=False, num_devices=1)
    t_in = {k[3:]: nc.dram_tensor(k, a.shape, mybir.dt.from_np(a.dtype), kind="ExternalInput").ap()
            for k, a in arrays.items()}
    out = nc.dram_tensor("out", (B, T, D), F32, kind="ExternalOutput").ap()
    program(nc, t_in, out)
    r = run_bass_kernel_spmd(nc, [arrays], core_ids=[0])
    return r.results[0]["out"]
```
